# Optimizing a Trainium2 kernel written in Bass

```python
import numpy as np
import jax
import jax.numpy as jnp

def _softmax(x, axis=-1):
    return jax.nn.softmax(x, axis=axis)

def _gelu(x):
    return jax.nn.gelu(x, approximate=True)

def _silu(x):
    return jax.nn.silu(x)

def _sigmoid(x):
    return jax.nn.sigmoid(x)

def _layernorm(x, axis=-1, eps=1e-05):
    m = jnp.mean(x, axis=axis, keepdims=True)
    v = jnp.var(x, axis=axis, keepdims=True)
    return (x - m) / jnp.sqrt(v + eps)

def _scatter_add(tgt, idx, src, axis=0):
    return tgt.at[idx].add(src)

def _segment_sum(src, seg, n):
    return jax.ops.segment_sum(src, seg, n)
kernel_name = 'mk_hybrid_d2_jaxref_r8_389cde'

def setup_inputs(seed: int=0):
    np.random.seed(seed)
    _w = jnp.asarray

    def _L0_attn_a_setup():
        import jax, jax.numpy as jnp
        import numpy as np
        HEADS = 16
        DIM_HEAD = 64
        key = jax.random.key(seed)
        k1, k2, k3 = jax.random.split(key, 3)
        b, n, dim = (2, 256, 128)
        x = jax.random.normal(k1, (b, n, dim), dtype=jnp.float32)
        W_qkv = jax.random.normal(k2, (dim, 6 * HEADS * DIM_HEAD), dtype=jnp.float32) * 0.02
        W_out = jax.random.normal(k3, (HEADS * DIM_HEAD, dim), dtype=jnp.float32) * 0.02
        return {'x': x, 'W_qkv': W_qkv, 'W_out': W_out}
    _L0_attn_a_in = _L0_attn_a_setup()

    def _L0_attn_b_setup():
        import jax, jax.numpy as jnp
        import numpy as np
        B, T, C = (64, 32, 128)
        N_HEAD, HEAD_SIZE, KV_RANK = (16, 64, 128)
        BLOCK_SIZE = 32
        key = jax.random.key(seed)
        ks = jax.random.split(key, 5)
        HD = N_HEAD * HEAD_SIZE

        def init(k, shape):
            fan_in = shape[0]
            bound = 1.0 / np.sqrt(fan_in)
            return jax.random.uniform(k, shape, jnp.float32, -bound, bound)
        return {'x': jax.random.normal(ks[0], (B, T, C), jnp.float32), 'w_kv_down': init(ks[1], (C, KV_RANK)), 'w_kv_up': init(ks[2], (KV_RANK, 2 * HD)), 'w_q': init(ks[3], (C, HD)), 'w_out': init(ks[4], (HD, C))}
    _L0_attn_b_in = _L0_attn_b_setup()

    def _L0_ffn_setup():
        import jax, jax.numpy as jnp
        import numpy as np
        D_MODEL = 128
        N_EXPERTS = 8
        TOP_K = 2
        LN_EPS = 1e-05
        key = jax.random.key(seed)
        ks = jax.random.split(key, 8)
        B, S, d, E = (2, 256, D_MODEL, N_EXPERTS)
        f = 2 * d
        s_in = 0.02
        return {'x': jax.random.normal(ks[0], (B, S, d), jnp.float32), 'Wg': jax.random.normal(ks[1], (d, E), jnp.float32) * s_in, 'bg': jnp.zeros((E,), jnp.float32), 'W1': jax.random.normal(ks[2], (E, d, f), jnp.float32) * s_in, 'b1': jnp.zeros((E, f), jnp.float32), 'W2': jax.random.normal(ks[3], (E, f, d), jnp.float32) * s_in, 'b2': jnp.zeros((E, d), jnp.float32), 'gamma': jnp.ones((d,), jnp.float32), 'beta': jnp.zeros((d,), jnp.float32)}
    _L0_ffn_in = _L0_ffn_setup()

    def _L1_attn_a_setup():
        import jax, jax.numpy as jnp
        import numpy as np
        import math
        B, S, E, H = (2, 256, 128, 16)
        HD = E // H
        HX = 64
        P = HX // 2

        def _l2norm(x, eps=1e-12):
            n = jnp.sqrt(jnp.sum(x * x, axis=-1, keepdims=True))
            return x / jnp.maximum(n, eps)

        def _scramble(t):
            b, h, p, s, _ = t.shape
            return jnp.swapaxes(t, -1, -2).reshape(b, h, p, s, 2)
        key = jax.random.key(seed)
        ks = jax.random.split(key, 12)
        sc = 0.02
        return {'x': jax.random.normal(ks[0], (B, S, E), dtype=jnp.float32), 'Wq': jax.random.normal(ks[1], (E, E), dtype=jnp.float32) * sc, 'bq': jnp.zeros((E,), dtype=jnp.float32), 'Wk': jax.random.normal(ks[2], (E, E), dtype=jnp.float32) * sc, 'bk': jnp.zeros((E,), dtype=jnp.float32), 'Wv': jax.random.normal(ks[3], (E, E), dtype=jnp.float32) * sc, 'bv': jnp.zeros((E,), dtype=jnp.float32), 'Wo': jax.random.normal(ks[4], (E, E), dtype=jnp.float32) * sc, 'bo': jnp.zeros((E,), dtype=jnp.float32), 'Whel': jax.random.normal(ks[5], (H, HX, HD), dtype=jnp.float32) * sc, 'bhel': jnp.zeros((H, HX), dtype=jnp.float32)}
    _L1_attn_a_in = _L1_attn_a_setup()

    def _L1_attn_b_setup():
        import jax, jax.numpy as jnp
        import numpy as np
        from jax import lax
        B, T, D, H = (4, 512, 128, 16)
        d = D // H
        key = jax.random.key(seed)
        k0, k1, k2, k3, k4 = jax.random.split(key, 5)
        s = 1.0 / np.sqrt(D)
        x = jax.random.normal(k0, (B, T, D), dtype=jnp.float32)
        Wv = jax.random.normal(k1, (D, D), dtype=jnp.float32) * s
        Wo = jax.random.normal(k2, (D, D), dtype=jnp.float32) * s
        Wg = jax.random.normal(k3, (H, D), dtype=jnp.float32) * s
        Wb = jax.random.normal(k4, (H, D), dtype=jnp.float32) * s
        return {'x': x, 'Wv': Wv, 'Wo': Wo, 'Wg': Wg, 'Wb': Wb}
    _L1_attn_b_in = _L1_attn_b_setup()

    def _L1_ffn_setup():
        import jax, jax.numpy as jnp
        import numpy as np
        B, S, H, F, E = (1, 256, 128, 256, 8)

        def _swiglu(x, wg, wu, wd):
            return jax.nn.silu(x @ wg.T) * (x @ wu.T) @ wd.T
        key = jax.random.key(seed)
        ks = jax.random.split(key, 8)
        sc = 1.0 / np.sqrt(H)
        scf = 1.0 / np.sqrt(F)
        return {'hidden_states': jax.random.normal(ks[0], (B, S, H), jnp.float32), 'gate_w': jax.random.normal(ks[1], (E, H), jnp.float32) * sc, 'shared_gate': jax.random.normal(ks[2], (F, H), jnp.float32) * sc, 'shared_up': jax.random.normal(ks[3], (F, H), jnp.float32) * sc, 'shared_down': jax.random.normal(ks[4], (H, F), jnp.float32) * scf, 'r_gate': jax.random.normal(ks[5], (E, F, H), jnp.float32) * sc, 'r_up': jax.random.normal(ks[6], (E, F, H), jnp.float32) * sc, 'r_down': jax.random.normal(ks[7], (E, H, F), jnp.float32) * scf}
    _L1_ffn_in = _L1_ffn_setup()
    _d = {'L0_attn_a_x': _L0_attn_a_in['x'], 'L0_attn_a_W_qkv': _L0_attn_a_in['W_qkv'], 'L0_attn_a_W_out': _L0_attn_a_in['W_out'], 'L0_attn_b_w_kv_down': _L0_attn_b_in['w_kv_down'], 'L0_attn_b_w_kv_up': _L0_attn_b_in['w_kv_up'], 'L0_attn_b_w_q': _L0_attn_b_in['w_q'], 'L0_attn_b_w_out': _L0_attn_b_in['w_out'], 'L0_ffn_Wg': _L0_ffn_in['Wg'], 'L0_ffn_bg': _L0_ffn_in['bg'], 'L0_ffn_W1': _L0_ffn_in['W1'], 'L0_ffn_b1': _L0_ffn_in['b1'], 'L0_ffn_W2': _L0_ffn_in['W2'], 'L0_ffn_b2': _L0_ffn_in['b2'], 'L0_ffn_gamma': _L0_ffn_in['gamma'], 'L0_ffn_beta': _L0_ffn_in['beta'], 'L1_attn_a_Wq': _L1_attn_a_in['Wq'], 'L1_attn_a_bq': _L1_attn_a_in['bq'], 'L1_attn_a_Wk': _L1_attn_a_in['Wk'], 'L1_attn_a_bk': _L1_attn_a_in['bk'], 'L1_attn_a_Wv': _L1_attn_a_in['Wv'], 'L1_attn_a_bv': _L1_attn_a_in['bv'], 'L1_attn_a_Wo': _L1_attn_a_in['Wo'], 'L1_attn_a_bo': _L1_attn_a_in['bo'], 'L1_attn_a_Whel': _L1_attn_a_in['Whel'], 'L1_attn_a_bhel': _L1_attn_a_in['bhel'], 'L1_attn_b_Wv': _L1_attn_b_in['Wv'], 'L1_attn_b_Wo': _L1_attn_b_in['Wo'], 'L1_attn_b_Wg': _L1_attn_b_in['Wg'], 'L1_attn_b_Wb': _L1_attn_b_in['Wb'], 'L1_ffn_gate_w': _L1_ffn_in['gate_w'], 'L1_ffn_shared_gate': _L1_ffn_in['shared_gate'], 'L1_ffn_shared_up': _L1_ffn_in['shared_up'], 'L1_ffn_shared_down': _L1_ffn_in['shared_down'], 'L1_ffn_r_gate': _L1_ffn_in['r_gate'], 'L1_ffn_r_up': _L1_ffn_in['r_up'], 'L1_ffn_r_down': _L1_ffn_in['r_down']}
    _x0 = _d['L0_attn_a_x']
    _d['L0_attn_a_x'] = jax.random.normal(jax.random.fold_in(jax.random.key(seed), 1), (16, 256, 128), dtype=_x0.dtype)
    del _x0
    return _d

def reference(L0_attn_a_x, L0_attn_a_W_qkv, L0_attn_a_W_out, L0_attn_b_w_kv_down, L0_attn_b_w_kv_up, L0_attn_b_w_q, L0_attn_b_w_out, L0_ffn_Wg, L0_ffn_bg, L0_ffn_W1, L0_ffn_b1, L0_ffn_W2, L0_ffn_b2, L0_ffn_gamma, L0_ffn_beta, L1_attn_a_Wq, L1_attn_a_bq, L1_attn_a_Wk, L1_attn_a_bk, L1_attn_a_Wv, L1_attn_a_bv, L1_attn_a_Wo, L1_attn_a_bo, L1_attn_a_Whel, L1_attn_a_bhel, L1_attn_b_Wv, L1_attn_b_Wo, L1_attn_b_Wg, L1_attn_b_Wb, L1_ffn_gate_w, L1_ffn_shared_gate, L1_ffn_shared_up, L1_ffn_shared_down, L1_ffn_r_gate, L1_ffn_r_up, L1_ffn_r_down):

    def _L0_attn_a_ref(x, W_qkv, W_out):
        import jax, jax.numpy as jnp
        import numpy as np
        HEADS = 16
        DIM_HEAD = 64
        b, n, _ = x.shape
        h, d = (HEADS, DIM_HEAD)
        scale = d ** (-0.5)
        qkv = (x @ W_qkv).reshape(b, n, 6, h, d).transpose(2, 0, 3, 1, 4)
        qu, ku, vu, qc, kc, vc = qkv
        qu_s = qu * scale
        qc_s = qc * scale
        idx = jnp.arange(n)
        future = idx[None, :] > idx[:, None]
        term1 = jnp.einsum('bhid,bhjd->bhij', qc_s, vu)
        term1 = jnp.where(future, 0.0, term1)
        lookahead = jax.nn.sigmoid(jnp.einsum('bhid,bhjd->bhij', qu_s, ku))
        lookahead = jnp.where(future, lookahead, 0.0)
        Su = jnp.einsum('bhij,bhkj->bhik', term1, lookahead)
        Sc = jnp.einsum('bhid,bhjd->bhij', qc_s, kc)
        scores = Sc - jax.nn.silu(Su)
        neg = -jnp.finfo(scores.dtype).max
        scores = jnp.where(future, neg, scores)
        attn = jax.nn.softmax(scores, axis=-1)
        out = jnp.einsum('bhij,bhjd->bhid', attn, vc)
        out = out.transpose(0, 2, 1, 3).reshape(b, n, h * d)
        return out @ W_out

    def _L0_attn_b_ref(x, w_kv_down, w_kv_up, w_q, w_out):
        import jax, jax.numpy as jnp
        import numpy as np
        B, T, C = (64, 32, 128)
        N_HEAD, HEAD_SIZE, KV_RANK = (16, 64, 128)
        BLOCK_SIZE = 32
        Bx, Tx, Cx = x.shape
        HD = N_HEAD * HEAD_SIZE
        latent_kv = x @ w_kv_down
        kv = latent_kv @ w_kv_up
        k, v = (kv[..., :HD], kv[..., HD:])
        k = k.reshape(Bx, Tx, N_HEAD, HEAD_SIZE)
        v = v.reshape(Bx, Tx, N_HEAD, HEAD_SIZE)
        q = (x @ w_q).reshape(Bx, Tx, N_HEAD, HEAD_SIZE)
        scale = HEAD_SIZE ** (-0.5)
        att = jnp.einsum('bqhd,bkhd->bhqk', q, k) * scale
        causal = jnp.tril(jnp.ones((Tx, Tx), dtype=bool))
        att = jnp.where(causal, att, -jnp.inf)
        att = jax.nn.softmax(att, axis=-1)
        y = jnp.einsum('bhqk,bkhd->bqhd', att, v)
        y = y.reshape(Bx, Tx, HD)
        return y @ w_out

    def _L0_ffn_ref(x, Wg, bg, W1, b1, W2, b2, gamma, beta):
        import jax, jax.numpy as jnp
        import numpy as np
        D_MODEL = 128
        N_EXPERTS = 8
        TOP_K = 2
        LN_EPS = 1e-05
        logits = jnp.einsum('bsd,de->bse', x, Wg) + bg
        topk_vals, topk_idx = jax.lax.top_k(logits, TOP_K)
        topk_w = jax.nn.softmax(topk_vals, axis=-1)
        h = jax.nn.relu(jnp.einsum('bsd,edf->bsef', x, W1) + b1)
        eo = jnp.einsum('bsef,efd->bsed', h, W2) + b2
        sel = jnp.take_along_axis(eo, topk_idx[..., None], axis=2)
        mixed = jnp.sum(sel * topk_w[..., None], axis=2)
        y = mixed + x
        mu = jnp.mean(y, axis=-1, keepdims=True)
        var = jnp.mean(jnp.square(y - mu), axis=-1, keepdims=True)
        return gamma * (y - mu) * jax.lax.rsqrt(var + LN_EPS) + beta

    def _L1_attn_a_ref(x, Wq, bq, Wk, bk, Wv, bv, Wo, bo, Whel, bhel):
        import jax, jax.numpy as jnp
        import numpy as np
        import math
        B, S, E, H = (2, 256, 128, 16)
        HD = E // H
        HX = 64
        P = HX // 2

        def _l2norm(x, eps=1e-12):
            n = jnp.sqrt(jnp.sum(x * x, axis=-1, keepdims=True))
            return x / jnp.maximum(n, eps)

        def _scramble(t):
            b, h, p, s, _ = t.shape
            return jnp.swapaxes(t, -1, -2).reshape(b, h, p, s, 2)
        b, s, e = x.shape
        h, hx, hd = Whel.shape
        p = hx // 2
        q = x @ Wq.T + bq
        k = x @ Wk.T + bk
        v = x @ Wv.T + bv
        qh = q.reshape(b, s, h, hd)
        kh = k.reshape(b, s, h, hd)
        q_hel = jnp.einsum('bshd,hed->bshe', qh, Whel) + bhel
        k_hel = jnp.einsum('bshd,hed->bshe', kh, Whel) + bhel
        qn = _l2norm(q_hel.reshape(b, s, h, p, 2)).transpose(0, 2, 3, 1, 4)
        kn = _l2norm(k_hel.reshape(b, s, h, p, 2)).transpose(0, 2, 3, 1, 4)
        qn = _scramble(qn)
        kn = _scramble(kn)
        helical = jnp.einsum('bhpsc,bhptc->bhst', qn, kn) / p
        dot = jnp.einsum('bshd,bthd->bhst', qh, kh) / math.sqrt(hd)
        alpha = 0.5
        attn = jax.nn.softmax(alpha * dot + (1.0 - alpha) * helical, axis=-1)
        vh = v.reshape(b, s, h, hd)
        out = jnp.einsum('bhst,bthd->bshd', attn, vh).reshape(b, s, e)
        return out @ Wo.T + bo

    def _L1_attn_b_ref(x, Wv, Wo, Wg, Wb):
        import jax, jax.numpy as jnp
        import numpy as np
        from jax import lax
        B, T, D, H = (4, 512, 128, 16)
        d = D // H
        Bb, Tt, Dd = x.shape
        dd = Dd // H
        rk = x.reshape(Bb, Tt, H, dd)
        rk = rk / jnp.maximum(jnp.linalg.norm(rk, axis=-1, keepdims=True), 1e-12)
        wk = jnp.pad(rk[:, :-1], ((0, 0), (1, 0), (0, 0), (0, 0)))
        v = (x @ Wv.T).reshape(Bb, Tt, H, dd)
        gate = jax.nn.sigmoid(x @ Wg.T)
        beta = jax.nn.sigmoid(x @ Wb.T)

        def step(S, inp):
            rk_t, wk_t, v_t, g_t, b_t = inp
            pred = jnp.einsum('bhk,bhkd->bhd', wk_t, S)
            err = (v_t - pred) * b_t[..., None]
            S = S + wk_t[..., None] * err[..., None, :]
            o = jnp.einsum('bhk,bhkd->bhd', rk_t, S) * g_t[..., None]
            return (S, o)
        to_time = lambda a: jnp.moveaxis(a, 1, 0)
        xs = (to_time(rk), to_time(wk), to_time(v), to_time(gate), to_time(beta))
        S0 = jnp.zeros((Bb, H, dd, dd), x.dtype)
        _, out = lax.scan(step, S0, xs)
        out = jnp.moveaxis(out, 0, 1).reshape(Bb, Tt, Dd)
        return out @ Wo.T

    def _L1_ffn_ref(hidden_states, gate_w, shared_gate, shared_up, shared_down, r_gate, r_up, r_down):
        import jax, jax.numpy as jnp
        import numpy as np
        B, S, H, F, E = (1, 256, 128, 256, 8)

        def _swiglu(x, wg, wu, wd):
            return jax.nn.silu(x @ wg.T) * (x @ wu.T) @ wd.T
        b, s, h = hidden_states.shape
        x = hidden_states.reshape(-1, h)
        shared_out = _swiglu(x, shared_gate, shared_up, shared_down)
        logits = x @ gate_w.T
        top_id = jnp.argmax(logits, axis=-1)
        score = jax.nn.sigmoid(jnp.max(logits, axis=-1))
        xs = x * score[:, None]

        def body(acc, ws):
            wg, wu, wd, e = ws
            xe = jnp.where((top_id == e)[:, None], xs, 0.0)
            return (acc + _swiglu(xe, wg, wu, wd), None)
        acc0 = jnp.zeros_like(x)
        routed_out, _ = jax.lax.scan(body, acc0, (r_gate, r_up, r_down, jnp.arange(E)))
        return (shared_out + routed_out).reshape(b, s, h)
    x = L0_attn_a_x
    x = x + _L0_attn_a_ref(_layernorm(x, axis=-1), L0_attn_a_W_qkv, L0_attn_a_W_out)
    x = x + _L0_ffn_ref(_layernorm(x, axis=-1), L0_ffn_Wg, L0_ffn_bg, L0_ffn_W1, L0_ffn_b1, L0_ffn_W2, L0_ffn_b2, L0_ffn_gamma, L0_ffn_beta)
    x = x + _L0_attn_b_ref(_layernorm(x, axis=-1), L0_attn_b_w_kv_down, L0_attn_b_w_kv_up, L0_attn_b_w_q, L0_attn_b_w_out)
    x = x + _L0_ffn_ref(_layernorm(x, axis=-1), L0_ffn_Wg, L0_ffn_bg, L0_ffn_W1, L0_ffn_b1, L0_ffn_W2, L0_ffn_b2, L0_ffn_gamma, L0_ffn_beta)
    x = x + _L1_attn_a_ref(_layernorm(x, axis=-1), L1_attn_a_Wq, L1_attn_a_bq, L1_attn_a_Wk, L1_attn_a_bk, L1_attn_a_Wv, L1_attn_a_bv, L1_attn_a_Wo, L1_attn_a_bo, L1_attn_a_Whel, L1_attn_a_bhel)
    x = x + _L1_ffn_ref(_layernorm(x, axis=-1), L1_ffn_gate_w, L1_ffn_shared_gate, L1_ffn_shared_up, L1_ffn_shared_down, L1_ffn_r_gate, L1_ffn_r_up, L1_ffn_r_down)
    x = x + _L1_attn_b_ref(_layernorm(x, axis=-1), L1_attn_b_Wv, L1_attn_b_Wo, L1_attn_b_Wg, L1_attn_b_Wb)
    x = x + _L1_ffn_ref(_layernorm(x, axis=-1), L1_ffn_gate_w, L1_ffn_shared_gate, L1_ffn_shared_up, L1_ffn_shared_down, L1_ffn_r_gate, L1_ffn_r_up, L1_ffn_r_down)
    return x

_drawn_inputs = setup_inputs


def setup_inputs(seed=0):
    import zlib

    import numpy as np

    out = dict(_drawn_inputs(seed))
    spreads = {'L0_ffn_bg': (0.0, 0.1),
     'L0_ffn_b1': (0.0, 0.321),
     'L0_ffn_b2': (0.0, 0.1),
     'L0_ffn_gamma': (1.0, 0.2),
     'L0_ffn_beta': (0.0, 0.1),
     'L1_attn_a_bq': (0.0, 0.8),
     'L1_attn_a_bk': (0.0, 0.8),
     'L1_attn_a_bv': (0.0, 0.506),
     'L1_attn_a_bo': (0.0, 0.1),
     'L1_attn_a_bhel': (0.0, 0.8)}
    factors = {'L0_attn_b_w_q': 5.635,
     'L1_attn_a_Wq': 8.0,
     'L1_attn_a_Wk': 8.0,
     'L1_attn_a_Wv': 8.0,
     'L1_attn_a_Wo': 4.243,
     'L1_attn_a_Whel': 8.0}
    for name, (base, spread) in spreads.items():
        noise = np.random.default_rng([zlib.crc32(name.encode()), seed]).standard_normal(out[name].shape)
        drawn = base * np.exp(spread * noise) if base else spread * noise
        out[name] = jnp.asarray(drawn.astype(out[name].dtype))
    for name, factor in factors.items():
        out[name] = (out[name] * factor).astype(out[name].dtype)
    return out
```

```python
from contextlib import ExitStack

import concourse.bass as bass
from concourse import mybir

F32 = mybir.dt.float32
BF16 = mybir.dt.bfloat16
I32 = mybir.dt.int32
ACT = mybir.ActivationFunctionType
ALU = mybir.AluOpType
AX = mybir.AxisListType

P = 128
BATCH = 16
SEQ = 256
TOK = BATCH * SEQ
TILES = TOK // P
HEADS = 16
PAIRS = HEADS // 2
STEPS = PAIRS * BATCH
TRI = 3 * P
NEG = -3.0e38


def reached(eng, sem, count):
    if not isinstance(count, int) or count > 0:
        eng.wait_ge(sem, count)


def skewed(eng, steps, lag, body, unroll=2):
    head = -(-lag // unroll) * unroll
    for n in range(head):
        body(n, n % unroll)
    with eng.Fori(head // unroll, steps // unroll) as m:
        for k in range(unroll):
            body(unroll * m + k, k)
    for n in range(steps, steps + lag):
        body(n, n % unroll)


def live(n, steps):
    return not isinstance(n, int) or 0 <= n < steps


def turns(eng, count):
    yield 0
    with eng.Fori(1, count) as i:
        yield i


class Phase:

    def __init__(self, nc, name):
        self.nc, self.name, self.ctx, self.sems = nc, name, ExitStack(), []

    def sb(self, name, shape, dt=F32):
        return self.ctx.enter_context(self.nc.sbuf_tensor(f"{self.name}_{name}", shape, dt))

    def bank(self, name, shape=(P, 512), dt=F32):
        return self.ctx.enter_context(self.nc.psum_tensor(f"{self.name}_{name}", list(shape), dt))

    def sem(self, name):
        s = self.nc.alloc_semaphore(f"{self.name}_{name}")
        self.sems.append(s)
        return s

    def __enter__(self):
        return self

    def __exit__(self, *error):
        if error[0] is None:
            self.nc.clear_and_free_semaphores(self.sems)
            self.nc.all_engine_barrier()
        self.ctx.close()


class Shared:

    def __init__(self, nc, ctx):
        def sb(name, shape, dt=F32):
            return ctx.enter_context(nc.sbuf_tensor(name, shape, dt))

        self.X = sb("X", [P, TILES, P])
        self.XN = sb("XN", [P, TILES, P])
        self.XNT = sb("XNT", [P, TOK])
        self.ident = sb("ident", [P, P])
        self.ident16 = sb("ident16", [P, P], BF16)
        self.future16 = sb("future16", [P, P], BF16)


def load_and_constants(nc, sh, x):
    with Phase(nc, "ld") as ph:
        loaded, zeroed, made = ph.sem("loaded"), ph.sem("zeroed"), ph.sem("made")
        with nc.Block() as block:
            @block.sync
            def _(sp):
                sp.dma_start(sh.X[:], x.rearrange("b (h p) c -> p (b h) c", p=P)).then_inc(loaded, 16)
                sp.wait_ge(loaded, 16)

            @block.gpsimd
            def _(pool):
                nc.gpsimd.memset(sh.ident[:], 0.0).then_inc(zeroed, 1)
                nc.gpsimd.memset(sh.ident16[:], 0.0).then_inc(zeroed, 1)
                nc.gpsimd.memset(sh.future16[:], 0.0).then_inc(zeroed, 1)
                pool.wait_ge(zeroed, 3)
                for t in (sh.ident, sh.ident16):
                    nc.gpsimd.affine_select(out=t[:], in_=t[:], compare_op=ALU.not_equal, fill=1.0, base=0,
                                            pattern=[[-1, P]], channel_multiplier=1).then_inc(made, 1)
                nc.gpsimd.affine_select(out=sh.future16[:], in_=sh.future16[:], compare_op=ALU.is_ge, fill=NEG,
                                        base=0, pattern=[[-1, P]], channel_multiplier=1).then_inc(made, 1)
                pool.wait_ge(made, 3)


def row_statistics(nc, dve, st, mean, rstd, work, chain, sqrt_in, sqrt_done):
    even, odd = (st[:, :, 1], st[:, :, 2]), (st[:, :, 4], st[:, :, 5])
    a, b, c = work[:, 0, :], work[:, 1, :], work[:, 2, :]
    nc.vector.tensor_tensor(a, even[0], odd[0], ALU.add).then_inc(chain, 1)
    nc.vector.tensor_tensor(b, even[0], odd[0], ALU.subtract).then_inc(chain, 1)
    nc.vector.tensor_tensor(c, even[1], odd[1], ALU.add).then_inc(chain, 1)
    dve.wait_ge(chain, 3)
    nc.vector.tensor_scalar(mean[:], a, 0.5, None, ALU.mult).then_inc(chain, 1)
    nc.vector.scalar_tensor_tensor(out=work[:, 3, :], in0=b, scalar=0.25, in1=b, op0=ALU.mult,
                                   op1=ALU.mult).then_inc(chain, 1)
    dve.wait_ge(chain, 5)
    nc.vector.scalar_tensor_tensor(out=work[:, 4, :], in0=c, scalar=1.0 / P, in1=work[:, 3, :], op0=ALU.mult,
                                   op1=ALU.add).then_inc(chain, 1)
    dve.wait_ge(chain, 6)
    nc.vector.tensor_scalar(work[:, 5, :], work[:, 4, :], 1e-5, None, ALU.add).then_inc(sqrt_in, 1)
    dve.wait_ge(sqrt_done, 1)
    nc.vector.reciprocal(rstd[:], work[:, 6, :]).then_inc(chain, 1)
    dve.wait_ge(chain, 7)


def layernorm(nc, sh, name, keep=None):
    G = TILES // 4
    with Phase(nc, name) as ph:
        st, mean, rstd, work = ph.sb("st", [P, TILES, 6]), ph.sb("mean", [P, TILES]), ph.sb("rstd", [P, TILES]), \
            ph.sb("work", [P, 7, TILES])
        xr = ph.sb("xr", [P, 2, 4, P])
        turned = ph.bank("turned", (P, 2, 512))
        stats, chain, sqrt_in, sqrt_done = ph.sem("stats"), ph.sem("chain"), ph.sem("sqrt_in"), ph.sem("sqrt_done")
        normed, kept, turn, evac = ph.sem("normed"), ph.sem("kept"), ph.sem("turn"), ph.sem("evac")
        with nc.Block() as block:
            @block.vector
            def _(dve):
                with dve.Fori(0, TILES) as t:
                    nc.vector.bn_stats(st[:, bass.ds(t, 1), :].rearrange("p a s -> p (a s)"),
                                       sh.X[:, bass.ds(t, 1), :].rearrange("p a c -> p (a c)")).then_inc(stats, 1)
                dve.wait_ge(stats, TILES)
                row_statistics(nc, dve, st, mean, rstd, work, chain, sqrt_in, sqrt_done)
                for m in turns(dve, G // 2):
                    for k in range(2):
                        g = 2 * m + k
                        reached(dve, turn, 2 * m)
                        if keep is not None:
                            reached(dve, kept, 2 * m)
                        for i in range(4):
                            ins = nc.vector.tensor_scalar(
                                xr[:, k, i, :], sh.X[:, bass.ds(4 * g + i, 1), :].rearrange("p a c -> p (a c)"),
                                mean[:, bass.ds(4 * g + i, 1)], rstd[:, bass.ds(4 * g + i, 1)],
                                ALU.subtract, ALU.mult)
                        ins.then_inc(normed, 1)

            @block.scalar
            def _(act):
                act.wait_ge(sqrt_in, 1)
                nc.scalar.activation(work[:, 6, :], work[:, 5, :], ACT.Sqrt).then_inc(sqrt_done, 1)
                for m in turns(act, G // 2):
                    for k in range(2):
                        g = 2 * m + k
                        act.wait_ge(turn, g + 1)
                        nc.scalar.activation(sh.XNT[:, bass.ds(g * 512, 512)], turned[:, k, :],
                                             ACT.Copy).then_inc(evac, 1)

            @block.tensor
            def _(pe):
                for m in turns(pe, G // 2):
                    for k in range(2):
                        g = 2 * m + k
                        pe.wait_ge(normed, g + 1)
                        reached(pe, evac, 2 * m)
                        for i in range(4):
                            ins = nc.tensor.transpose(turned[:, k, i * P:(i + 1) * P], xr[:, k, i, :], sh.ident[:])
                        ins.then_inc(turn, 1)

            @block.gpsimd
            def _(pool):
                if keep is None:
                    return
                for m in turns(pool, G // 2):
                    for k in range(2):
                        g = 2 * m + k
                        pool.wait_ge(normed, g + 1)
                        nc.gpsimd.tensor_copy(keep[:, bass.ds(4 * g, 4), :], xr[:, k, :, :]).then_inc(kept, 1)


def lookahead_attention(nc, sh, W_qkv, W_out):
    D = 64
    SCALE = D ** -0.5
    with Phase(nc, "aa") as ph:
        w = ph.sb("w", [P, 6, P])
        wo = ph.sb("wo", [P, P])
        xs = ph.sb("xs", [P, 2, SEQ])
        qkv = ph.sb("qkv", [P, 2, 3, 2, SEQ])
        causal = ph.sb("causal", [P, TRI])
        ahead = ph.sb("ahead", [P, TRI])
        th_look, th_su = ph.sb("th_look", [P, 2, TRI]), ph.sb("th_su", [P, 2, TRI])
        look, term = ph.sb("look", [P, 2, TRI]), ph.sb("term", [P, 2, TRI])
        gated, minus = ph.sb("gated", [P, 2, TRI]), ph.sb("minus", [P, 2, TRI])
        prob, probT = ph.sb("prob", [P, 2, TRI]), ph.sb("probT", [P, 2, TRI])
        low, total, inv = ph.sb("low", [P, 2, 2]), ph.sb("total", [P, 2, 2]), ph.sb("inv", [P, 2, 2])
        headsT = ph.sb("headsT", [P, SEQ])
        carrier = ph.sb("carrier", [P, 1])
        proj = ph.bank("proj", (P, 2, 512))
        ps_look, ps_term, ps_score, ps_su, ps_turn, ps_out = (
            ph.bank(x) for x in ("ps_look", "ps_term", "ps_score", "ps_su", "ps_turn", "ps_out"))
        w_in, wo_in, masks0, masks, staged = (ph.sem(x) for x in ("w_in", "wo_in", "masks0", "masks", "staged"))
        projected, kept = ph.sem("projected"), ph.sem("kept")
        look_mm, term_mm, score_mm, su_mm, turned, out_mm, y_mm = (
            ph.sem(x) for x in ("look_mm", "term_mm", "score_mm", "su_mm", "turned", "out_mm", "y_mm"))
        th_look_ok, th_su_ok, exp_ok, heads_ok = (ph.sem(x) for x in ("th_look_ok", "th_su_ok", "exp_ok", "heads_ok"))
        look_ok, term_ok, gated_ok, minus_ok, inv_ok, prob_ok, probT_ok, added = (
            ph.sem(x) for x in ("look_ok", "term_ok", "gated_ok", "minus_ok", "inv_ok", "prob_ok", "probT_ok", "added"))
        w_dram = W_qkv.rearrange("c (j q) -> c j q", j=6)
        QU, KU, VU, QC, KC, VC = range(6)

        with nc.Block() as block:
            @block.sync
            def _(sp):
                for p in turns(sp, PAIRS):
                    reached(sp, projected, 3 * BATCH * p)
                    sp.dma_start(w[:], w_dram[:, :, bass.ds(p * P, P)]).then_inc(w_in, 16)
                    reached(sp, y_mm, BATCH * p)
                    sp.dma_start(wo[:], W_out[bass.ds(p * P, P), :]).then_inc(wo_in, 16)

            @block.gpsimd
            def _(pool):
                nc.gpsimd.memset(causal[:], 1.0).then_inc(masks0, 1)
                nc.gpsimd.memset(ahead[:], -0.25).then_inc(masks0, 1)
                pool.wait_ge(masks0, 2)
                for at in (0, 2 * P):
                    nc.gpsimd.affine_select(out=causal[:, at:at + P], in_=causal[:, at:at + P], compare_op=ALU.is_ge,
                                            fill=0.0, base=0, pattern=[[1, P]], channel_multiplier=-1).then_inc(masks, 1)
                    nc.gpsimd.affine_select(out=ahead[:, at:at + P], in_=ahead[:, at:at + P], compare_op=ALU.is_gt,
                                            fill=0.0, base=0, pattern=[[-1, P]], channel_multiplier=1).then_inc(masks, 1)

                def stage(n, k):
                    reached(pool, projected, 3 * (n - 1))
                    nc.gpsimd.tensor_copy(xs[:, k, :], sh.XNT[:, bass.ds((n % BATCH) * SEQ, SEQ)]).then_inc(staged, 1)
                skewed(pool, STEPS, 2, lambda n, k: stage(n, k) if live(n, STEPS) else None)

            @block.tensor
            def _(pe):
                def project(n, k, j):
                    if j == 0:
                        pe.wait_ge(staged, n + 1)
                        pe.wait_ge(w_in, 16 * (n // BATCH + 1))
                    reached(pe, kept, 3 * n + j - 1)
                    bank = proj[:, (k + j) % 2, :]
                    pair = ((QU, QC), (KU, KC), (VU,))[j]
                    for i, m in enumerate(pair):
                        ins = nc.tensor.matmul(bank[:, i * SEQ:(i + 1) * SEQ], w[:, m, :], xs[:, k, :],
                                               start=True, stop=True)
                    if j == 2:
                        for t in range(2):
                            ins = nc.tensor.matmul(bank[:, SEQ + t * P:SEQ + (t + 1) * P], xs[:, k, t * P:(t + 1) * P],
                                                   w[:, VC, :], start=True, stop=True)
                    ins.then_inc(projected, 1)

                def rows(k, h, part, side):
                    return qkv[64 * h:64 * h + 64, k, part, side, :]

                def look_and_term(n, k, h):
                    q, kk, vu, qc = rows(k, h, 0, 0), rows(k, h, 1, 0), rows(k, h, 2, 0), rows(k, h, 0, 1)
                    pe.wait_ge(kept, 3 * n + 2)
                    reached(pe, th_look_ok, 2 * n + h)
                    nc.tensor.matmul(ps_look[:, 0:P], kk[:, 0:P], q[:, 0:P], start=True, stop=True)
                    nc.tensor.matmul(ps_look[:, P:TRI], kk[:, P:SEQ], q, start=True, stop=True).then_inc(look_mm, 1)
                    pe.wait_ge(kept, 3 * n + 3)
                    reached(pe, term_ok, 2 * n + h)
                    nc.tensor.matmul(ps_term[:, 0:SEQ], vu[:, 0:P], qc, start=True, stop=True)
                    nc.tensor.matmul(ps_term[:, SEQ:TRI], vu[:, P:SEQ], qc[:, P:SEQ], start=True,
                                     stop=True).then_inc(term_mm, 1)

                def score(n, k, h):
                    qc, kc = rows(k, h, 0, 1), rows(k, h, 1, 1)
                    reached(pe, minus_ok, 2 * n + h)
                    nc.tensor.matmul(ps_score[:, 0:P], qc[:, 0:P], kc[:, 0:P], start=True, stop=False)
                    nc.tensor.matmul(ps_score[:, 0:P], sh.ident16[:], sh.future16[:], start=False, stop=True)
                    nc.tensor.matmul(ps_score[:, P:TRI], qc[:, P:SEQ], kc, start=True, stop=False)
                    nc.tensor.matmul(ps_score[:, SEQ:TRI], sh.ident16[:], sh.future16[:], start=False,
                                     stop=True).then_inc(score_mm, 1)

                def lookup_sum(n, h):
                    pe.wait_ge(look_ok, 2 * n + h + 1)
                    pe.wait_ge(term_ok, 2 * n + h + 1)
                    reached(pe, gated_ok, 2 * n + h)
                    T, L = term[:, h, :], look[:, h, :]
                    nc.tensor.matmul(ps_su[:, P:TRI], T[:, SEQ:TRI], L[:, P:TRI], start=True, stop=False)
                    nc.tensor.matmul(ps_su[:, P:SEQ], T[:, P:SEQ], L[:, 0:P], start=False, stop=True)
                    nc.tensor.matmul(ps_su[:, 0:P], T[:, 0:P], L[:, 0:P], start=True, stop=True).then_inc(su_mm, 1)

                def turn(n, h):
                    pe.wait_ge(prob_ok, 2 * n + h + 1)
                    reached(pe, probT_ok, 2 * n + h)
                    for b in range(3):
                        ins = nc.tensor.transpose(ps_turn[:, b * P:(b + 1) * P], prob[:, h, b * P:(b + 1) * P],
                                                  sh.ident[:])
                    ins.then_inc(turned, 1)

                def attend(n, k):
                    pe.wait_ge(probT_ok, 2 * n + 2)
                    reached(pe, added, n)
                    v = qkv[:, k, 2, 1, :]
                    for h in range(2):
                        nc.tensor.matmul(ps_out[64 * h:64 * h + 64, 0:SEQ], v[:, 64 * h:64 * h + 64],
                                         probT[:, h, 0:SEQ], start=True, stop=False)
                    for h in range(2):
                        ins = nc.tensor.matmul(ps_out[64 * h:64 * h + 64, P:SEQ], v[:, P + 64 * h:P + 64 * h + 64],
                                               probT[:, h, SEQ:TRI], start=False, stop=True)
                    ins.then_inc(out_mm, 1)

                def output(n):
                    pe.wait_ge(heads_ok, n + 1)
                    pe.wait_ge(wo_in, 16 * (n // BATCH + 1))
                    for t in range(2):
                        ins = nc.tensor.matmul(ps_out[:, SEQ + t * P:SEQ + (t + 1) * P], headsT[:, t * P:(t + 1) * P],
                                               wo[:], start=True, stop=True)
                    ins.then_inc(y_mm, 1)

                def body(n, k):
                    q, a, o, y = (live(n - lag, STEPS) for lag in range(4))
                    ka = 1 - k
                    if a:
                        look_and_term(n - 1, ka, 0)
                    if q:
                        project(n, k, 0)
                    if y:
                        output(n - 3)
                    if a:
                        lookup_sum(n - 1, 0)
                        score(n - 1, ka, 0)
                    if o:
                        turn(n - 2, 1)
                    if a:
                        look_and_term(n - 1, ka, 1)
                    if q:
                        project(n, k, 1)
                    if o:
                        attend(n - 2, k)
                    if a:
                        lookup_sum(n - 1, 1)
                        score(n - 1, ka, 1)
                    if q:
                        project(n, k, 2)
                    if a:
                        turn(n - 1, 0)
                pe.wait_ge(masks, 4)
                skewed(pe, STEPS, 3, body)

            @block.scalar
            def _(act):
                def keep(n, k, j):
                    act.wait_ge(projected, 3 * n + j + 1)
                    reached(act, score_mm, 2 * n - 2)
                    if j == 2:
                        reached(act, out_mm, n - 1)
                    nc.scalar.activation(qkv[:, k, j, :, :].rearrange("p a b -> p (a b)"), proj[:, (k + j) % 2, :], ACT.Copy,
                                         scale=SCALE if j == 0 else 1.0).then_inc(kept, 1)

                def tanh_look(n, h):
                    act.wait_ge(look_mm, 2 * n + h + 1)
                    reached(act, look_ok, 2 * n + h - 1)
                    nc.scalar.activation(th_look[:, h, :], ps_look[:, 0:TRI], ACT.Tanh, scale=0.5).then_inc(th_look_ok, 1)

                def tanh_su(n, h):
                    act.wait_ge(su_mm, 2 * n + h + 1)
                    reached(act, gated_ok, 2 * n + h - 1)
                    nc.scalar.activation(th_su[:, h, :], ps_su[:, 0:TRI], ACT.Tanh, scale=-1.0).then_inc(th_su_ok, 1)

                def exps(n, h):
                    act.wait_ge(minus_ok, 2 * n + h + 1)
                    reached(act, turned, 2 * n + h - 1)
                    for t, (a, b) in enumerate(((0, P), (P, TRI))):
                        nc.scalar.activation(prob[:, h, a:b], minus[:, h, a:b], ACT.Exp, bias=low[:, h, t:t + 1],
                                             scale=-1.0, accum_out=total[:, h, t:t + 1]).then_inc(exp_ok, 1)

                def heads(n):
                    act.wait_ge(out_mm, n + 1)
                    reached(act, y_mm, n)
                    nc.scalar.activation(headsT[:], ps_out[:, 0:SEQ], ACT.Copy).then_inc(heads_ok, 1)

                def body(n, k):
                    q, a, o = live(n, STEPS), live(n - 1, STEPS), live(n - 2, STEPS)
                    if a:
                        tanh_look(n - 1, 0)
                    if o:
                        exps(n - 2, 1)
                    if q:
                        keep(n, k, 0)
                    if a:
                        tanh_su(n - 1, 0)
                        tanh_look(n - 1, 1)
                        exps(n - 1, 0)
                    if q:
                        keep(n, k, 1)
                    if o:
                        heads(n - 2)
                    if a:
                        tanh_su(n - 1, 1)
                    if q:
                        keep(n, k, 2)
                skewed(act, STEPS, 2, body)

            @block.vector
            def _(dve):
                def mask_term(n, h):
                    dve.wait_ge(term_mm, 2 * n + h + 1)
                    reached(dve, su_mm, 2 * n + h - 1)
                    nc.vector.tensor_tensor(term[:, h, :], ps_term[:, 0:TRI], causal[:], ALU.mult).then_inc(term_ok, 1)

                def mask_look(n, h):
                    dve.wait_ge(th_look_ok, 2 * n + h + 1)
                    reached(dve, su_mm, 2 * n + h - 1)
                    nc.vector.scalar_tensor_tensor(out=look[:, h, :], in0=th_look[:, h, :], scalar=1.0, in1=ahead[:],
                                                   op0=ALU.add, op1=ALU.mult).then_inc(look_ok, 1)

                def gate(n, h):
                    dve.wait_ge(th_su_ok, 2 * n + h + 1)
                    reached(dve, minus_ok, 2 * n + h - 1)
                    nc.vector.scalar_tensor_tensor(out=gated[:, h, :], in0=th_su[:, h, :], scalar=1.0,
                                                   in1=ps_su[:, 0:TRI], op0=ALU.add, op1=ALU.mult).then_inc(gated_ok, 1)

                def may_lower(n, h):
                    dve.wait_ge(gated_ok, 2 * n + h + 1)
                    dve.wait_ge(score_mm, 2 * n + h + 1)
                    reached(dve, exp_ok, 2 * (2 * n + h - 1))

                def lowest(n, h):
                    for t, (a, b) in enumerate(((0, P), (P, TRI))):
                        ins = nc.vector.tensor_tensor_reduce(
                            out=minus[:, h, a:b], in0=gated[:, h, a:b], in1=ps_score[:, a:b], scale=-1.0, scalar=3.0e38,
                            op0=ALU.add, op1=ALU.min, accum_out=low[:, h, t:t + 1])
                    ins.then_inc(minus_ok, 1)

                def normalise(n, h):
                    dve.wait_ge(exp_ok, 2 * (2 * n + h) + 2)
                    nc.vector.reciprocal(inv[:, h, :], total[:, h, :]).then_inc(inv_ok, 1)
                    dve.wait_ge(inv_ok, 2 * n + h + 1)
                    for t, (a, b) in enumerate(((0, P), (P, TRI))):
                        ins = nc.vector.tensor_scalar(prob[:, h, a:b], prob[:, h, a:b], inv[:, h, t:t + 1], None, ALU.mult)
                    ins.then_inc(prob_ok, 1)

                def keep_turned(n, h):
                    dve.wait_ge(turned, 2 * n + h + 1)
                    reached(dve, out_mm, n)
                    nc.vector.tensor_copy(probT[:, h, :], ps_turn[:, 0:TRI]).then_inc(probT_ok, 1)

                def add(n):
                    dve.wait_ge(y_mm, n + 1)
                    x = sh.X[:, bass.ds((n % BATCH) * 2, 2), :]
                    nc.vector.tensor_tensor(x, x, ps_out[:, SEQ:512].rearrange("p (t c) -> p t c", t=2),
                                            ALU.add).then_inc(added, 1)

                def body(n, k):
                    a, o, y = live(n - 1, STEPS), live(n - 2, STEPS), live(n - 3, STEPS)
                    if a:
                        mask_look(n - 1, 0)
                        mask_term(n - 1, 0)
                    if o:
                        normalise(n - 2, 1)
                    if y:
                        add(n - 3)
                    if a:
                        gate(n - 1, 0)
                        may_lower(n - 1, 0)
                    if o:
                        keep_turned(n - 2, 1)
                    if a:
                        lowest(n - 1, 0)
                        mask_term(n - 1, 1)
                        mask_look(n - 1, 1)
                        normalise(n - 1, 0)
                        gate(n - 1, 1)
                        may_lower(n - 1, 1)
                        nc.vector.memset(carrier[:], 0.0)
                        lowest(n - 1, 1)
                        keep_turned(n - 1, 0)
                dve.wait_ge(masks, 4)
                skewed(dve, STEPS, 3, body)


def latent_attention(nc, sh, w_down, w_up, w_q, w_out):
    SCALE = 64 ** -0.5
    HD = HEADS * 64
    CHUNKS = TOK // 512
    with Phase(nc, "ab") as ph:
        wd = ph.sb("wd", [P, P])
        latT = ph.sb("latT", [P, TOK])
        w = ph.sb("w", [P, 3, P])
        wo = ph.sb("wo", [P, P])
        xs = ph.sb("xs", [P, 2, SEQ])
        qkv = ph.sb("qkv", [P, 2, 3, SEQ])
        prob, probT = ph.sb("prob", [P, 2, TRI]), ph.sb("probT", [P, 2, TRI])
        top, low, total, inv = (ph.sb(x, [P, 2, 2]) for x in ("top", "low", "total", "inv"))
        headsT = ph.sb("headsT", [P, SEQ])
        proj, ps_score, ps_turn = (ph.bank(x, (P, 2, 512)) for x in ("proj", "ps_score", "ps_turn"))
        ps_out = ph.bank("ps_out", (P, 2, 512))
        (wd_in, lat_mm, lat_ok, w_in, wo_in, staged, projected, kept, score_mm, turned, out_mm, y_mm, exp_ok, heads_ok,
         top_ok, low_ok, inv_ok, prob_ok, probT_ok, added) = (ph.sem(x) for x in (
             "wd_in", "lat_mm", "lat_ok", "w_in", "wo_in", "staged", "projected", "kept", "score_mm", "turned",
             "out_mm", "y_mm", "exp_ok", "heads_ok", "top_ok", "low_ok", "inv_ok", "prob_ok", "probT_ok", "added"))

        with nc.Block() as block:
            @block.sync
            def _(sp):
                sp.dma_start(wd[:], w_down).then_inc(wd_in, 16)
                for p in turns(sp, PAIRS):
                    reached(sp, projected, 2 * BATCH * p)
                    sp.dma_start(w[:, 0, :], w_q[:, bass.ds(p * P, P)]).then_inc(w_in, 16)
                    sp.dma_start(w[:, 1:3, :], w_up.rearrange("c (j q) -> c j q", j=2)[:, :, bass.ds(p * P, P)]
                                 ).then_inc(w_in, 16)
                    reached(sp, y_mm, BATCH * p)
                    sp.dma_start(wo[:], w_out[bass.ds(p * P, P), :]).then_inc(wo_in, 16)

            @block.gpsimd
            def _(pool):
                def stage(n, k):
                    reached(pool, projected, 2 * (n - 1))
                    nc.gpsimd.tensor_copy(xs[:, k, :], latT[:, bass.ds((n % BATCH) * SEQ, SEQ)]).then_inc(staged, 1)
                pool.wait_ge(lat_ok, CHUNKS)
                skewed(pool, STEPS, 2, lambda n, k: stage(n, k) if live(n, STEPS) else None)

            @block.tensor
            def _(pe):
                def project(n, k, j):
                    reached(pe, kept, 2 * n + j - 1)
                    if j == 0:
                        pe.wait_ge(staged, n + 1)
                        pe.wait_ge(w_in, 32 * (n // BATCH + 1))
                        nc.tensor.matmul(proj[:, 0, 0:SEQ], w[:, 0, :], sh.XNT[:, bass.ds((n % BATCH) * SEQ, SEQ)],
                                         start=True, stop=True)
                        nc.tensor.matmul(proj[:, 0, SEQ:512], w[:, 1, :], xs[:, k, :], start=True,
                                         stop=True).then_inc(projected, 1)
                    else:
                        for t in range(2):
                            ins = nc.tensor.matmul(proj[:, 1, t * P:(t + 1) * P], xs[:, k, t * P:(t + 1) * P], w[:, 2, :],
                                                   start=True, stop=True)
                        ins.then_inc(projected, 1)

                def score(n, k, h):
                    q, kk = (qkv[64 * h:64 * h + 64, k, i, :] for i in range(2))
                    bank = ps_score[:, h, :]
                    pe.wait_ge(kept, 2 * n + 1)
                    reached(pe, exp_ok, 2 * (2 * n + h - 1))
                    nc.tensor.matmul(bank[:, 0:P], q[:, 0:P], kk[:, 0:P], start=True, stop=False)
                    nc.tensor.matmul(bank[:, 0:P], sh.ident16[:], sh.future16[:], start=False, stop=True)
                    nc.tensor.matmul(bank[:, P:TRI], q[:, P:SEQ], kk, start=True, stop=False)
                    nc.tensor.matmul(bank[:, SEQ:TRI], sh.ident16[:], sh.future16[:], start=False,
                                     stop=True).then_inc(score_mm, 1)

                def turn(n, h):
                    pe.wait_ge(prob_ok, 2 * n + h + 1)
                    reached(pe, probT_ok, 2 * n + h - 1)
                    for b in range(3):
                        ins = nc.tensor.transpose(ps_turn[:, h, b * P:(b + 1) * P], prob[:, h, b * P:(b + 1) * P],
                                                  sh.ident[:])
                    ins.then_inc(turned, 1)

                def attend(n, k):
                    pe.wait_ge(kept, 2 * n + 2)
                    pe.wait_ge(probT_ok, 2 * n + 2)
                    reached(pe, heads_ok, n)
                    v = qkv[:, k, 2, :]
                    for h in range(2):
                        nc.tensor.matmul(ps_out[64 * h:64 * h + 64, 0, 0:SEQ], v[:, 64 * h:64 * h + 64],
                                         probT[:, h, 0:SEQ], start=True, stop=False)
                    for h in range(2):
                        ins = nc.tensor.matmul(ps_out[64 * h:64 * h + 64, 0, P:SEQ], v[:, P + 64 * h:P + 64 * h + 64],
                                               probT[:, h, SEQ:TRI], start=False, stop=True)
                    ins.then_inc(out_mm, 1)

                def output(n):
                    pe.wait_ge(heads_ok, n + 1)
                    pe.wait_ge(wo_in, 16 * (n // BATCH + 1))
                    reached(pe, added, n)
                    for t in range(2):
                        ins = nc.tensor.matmul(ps_out[:, 1, t * P:(t + 1) * P], headsT[:, t * P:(t + 1) * P], wo[:],
                                               start=True, stop=True)
                    ins.then_inc(y_mm, 1)

                def body(n, k):
                    q, a, o = live(n, STEPS), live(n - 1, STEPS), live(n - 2, STEPS)
                    if a:
                        score(n - 1, 1 - k, 0)
                        score(n - 1, 1 - k, 1)
                    if q:
                        project(n, k, 0)
                    if o:
                        attend(n - 2, k)
                    if q:
                        project(n, k, 1)
                    if a:
                        turn(n - 1, 0)
                    if o:
                        output(n - 2)
                    if a:
                        turn(n - 1, 1)

                pe.wait_ge(wd_in, 16)
                for c in range(CHUNKS):
                    reached(pe, lat_ok, c - 1)
                    nc.tensor.matmul(proj[:, c % 2, :], wd[:], sh.XNT[:, c * 512:(c + 1) * 512], start=True,
                                     stop=True).then_inc(lat_mm, 1)
                pe.wait_ge(lat_ok, CHUNKS)
                skewed(pe, STEPS, 2, body)

            @block.scalar
            def _(act):
                def keep(n, k, j):
                    act.wait_ge(projected, 2 * n + j + 1)
                    if j == 0:
                        reached(act, score_mm, 2 * n - 2)
                        nc.scalar.activation(qkv[:, k, 0:2, :].rearrange("p a b -> p (a b)"), proj[:, 0, :],
                                             ACT.Copy).then_inc(kept, 1)
                    else:
                        reached(act, out_mm, n - 1)
                        nc.scalar.activation(qkv[:, k, 2, :], proj[:, 1, 0:SEQ], ACT.Copy).then_inc(kept, 1)

                def exps(n, h):
                    act.wait_ge(low_ok, 2 * n + h + 1)
                    reached(act, turned, 2 * n + h - 1)
                    for t, (a, b) in enumerate(((0, P), (P, TRI))):
                        nc.scalar.activation(prob[:, h, a:b], ps_score[:, h, a:b], ACT.Exp, bias=low[:, h, t:t + 1],
                                             scale=SCALE, accum_out=total[:, h, t:t + 1]).then_inc(exp_ok, 1)

                def heads(n):
                    act.wait_ge(out_mm, n + 1)
                    reached(act, y_mm, n)
                    nc.scalar.activation(headsT[:], ps_out[:, 0, 0:SEQ], ACT.Copy).then_inc(heads_ok, 1)

                def body(n, k):
                    q, a, o = live(n, STEPS), live(n - 1, STEPS), live(n - 2, STEPS)
                    if a:
                        exps(n - 1, 0)
                    if q:
                        keep(n, k, 0)
                    if a:
                        exps(n - 1, 1)
                    if o:
                        heads(n - 2)
                    if q:
                        keep(n, k, 1)

                for c in range(CHUNKS):
                    act.wait_ge(lat_mm, c + 1)
                    nc.scalar.activation(latT[:, c * 512:(c + 1) * 512], proj[:, c % 2, :], ACT.Copy).then_inc(lat_ok, 1)
                skewed(act, STEPS, 2, body)

            @block.vector
            def _(dve):
                def maximum(n, h):
                    dve.wait_ge(score_mm, 2 * n + h + 1)
                    reached(dve, exp_ok, 2 * (2 * n + h - 1))
                    for t, (a, b) in enumerate(((0, P), (P, TRI))):
                        ins = nc.vector.tensor_reduce(top[:, h, t:t + 1], ps_score[:, h, a:b], AX.X, ALU.max)
                    ins.then_inc(top_ok, 1)
                    dve.wait_ge(top_ok, 2 * n + h + 1)
                    nc.vector.tensor_scalar(low[:, h, :], top[:, h, :], -SCALE, None, ALU.mult).then_inc(low_ok, 1)

                def normalise(n, h):
                    dve.wait_ge(exp_ok, 2 * (2 * n + h) + 2)
                    nc.vector.reciprocal(inv[:, h, :], total[:, h, :]).then_inc(inv_ok, 1)
                    dve.wait_ge(inv_ok, 2 * n + h + 1)
                    for t, (a, b) in enumerate(((0, P), (P, TRI))):
                        ins = nc.vector.tensor_scalar(prob[:, h, a:b], prob[:, h, a:b], inv[:, h, t:t + 1], None, ALU.mult)
                    ins.then_inc(prob_ok, 1)

                def keep_turned(n, h):
                    dve.wait_ge(turned, 2 * n + h + 1)
                    reached(dve, out_mm, n)
                    nc.vector.tensor_copy(probT[:, h, :], ps_turn[:, h, 0:TRI]).then_inc(probT_ok, 1)

                def add(n):
                    dve.wait_ge(y_mm, n + 1)
                    x = sh.X[:, bass.ds((n % BATCH) * 2, 2), :]
                    nc.vector.tensor_tensor(x, x, ps_out[:, 1, 0:SEQ].rearrange("p (t c) -> p t c", t=2),
                                            ALU.add).then_inc(added, 1)

                def body(n, k):
                    a, o = live(n - 1, STEPS), live(n - 2, STEPS)
                    if a:
                        maximum(n - 1, 0)
                    if o:
                        keep_turned(n - 2, 0)
                        keep_turned(n - 2, 1)
                    if a:
                        maximum(n - 1, 1)
                        normalise(n - 1, 0)
                        normalise(n - 1, 1)
                    if o:
                        add(n - 2)
                skewed(dve, STEPS, 2, body)


def top2_mixture(nc, sh, name, Wg, bg, W1, b1, W2, b2, gamma, beta):
    E, F = 8, 256
    CHUNKS = TOK // 512
    N = E * CHUNKS
    with Phase(nc, name) as ph:
        wg = ph.sb("wg", [P, E])
        bgb = ph.sb("bgb", [P, E])
        w1, b1s = ph.sb("w1", [P, E, F]), ph.sb("b1s", [P, E, 2])
        w2, b2s = ph.sb("w2", [P, E, 2, P]), ph.sb("b2s", [E, P])
        gam, bet = ph.sb("gam", [P, P]), ph.sb("bet", [P, P])
        prefer = ph.sb("prefer", [P, E])
        logit, hit, first, second, gate = (ph.sb(x, [P, TILES, E]) for x in ("logit", "hit", "first", "second", "gate"))
        m1, m2, best, e, weight1, weight2 = (ph.sb(x, [P, TILES]) for x in ("m1", "m2", "best", "e", "weight1", "weight2"))
        gateT = ph.sb("gateT", [E, TOK])
        hid = ph.sb("hid", [P, 2, 2, 512])
        acc = sh.XN
        ps_logit = ph.bank("ps_logit")
        ps_hid = ph.bank("ps_hid", (P, 4, 512))
        ps_y = ph.bank("ps_y", (P, 2, 512))
        (loaded, wl, preferred, logit_mm, chain, exp_in, exp_ok, gate_ok, gateT_mm, gateT_ok, b2_mm, b2_ok, up_mm, hid_ok,
         down_mm, acc_ok) = (ph.sem(x) for x in (
             "loaded", "wl", "preferred", "logit_mm", "chain", "exp_in", "exp_ok", "gate_ok", "gateT_mm", "gateT_ok",
             "b2_mm", "b2_ok", "up_mm", "hid_ok", "down_mm", "acc_ok"))
        with nc.Block() as block:
            @block.sync
            def _(sp):
                sp.dma_start(wg[:], Wg).then_inc(wl, 16)
                sp.dma_start(bgb[:], bg.partition_broadcast(P)).then_inc(wl, 16)
                sp.dma_start(b2s[:], b2).then_inc(wl, 16)
                sp.dma_start(w1[:], W1.rearrange("e d f -> d e f")).then_inc(loaded, 16)
                sp.dma_start(w2[:], W2.rearrange("e (j f) d -> f e j d", j=2)).then_inc(loaded, 16)
                with nc.allow_non_contiguous_dma("the biases are a few thousand values"):
                    sp.dma_start(b1s[:], b1.rearrange("e (j f) -> f e j", j=2)).then_inc(loaded, 16)
                sp.dma_start(gam[:], gamma.partition_broadcast(P)).then_inc(loaded, 16)
                sp.dma_start(bet[:], beta.partition_broadcast(P)).then_inc(loaded, 16)

            @block.gpsimd
            def _(pool):
                for i in range(E):
                    ins = nc.gpsimd.memset(prefer[:, i:i + 1], float(E - i))
                ins.then_inc(preferred, 1)

            @block.tensor
            def _(pe):
                pe.wait_ge(wl, 48)
                for t in range(TILES):
                    ins = nc.tensor.matmul(ps_logit[:, t * E:(t + 1) * E], sh.XNT[:, t * P:(t + 1) * P], wg[:],
                                           start=True, stop=True)
                ins.then_inc(logit_mm, 1)
                pe.wait_ge(gate_ok, 1)
                for c in range(CHUNKS):
                    reached(pe, gateT_ok, c - 1)
                    for i in range(4):
                        ins = nc.tensor.transpose(ps_hid[0:E, c % 2, i * P:(i + 1) * P], gate[:, 4 * c + i, :], sh.ident[:])
                    ins.then_inc(gateT_mm, 1)
                for c in range(CHUNKS):
                    pe.wait_ge(gateT_ok, c + 1)
                    reached(pe, b2_ok, c - 1)
                    for i in range(4):
                        t = 4 * c + i
                        ins = nc.tensor.matmul(ps_y[:, c % 2, i * P:(i + 1) * P], gateT[:, t * P:(t + 1) * P], b2s[:],
                                               start=True, stop=True)
                    ins.then_inc(b2_mm, 1)

                def up(n, e_):
                    bank = 2 * (e_ % 2)
                    reached(pe, hid_ok, 2 * (n - 1))
                    for j in range(2):
                        nc.tensor.matmul(ps_hid[:, bank + j, :], w1[:, e_, j * P:(j + 1) * P],
                                         sh.XNT[:, bass.ds((n // E) * 512, 512)], start=True,
                                         stop=True).then_inc(up_mm, 1)

                def down(n, e_):
                    pe.wait_ge(hid_ok, 2 * (n + 1))
                    reached(pe, acc_ok, n - 1)
                    for i in range(4):
                        for j in range(2):
                            ins = nc.tensor.matmul(ps_y[:, e_ % 2, i * P:(i + 1) * P], hid[:, e_ % 2, j, i * P:(i + 1) * P],
                                                   w2[:, e_, j, :], start=j == 0, stop=j == 1)
                    ins.then_inc(down_mm, 1)

                def body(n, e_):
                    if live(n, N):
                        up(n, e_)
                    if live(n - 1, N):
                        down(n - 1, (e_ - 1) % E)
                pe.wait_ge(loaded, 80)
                pe.wait_ge(gateT_ok, CHUNKS)
                pe.wait_ge(b2_ok, CHUNKS)
                skewed(pe, N, 1, body, E)

            @block.scalar
            def _(act):
                act.wait_ge(exp_in, 1)
                nc.scalar.activation(e[:], m2[:], ACT.Exp).then_inc(exp_ok, 1)
                for c in range(CHUNKS):
                    act.wait_ge(gateT_mm, c + 1)
                    nc.scalar.activation(gateT[:, c * 512:(c + 1) * 512], ps_hid[0:E, c % 2, :],
                                         ACT.Copy).then_inc(gateT_ok, 1)

                def relu(n, e_):
                    reached(act, down_mm, n - 1)
                    for j in range(2):
                        act.wait_ge(up_mm, 2 * n + j + 1)
                        nc.scalar.activation(hid[:, e_ % 2, j, :], ps_hid[:, 2 * (e_ % 2) + j, :], ACT.Relu,
                                             bias=b1s[:, e_, j:j + 1]).then_inc(hid_ok, 1)
                act.wait_ge(loaded, 80)
                skewed(act, N, 1, lambda n, e_: relu(n, e_) if live(n, N) else None, E)

            @block.vector
            def _(dve):
                wide = [P, TILES, E]
                count = [0]

                def then(ins):
                    count[0] += 1
                    ins.then_inc(chain, 1)
                    dve.wait_ge(chain, count[0])

                def choose(onehot, top):
                    then(nc.vector.tensor_reduce(top[:], logit[:], AX.X, ALU.max))
                    then(nc.vector.tensor_tensor(hit[:], logit[:], top[:].unsqueeze(2).broadcast_to(wide), ALU.is_equal))
                    then(nc.vector.tensor_tensor(hit[:], hit[:], prefer[:].unsqueeze(1).broadcast_to(wide), ALU.mult))
                    then(nc.vector.tensor_reduce(best[:], hit[:], AX.X, ALU.max))
                    then(nc.vector.tensor_tensor(onehot[:], hit[:], best[:].unsqueeze(2).broadcast_to(wide), ALU.is_equal))

                dve.wait_ge(wl, 48)
                dve.wait_ge(preferred, 1)
                dve.wait_ge(logit_mm, 1)
                then(nc.vector.tensor_tensor(logit[:], ps_logit[:, 0:TILES * E].rearrange("p (t e) -> p t e", e=E),
                                             bgb[:].unsqueeze(1).broadcast_to(wide), ALU.add))
                choose(first, m1)
                then(nc.vector.scalar_tensor_tensor(out=logit[:], in0=first[:], scalar=NEG, in1=logit[:], op0=ALU.mult,
                                                    op1=ALU.add))
                choose(second, m2)
                nc.vector.tensor_tensor(m2[:], m2[:], m1[:], ALU.subtract).then_inc(exp_in, 1)
                dve.wait_ge(exp_ok, 1)
                then(nc.vector.tensor_scalar(m1[:], e[:], 1.0, None, ALU.add))
                then(nc.vector.reciprocal(weight1[:], m1[:]))
                then(nc.vector.tensor_tensor(weight2[:], e[:], weight1[:], ALU.mult))
                then(nc.vector.tensor_tensor(first[:], first[:], weight1[:].unsqueeze(2).broadcast_to(wide), ALU.mult))
                then(nc.vector.tensor_tensor(second[:], second[:], weight2[:].unsqueeze(2).broadcast_to(wide), ALU.mult))
                nc.vector.tensor_tensor(gate[:], first[:], second[:], ALU.add).then_inc(gate_ok, 1)
                for c in range(CHUNKS):
                    dve.wait_ge(b2_mm, c + 1)
                    nc.vector.tensor_tensor(acc[:, 4 * c:4 * c + 4, :], acc[:, 4 * c:4 * c + 4, :],
                                            ps_y[:, c % 2, :].rearrange("p (t c) -> p t c", t=4), ALU.add).then_inc(b2_ok, 1)
                dve.wait_ge(b2_ok, CHUNKS)
                dve.wait_ge(gate_ok, 1)

                def weigh(n, e_):
                    dve.wait_ge(down_mm, n + 1)
                    reached(dve, acc_ok, n)
                    for i in range(4):
                        a = acc[:, bass.ds((n // E) * 4 + i, 1), :].rearrange("p a c -> p (a c)")
                        ins = nc.vector.scalar_tensor_tensor(
                            out=a, in0=ps_y[:, e_ % 2, i * P:(i + 1) * P],
                            scalar=gate[:, bass.ds((n // E) * 4 + i, 1), e_:e_ + 1].rearrange("p a c -> p (a c)"), in1=a,
                            op0=ALU.mult, op1=ALU.add)
                    ins.then_inc(acc_ok, 1)
                skewed(dve, N, 1, lambda n, e_: weigh(n, e_) if live(n, N) else None, E)

        st, mean, rstd, work = ph.sb("st", [P, TILES, 6]), ph.sb("mean", [P, TILES]), ph.sb("rstd", [P, TILES]), \
            ph.sb("work", [P, 7, TILES])
        stats, chain2, sqrt_in, sqrt_done, centred, scaled, shifted, summed = (ph.sem(x) for x in (
            "stats", "chain2", "sqrt_in", "sqrt_done", "centred", "scaled", "shifted", "summed"))
        with nc.Block() as block:
            @block.vector
            def _(dve):
                with dve.Fori(0, TILES) as t:
                    nc.vector.bn_stats(st[:, bass.ds(t, 1), :].rearrange("p a s -> p (a s)"),
                                       acc[:, bass.ds(t, 1), :].rearrange("p a c -> p (a c)")).then_inc(stats, 1)
                dve.wait_ge(stats, TILES)
                row_statistics(nc, dve, st, mean, rstd, work, chain2, sqrt_in, sqrt_done)
                with dve.Fori(0, TILES) as t:
                    a = acc[:, bass.ds(t, 1), :].rearrange("p a c -> p (a c)")
                    nc.vector.tensor_scalar(a, a, mean[:, bass.ds(t, 1)], rstd[:, bass.ds(t, 1)], ALU.subtract,
                                            ALU.mult).then_inc(centred, 1)
                for c in turns(dve, CHUNKS):
                    a, x = acc[:, bass.ds(4 * c, 4), :], sh.X[:, bass.ds(4 * c, 4), :]
                    dve.wait_ge(centred, 4 * c + 4)
                    nc.vector.tensor_tensor(a, a, gam[:].unsqueeze(1).broadcast_to([P, 4, P]), ALU.mult).then_inc(scaled, 1)
                    dve.wait_ge(shifted, c + 1)
                    dve.wait_ge(scaled, c + 1)
                    nc.vector.tensor_tensor(x, x, a, ALU.add).then_inc(summed, 1)

            @block.scalar
            def _(act):
                act.wait_ge(sqrt_in, 1)
                nc.scalar.activation(work[:, 6, :], work[:, 5, :], ACT.Sqrt).then_inc(sqrt_done, 1)

            @block.gpsimd
            def _(pool):
                with pool.Fori(0, CHUNKS) as c:
                    x = sh.X[:, bass.ds(4 * c, 4), :]
                    nc.gpsimd.tensor_tensor(x, x, bet[:].unsqueeze(1).broadcast_to([P, 4, P]), ALU.add).then_inc(shifted, 1)


def routed_mixture(nc, sh, ew, name, gate_w):
    E, F = 8, 256
    CHUNKS = TOK // 512
    N = E * CHUNKS
    with Phase(nc, name) as ph:
        wg = ph.sb("wg", [P, E])
        prefer = ph.sb("prefer", [P, E])
        logit, hit, chosen = (ph.sb(x, [P, TILES, E]) for x in ("logit", "hit", "chosen"))
        top, best, score, e = (ph.sb(x, [P, TILES]) for x in ("top", "best", "score", "e"))
        xr = ph.sb("xr", [P, 2, 4, P])
        xsT = ph.sb("xsT", [P, TOK])
        th, gu, hid = ph.sb("th", [P, 2, 512]), ph.sb("gu", [P, 2, 512]), ph.sb("hid", [P, 2, 2, 512])
        ps_g, ps_u, ps_y, ps_t = (ph.bank(x, (P, 2, 512)) for x in ("ps_g", "ps_u", "ps_y", "ps_t"))
        (wl, preferred, logit_mm, chain, exp_in, exp_ok, scaled, turned, xs_ok, up_mm, th_ok, gu_ok, hid_ok, down_mm,
         acc_ok) = (ph.sem(x) for x in (
             "wl", "preferred", "logit_mm", "chain", "exp_in", "exp_ok", "scaled", "turned", "xs_ok", "up_mm", "th_ok",
             "gu_ok", "hid_ok", "down_mm", "acc_ok"))

        def each_step(eng, early, late=None):
            def run(f, n, k):
                if f is None or (isinstance(n, int) and not -CHUNKS <= n < N):
                    return
                if isinstance(n, int) and n < 0:
                    f(n + CHUNKS, n % 2, E, n + CHUNKS)
                else:
                    f(n + CHUNKS, k % 2, k % E, n // E)

            for n in range(-CHUNKS, 0):
                run(early, n, n)
                run(late, n - 1, n - 1)

            for n in range(E):
                run(early, n, n)
                run(late, n - 1, n - 1)
            with eng.Fori(1, N // E) as c:
                for k in range(E):
                    run(early, c * E + k, k)
                    run(late, c * E + k - 1, (k - 1) % E)
            run(late, N - 1, E - 1)

        with nc.Block() as block:
            @block.sync
            def _(sp):
                with nc.allow_non_contiguous_dma("the router has a thousand weights"):
                    sp.dma_start(wg[:], gate_w.rearrange("e h -> h e")).then_inc(wl, 16)

            @block.gpsimd
            def _(pool):
                for i in range(E):
                    ins = nc.gpsimd.memset(prefer[:, i:i + 1], float(E - i))
                ins.then_inc(preferred, 1)

            @block.tensor
            def _(pe):
                pe.wait_ge(wl, 16)
                for t in range(TILES):
                    ins = nc.tensor.matmul(ps_g[:, 0, t * E:(t + 1) * E], sh.XNT[:, t * P:(t + 1) * P], wg[:],
                                           start=True, stop=True)
                ins.then_inc(logit_mm, 1)
                for m in turns(pe, CHUNKS // 2):
                    for k in range(2):
                        g = 2 * m + k
                        pe.wait_ge(scaled, g + 1)
                        reached(pe, xs_ok, 2 * m)
                        for i in range(4):
                            ins = nc.tensor.transpose(ps_t[:, k, i * P:(i + 1) * P], xr[:, k, i, :], sh.ident[:])
                        ins.then_inc(turned, 1)

                def up(s, k, e_, c):
                    x = sh.XNT if e_ == E else xsT
                    for j in range(2):
                        reached(pe, hid_ok, 2 * (s - 1) + j + 1)
                        for ps, w in ((ps_g, ew.gate), (ps_u, ew.up)):
                            ins = nc.tensor.matmul(ps[:, j, :], w[:, 2 * e_ + j, :], x[:, bass.ds(c * 512, 512)],
                                                   start=True, stop=True)
                        ins.then_inc(up_mm, 1)

                def down(s, k, e_, c):
                    pe.wait_ge(hid_ok, 2 * (s + 1))
                    reached(pe, acc_ok, s - 1)
                    for i in range(4):
                        for j in range(2):
                            ins = nc.tensor.matmul(ps_y[:, k, i * P:(i + 1) * P], hid[:, k, j, i * P:(i + 1) * P],
                                                   ew.down[:, 2 * e_ + j, :], start=j == 0, stop=j == 1)
                    ins.then_inc(down_mm, 1)
                pe.wait_ge(exp_in, 1)
                pe.wait_ge(xs_ok, CHUNKS)
                each_step(pe, up, down)

            @block.scalar
            def _(act):
                act.wait_ge(exp_in, 1)
                nc.scalar.activation(e[:], top[:], ACT.Exp, scale=-1.0).then_inc(exp_ok, 1)
                for m in turns(act, CHUNKS // 2):
                    for k in range(2):
                        g = 2 * m + k
                        act.wait_ge(turned, g + 1)
                        nc.scalar.activation(xsT[:, bass.ds(g * 512, 512)], ps_t[:, k, :], ACT.Copy).then_inc(xs_ok, 1)

                def tanh(s, k, e_, c):
                    for j in range(2):
                        act.wait_ge(up_mm, 2 * s + j + 1)
                        reached(act, gu_ok, 2 * (s - 1) + j + 1)
                        nc.scalar.activation(th[:, j, :], ps_g[:, j, :], ACT.Tanh, scale=0.5).then_inc(th_ok, 1)
                each_step(act, tanh)

            @block.vector
            def _(dve):
                wide = [P, TILES, E]
                count = [0]

                def then(ins):
                    count[0] += 1
                    ins.then_inc(chain, 1)
                    dve.wait_ge(chain, count[0])

                dve.wait_ge(wl, 16)
                dve.wait_ge(preferred, 1)
                dve.wait_ge(logit_mm, 1)
                then(nc.vector.tensor_copy(logit[:], ps_g[:, 0, 0:TILES * E].rearrange("p (t e) -> p t e", e=E)))
                then(nc.vector.tensor_reduce(top[:], logit[:], AX.X, ALU.max))
                then(nc.vector.tensor_tensor(hit[:], logit[:], top[:].unsqueeze(2).broadcast_to(wide), ALU.is_equal))
                hit_again = nc.vector.tensor_tensor(hit[:], hit[:], prefer[:].unsqueeze(1).broadcast_to(wide), ALU.mult)
                then(hit_again)
                then(nc.vector.tensor_reduce(best[:], hit[:], AX.X, ALU.max))
                nc.vector.tensor_tensor(chosen[:], hit[:], best[:].unsqueeze(2).broadcast_to(wide),
                                        ALU.is_equal).then_inc(exp_in, 1)
                dve.wait_ge(exp_ok, 1)
                then(nc.vector.tensor_scalar(best[:], e[:], 1.0, None, ALU.add))
                then(nc.vector.reciprocal(score[:], best[:]))
                for m in turns(dve, CHUNKS // 2):
                    for k in range(2):
                        g = 2 * m + k
                        reached(dve, turned, 2 * m)
                        for i in range(4):
                            ins = nc.vector.tensor_scalar(
                                xr[:, k, i, :], sh.XN[:, bass.ds(4 * g + i, 1), :].rearrange("p a c -> p (a c)"),
                                score[:, bass.ds(4 * g + i, 1)], None, ALU.mult)
                        ins.then_inc(scaled, 1)
                dve.wait_ge(exp_in, 1)

                def hidden(s, k, e_, c):
                    for j in range(2):
                        dve.wait_ge(th_ok, 2 * s + j + 1)
                        reached(dve, hid_ok, 2 * (s - 1) + j + 1)
                        nc.vector.scalar_tensor_tensor(out=gu[:, j, :], in0=th[:, j, :], scalar=1.0, in1=ps_g[:, j, :],
                                                       op0=ALU.add, op1=ALU.mult).then_inc(gu_ok, 1)
                        dve.wait_ge(gu_ok, 2 * s + j + 1)
                        reached(dve, down_mm, s - 1)
                        nc.vector.scalar_tensor_tensor(out=hid[:, k, j, :], in0=gu[:, j, :], scalar=0.5,
                                                       in1=ps_u[:, j, :], op0=ALU.mult, op1=ALU.mult).then_inc(hid_ok, 1)

                def collect(s, k, e_, c):
                    dve.wait_ge(down_mm, s + 1)
                    reached(dve, acc_ok, s)
                    if e_ == E:
                        x = sh.X[:, bass.ds(4 * c, 4), :]
                        nc.vector.tensor_tensor(x, x, ps_y[:, k, :].rearrange("p (t c) -> p t c", t=4),
                                                ALU.add).then_inc(acc_ok, 1)
                        return
                    for i in range(4):
                        x = sh.X[:, bass.ds(4 * c + i, 1), :].rearrange("p a c -> p (a c)")
                        ins = nc.vector.scalar_tensor_tensor(
                            out=x, in0=ps_y[:, k, i * P:(i + 1) * P],
                            scalar=chosen[:, bass.ds(4 * c + i, 1), e_:e_ + 1].rearrange("p a c -> p (a c)"), in1=x,
                            op0=ALU.mult, op1=ALU.add)
                    ins.then_inc(acc_ok, 1)
                each_step(dve, hidden, collect)


class ExpertWeights:

    def __init__(self, nc, ctx):
        def sb(name):
            return ctx.enter_context(nc.sbuf_tensor(name, [P, 18, P], F32))
        self.gate, self.up, self.down = sb("gateT"), sb("upT"), sb("downT")


def load_experts(nc, sh, ew, shared_gate, shared_up, shared_down, r_gate, r_up, r_down):
    with Phase(nc, "ew") as ph:
        raw = ph.sb("raw", [P, 3, 18, P])
        bank = ph.bank("bank", (P, 2, 512))
        loaded, turned, kept = ph.sem("loaded"), ph.sem("turned"), ph.sem("kept")
        groups = [(t, m, i) for t, m in ((ew.gate, 0), (ew.up, 1), (ew.down, 2)) for i in range(0, 18, 2)]
        with nc.Block() as block:
            @block.sync
            def _(sp):
                for m, (r, s) in enumerate(((r_gate, shared_gate), (r_up, shared_up))):
                    sp.dma_start(raw[:, m, 0:16, :], r.rearrange("e (j f) h -> f (e j) h", j=2)).then_inc(loaded, 16)
                    sp.dma_start(raw[:, m, 16:18, :], s.rearrange("(j f) h -> f j h", j=2)).then_inc(loaded, 16)
                sp.dma_start(raw[:, 2, 0:16, :].rearrange("p (e j) f -> p e (j f)", j=2),
                             r_down.rearrange("e h f -> h e f")).then_inc(loaded, 16)
                sp.dma_start(raw[:, 2, 16:18, :].rearrange("p j f -> p (j f)"), shared_down).then_inc(loaded, 16)

            @block.tensor
            def _(pe):
                pe.wait_ge(loaded, 96)
                for n, (_, m, i) in enumerate(groups):
                    reached(pe, kept, n - 1)
                    for b in range(2):
                        ins = nc.tensor.transpose(bank[:, n % 2, b * P:(b + 1) * P], raw[:, m, i + b, :], sh.ident[:])
                    ins.then_inc(turned, 1)

            @block.scalar
            def _(act):
                for n, (dst, m, i) in enumerate(groups):
                    act.wait_ge(turned, n + 1)
                    nc.scalar.activation(dst[:, i:i + 2, :].rearrange("p b c -> p (b c)"), bank[:, n % 2, 0:2 * P],
                                         ACT.Copy).then_inc(kept, 1)
                act.wait_ge(kept, len(groups))


def helical_attention(nc, sh, Wq, bq, Wk, bk, Wv, bv, Wo, bo, Whel, bhel):
    HD, HX = 8, 64
    TURNS = STEPS // 2
    HALF = SEQ // 2
    DOT = (HX // 2) / HD ** 0.5
    SCALE = 0.5 / (HX // 2)
    with Phase(nc, "la") as ph:
        woT = ph.sb("woT", [P, P])
        bob, bvb = ph.sb("bob", [P, P]), ph.sb("bvb", [P, P])
        qk = ph.sb("qk", [P, 2, TOK])
        v = ph.sb("v", [P, TILES, P])
        stack = ph.sb("stack", [P, 2, 2 * BATCH, HALF])
        helT = ph.sb("helT", [P, PAIRS, 2, P])
        bias = ph.sb("bias", [P, PAIRS, 2])
        heads = sh.XN

        with Phase(nc, "ls") as ps:
            raw = ps.sb("raw", [P, 4, P])
            wT = ps.sb("wT", [P, 4, P])
            hel = ps.sb("hel", [P, PAIRS, 2, P])
            pick = ps.sb("pick", [P, 2, 2, P])
            bqs, bks = ps.sb("bqs", [P, 1]), ps.sb("bks", [P, 1])
            bank = ps.bank("bank", (P, 2, 512))
            (loaded, zeroed, picked, hloaded, turned, kept, q_mm, q_ok, s_mm, s_ok, v_mm, v_ok) = (
                ps.sem(x) for x in ("loaded", "zeroed", "picked", "hloaded", "turned", "kept", "q_mm", "q_ok",
                                    "s_mm", "s_ok", "v_mm", "v_ok"))
            CH = TOK // 512
            with nc.Block() as block:
                @block.sync
                def _(sp):
                    for i, m in enumerate((Wq, Wk, Wv, Wo)):
                        sp.dma_start(raw[:, i, :], m).then_inc(loaded, 16)
                    sp.dma_start(bqs[:], bq.rearrange("(p a) -> p a", a=1)).then_inc(loaded, 16)
                    sp.dma_start(bks[:], bk.rearrange("(p a) -> p a", a=1)).then_inc(loaded, 16)
                    sp.dma_start(bvb[:], bv.partition_broadcast(P)).then_inc(loaded, 16)
                    sp.dma_start(bob[:], bo.partition_broadcast(P)).then_inc(loaded, 16)
                    sp.wait_ge(zeroed, 1)
                    for head in range(HEADS):
                        for c1 in range(2):
                            row, col = 64 * (head % 2) + 32 * c1, 16 * (head % 8) + 8 * c1
                            sp.dma_start(hel[row:row + 32, head // 2, :, col:col + HD],
                                         Whel[head].rearrange("(p c) d -> p c d", c=2)).then_inc(hloaded, 16)
                            sp.dma_start(bias[row:row + 32, head // 2, :],
                                         bhel[head].rearrange("(p c) -> p c", c=2)).then_inc(hloaded, 16)

                @block.gpsimd
                def _(pool):
                    nc.gpsimd.memset(hel[:], 0.0).then_inc(zeroed, 1)
                    nc.gpsimd.memset(pick[:], 0.0).then_inc(zeroed, 1)
                    pool.wait_ge(zeroed, 2)
                    for half in range(2):
                        for c1 in range(2):
                            view = pick[:, half, c1, :].rearrange("p (h c d) -> p h c d", c=2, d=HD)[:, :, c1, :]
                            nc.gpsimd.affine_select(out=view, in_=view, compare_op=ALU.not_equal, fill=1.0,
                                                    base=-64 * half, pattern=[[-HD, 8], [-1, HD]],
                                                    channel_multiplier=1).then_inc(picked, 1)

                blocks = [raw[:, i, :] for i in range(4)] + [hel[:, p, c, :] for p in range(PAIRS) for c in range(2)]

                @block.tensor
                def _(pe):
                    pe.wait_ge(loaded, 128)
                    def turn(g):
                        reached(pe, kept, g - 1)
                        for i in range(4):
                            ins = nc.tensor.transpose(bank[:, g % 2, i * P:(i + 1) * P], blocks[4 * g + i], sh.ident[:])
                        ins.then_inc(turned, 1)
                    turn(0)
                    pe.wait_ge(kept, 1)
                    for n in range(2 * CH):
                        reached(pe, q_ok, n - 1)
                        nc.tensor.matmul(bank[:, n % 2, :], wT[:, n // CH, :],
                                         sh.XNT[:, (n % CH) * 512:(n % CH + 1) * 512], start=True,
                                         stop=True).then_inc(q_mm, 1)
                    pe.wait_ge(q_ok, 2 * CH)
                    for c in range(CH):
                        reached(pe, v_ok, c - 1)
                        for i in range(4):
                            t = 4 * c + i
                            ins = nc.tensor.matmul(bank[:, c % 2, i * P:(i + 1) * P], sh.XNT[:, t * P:(t + 1) * P],
                                                   wT[:, 2, :], start=True, stop=True)
                        ins.then_inc(v_mm, 1)
                    pe.wait_ge(v_ok, CH)
                    pe.wait_ge(picked, 4)
                    n = 0
                    for side in range(2):
                        pairs = qk[:, side, :].rearrange("p (b s c) -> p b s c", b=BATCH, c=2)
                        for half in range(2):
                            for g in range(4):
                                reached(pe, s_ok, n - 1)
                                for c1 in range(2):
                                    ins = nc.tensor.matmul(bank[:, n % 2, :], pick[:, half, c1, :],
                                                           pairs[:, 4 * g:4 * g + 4, :, c1], start=c1 == 0, stop=c1 == 1)
                                ins.then_inc(s_mm, 1)
                                n += 1
                    pe.wait_ge(s_ok, n)
                    pe.wait_ge(hloaded, 16 * 4 * HEADS)
                    for g in range(1, 5):
                        turn(g)

                @block.scalar
                def _(act):
                    act.wait_ge(turned, 1)
                    nc.scalar.activation(wT[:].rearrange("p i c -> p (i c)"), bank[:, 0, :], ACT.Copy).then_inc(kept, 1)
                    act.wait_ge(kept, 1)
                    nc.scalar.activation(woT[:], wT[:, 3, :], ACT.Copy)
                    act.wait_ge(loaded, 128)
                    for n in range(2 * CH):
                        act.wait_ge(q_mm, n + 1)
                        nc.scalar.activation(qk[:, n // CH, (n % CH) * 512:(n % CH + 1) * 512], bank[:, n % 2, :],
                                             ACT.Identity, bias=(bqs, bks)[n // CH][:]).then_inc(q_ok, 1)
                    for n in range(16):
                        act.wait_ge(s_mm, n + 1)
                        side, half, g = n // 8, n // 4 % 2, n % 4
                        nc.scalar.activation(
                            stack[:, side, half * BATCH + 4 * g:half * BATCH + 4 * g + 4, :].rearrange("p b s -> p (b s)"),
                            bank[:, n % 2, :], ACT.Copy).then_inc(s_ok, 1)
                    for g in range(1, 5):
                        act.wait_ge(turned, g + 1)
                        nc.scalar.activation(helT[:, 2 * g - 2:2 * g, :, :].rearrange("p i c m -> p (i c m)"),
                                             bank[:, g % 2, :], ACT.Copy).then_inc(kept, 1)
                    nc.scalar.mul(qk[:, 0, :], qk[:, 0, :], DOT * SCALE)

                @block.vector
                def _(dve):
                    dve.wait_ge(loaded, 128)
                    for c in range(CH):
                        dve.wait_ge(v_mm, c + 1)
                        nc.vector.tensor_tensor(v[:, 4 * c:4 * c + 4, :],
                                                bank[:, c % 2, :].rearrange("p (t c) -> p t c", t=4),
                                                bvb[:].unsqueeze(1).broadcast_to([P, 4, P]), ALU.add).then_inc(v_ok, 1)

        with Phase(nc, "lm") as ps:
            wh = ps.sb("wh", [P, 2, P])
            comp = ps.sb("comp", [P, 2, 2, 2, 2, HALF])
            sq = ps.sb("sq", [P, 2, 2, 2, HALF])
            n2, norm, inv_n = (ps.sb(x, [P, 2, 2, 2, HALF]) for x in ("n2", "norm", "inv_n"))
            unit = ps.sb("unit", [P, 2, 2, 2, 2, 2, HALF])
            prob, probT = ps.sb("prob", [P, 2, 2, SEQ]), ps.sb("probT", [P, 2, 2, SEQ])
            low = ps.sb("low", [P, 2, 2])
            totals, inv = ps.sb("totals", [P, 2, 2, 2]), ps.sb("inv", [P, 2, 2])
            ps_hel, ps_score, ps_turn = (ps.bank(x, (P, 2, 512)) for x in ("ps_hel", "ps_score", "ps_turn"))
            ps_out = ps.bank("ps_out", (P, 2, 512))
            (wh_ok, hel_mm, comp_ok, sq_ok, n2_ok, cl_ok, norm_ok, inv_ok, unit_ok, bare, score_mm, low_ok,
             exp_ok, turned, probT_ok, out_mm, rec_ok, done) = (ps.sem(x) for x in (
                 "wh_ok", "hel_mm", "comp_ok", "sq_ok", "n2_ok", "cl_ok", "norm_ok", "inv_ok", "unit_ok", "bare",
                 "score_mm", "low_ok", "exp_ok", "turned", "probT_ok", "out_mm", "rec_ok", "done"))

            feat_ok = [[ps.sem(f"feat_ok{j}{i}") for i in range(2)] for j in range(2)]

            with nc.Block() as block:
                @block.sync
                def _(sp):
                    def features(p, m, j, i):
                        n = 2 * m + i
                        for h in range(2):
                            reached(sp, score_mm, 2 * n - 7 + h)
                            row = 64 * (1 - h)
                            sp.dma_start(unit[row:row + HD, j, i, h, :, :, :].rearrange("p a c s -> p a (c s)"),
                                         qk[(2 * p + h) * HD:(2 * p + h + 1) * HD, :, bass.ds((n % BATCH) * SEQ, SEQ)]
                                         ).then_inc(feat_ok[j][i], 16)

                    sp.wait_ge(bare, 2)
                    for p in range(PAIRS):
                        for b in turns(sp, BATCH // 4):
                            for j in range(2):
                                for i in range(2):
                                    features(p, p * (BATCH // 2) + 2 * b + j, j, i)

                @block.gpsimd
                def _(pool):
                    def squares(m, j, i):
                        n = 2 * m + i
                        pool.wait_ge(comp_ok, n + 1)
                        reached(pool, n2_ok, n - 1)
                        nc.gpsimd.tensor_tensor(sq[:, i], comp[:, j, i], comp[:, j, i], ALU.mult).then_inc(sq_ok, 1)
                        reached(pool, norm_ok, m - 1)
                        pool.wait_ge(sq_ok, n + 1)
                        nc.gpsimd.tensor_tensor(n2[:, j, i], sq[:, i, :, 0, :], sq[:, i, :, 1, :], ALU.add
                                                ).then_inc(n2_ok, 1)

                    for p in turns(pool, PAIRS):
                        reached(pool, hel_mm, BATCH * p)
                        nc.gpsimd.tensor_copy(wh[:], helT[:, bass.ds(p, 1), :, :].rearrange("p a c m -> p (a c) m")
                                              ).then_inc(wh_ok, 1)
                        for b in turns(pool, BATCH // 4):
                            for j in range(2):
                                for i in range(2):
                                    squares(p * (BATCH // 2) + 2 * b + j, j, i)

                @block.tensor
                def _(pe):
                    def helical(m, i):
                        n = 2 * m + i
                        pe.wait_ge(wh_ok, n // BATCH + 1)
                        reached(pe, comp_ok, n - 1)
                        at = (n // (4 * BATCH)) * BATCH + n % BATCH
                        for c in range(2):
                            for side in range(2):
                                col = (2 * side + c) * HALF
                                ins = nc.tensor.matmul(
                                    ps_hel[:, i, col:col + HALF], wh[:, c, :],
                                    stack[:, side, bass.ds(at, 1), :].rearrange("p a s -> p (a s)"), start=True, stop=True)
                        ins.then_inc(hel_mm, 1)

                    def score(m, j, i, h):
                        n = 2 * m + i
                        pe.wait_ge(unit_ok, n + 1)
                        pe.wait_ge(feat_ok[j][i], 32 * (m // 2 + 1))
                        reached(pe, exp_ok, 2 * (2 * n + h - 1))
                        for c in range(2):
                            ins = nc.tensor.matmul(ps_score[:, h, c * SEQ:(c + 1) * SEQ], unit[:, j, i, h, 0, c, :],
                                                   unit[:, j, i, h, 1, :, :], start=True, stop=True)
                        ins.then_inc(score_mm, 1)

                    def turn(m, i, h):
                        g = 2 * (2 * m + i) + h
                        pe.wait_ge(exp_ok, 2 * g + 2)
                        reached(pe, probT_ok, g - 1)
                        for t in range(2):
                            for s in range(2):
                                ins = nc.tensor.transpose(ps_turn[:, h, t * SEQ + s * P:t * SEQ + (s + 1) * P],
                                                          prob[:, h, s, t * P:(t + 1) * P], sh.ident[:])
                        ins.then_inc(turned, 1)

                    def attend(m, i, h):
                        n = 2 * m + i
                        g = 2 * n + h
                        pe.wait_ge(probT_ok, g + 1)
                        reached(pe, done, n - 1)
                        for s in range(2):
                            for t in range(2):
                                ins = nc.tensor.matmul(
                                    ps_out[:, i, (2 * h + s) * HD:(2 * h + s + 1) * HD],
                                    probT[:, h, t, s * P:(s + 1) * P],
                                    v[:, bass.ds((n % BATCH) * 2 + t, 1), bass.ds((n // BATCH) * 2 * HD + h * HD, HD)]
                                    .rearrange("p a d -> p (a d)"), start=t == 0, stop=t == 1)
                        ins.then_inc(out_mm, 1)

                    def body(m, j):
                        q, a, o = m, m - 2, m - 3
                        lq, la, lo = live(q, TURNS), live(a, TURNS), live(o, TURNS)
                        if la:
                            score(a, j, 0, 0)
                        if lo:
                            turn(o, 1, 1)
                        if lq:
                            helical(q, 0)
                        if lo:
                            attend(o, 1, 0)
                        if la:
                            score(a, j, 0, 1)
                        if lo:
                            attend(o, 1, 1)
                        if lq:
                            helical(q, 1)
                        if la:
                            turn(a, 0, 0)
                            score(a, j, 1, 0)
                            attend(a, 0, 0)
                            turn(a, 0, 1)
                            score(a, j, 1, 1)
                            attend(a, 0, 1)
                            turn(a, 1, 0)
                    skewed(pe, TURNS, 3, body)

                @block.scalar
                def _(act):
                    def root(m, j):
                        act.wait_ge(cl_ok, m + 1)
                        reached(act, inv_ok, 2 * m - 2)
                        nc.scalar.activation(norm[:, j].rearrange("p i a s -> p (i a s)"),
                                             n2[:, j].rearrange("p i a s -> p (i a s)"), ACT.Sqrt, scale=1 / SCALE
                                             ).then_inc(norm_ok, 1)

                    def exps(m, i, h):
                        n = 2 * m + i
                        g = 2 * n + h
                        act.wait_ge(low_ok, g + 1)
                        reached(act, turned, g - 1)
                        reached(act, rec_ok, n - 1)
                        for s in range(2):
                            nc.scalar.activation(prob[:, h, s, :], ps_score[:, h, s * SEQ:(s + 1) * SEQ], ACT.Exp,
                                                 bias=low[:, h, s:s + 1],
                                                 accum_out=totals[:, i, h, s:s + 1]).then_inc(exp_ok, 1)

                    def keep_turned(m, i, h):
                        g = 2 * (2 * m + i) + h
                        act.wait_ge(turned, g + 1)
                        reached(act, out_mm, g - 1)
                        nc.scalar.activation(probT[:, h].rearrange("p t s -> p (t s)"), ps_turn[:, h, :],
                                             ACT.Copy).then_inc(probT_ok, 1)

                    def body(m, j):
                        r, a, o = m - 1, m - 2, m - 3
                        lr, la, lo = live(r, TURNS), live(a, TURNS), live(o, TURNS)
                        if lo:
                            keep_turned(o, 1, 1)
                        if lr:
                            root(r, 1 - j)
                        if la:
                            exps(a, 0, 0)
                            exps(a, 0, 1)
                            keep_turned(a, 0, 0)
                            exps(a, 1, 0)
                            keep_turned(a, 0, 1)
                            exps(a, 1, 1)
                            keep_turned(a, 1, 0)
                    skewed(act, TURNS, 3, body)

                @block.vector
                def _(dve):
                    wide = [P, 2, 2, HALF]
                    for h in range(2):
                        row = 64 * (1 - h)
                        nc.vector.memset(unit[row:row + 64, :, :, h], 0.0).then_inc(bare, 1)

                    def components(m, j, i):
                        n = 2 * m + i
                        dve.wait_ge(hel_mm, n + 1)
                        reached(dve, unit_ok, n - 3)
                        nc.vector.tensor_tensor(
                            comp[:, j, i], ps_hel[:, i, :].rearrange("p (a c s) -> p a c s", a=2, c=2),
                            bias[:, bass.ds(n // BATCH, 1), :].unsqueeze(3).broadcast_to([P, 1, 2, HALF])
                            .broadcast_to(wide), ALU.add).then_inc(comp_ok, 1)

                    def clamp(m, j):
                        dve.wait_ge(n2_ok, 2 * m + 2)
                        f = n2[:, j].rearrange("p i a s -> p (i a s)")
                        nc.vector.tensor_scalar(f, f, 1e-24, None, ALU.max).then_inc(cl_ok, 1)

                    def inverses(m, j, i):
                        n = 2 * m + i
                        dve.wait_ge(norm_ok, m + 1)
                        reached(dve, unit_ok, n - 3)
                        nc.vector.reciprocal(inv_n[:, j, i], norm[:, j, i]).then_inc(inv_ok, 1)

                    def units(m, j, i):
                        n = 2 * m + i
                        dve.wait_ge(inv_ok, n + 1)
                        reached(dve, score_mm, 2 * n - 6)
                        for h in range(2):
                            rows = slice(64 * h, 64 * h + 64)
                            ins = nc.vector.tensor_tensor(unit[rows, j, i, h], comp[rows, j, i],
                                                          inv_n[rows, j, i].unsqueeze(2).broadcast_to([64, 2, 2, HALF]),
                                                          ALU.mult)
                        ins.then_inc(unit_ok, 1)

                    def maximum(m, i, h):
                        g = 2 * (2 * m + i) + h
                        dve.wait_ge(score_mm, g + 1)
                        reached(dve, exp_ok, 2 * (g - 1))
                        nc.vector.tensor_reduce(low[:, h, :], ps_score[:, h, :].rearrange("p (s t) -> p s t", s=2), AX.X,
                                                ALU.max, negate=True).then_inc(low_ok, 1)

                    def weigh(m, i):
                        n = 2 * m + i
                        dve.wait_ge(exp_ok, 4 * n + 4)
                        reached(dve, done, n)
                        nc.vector.reciprocal(inv[:], totals[:, i]).then_inc(rec_ok, 1)

                    def collect(m, i):
                        n = 2 * m + i
                        dve.wait_ge(rec_ok, n + 1)
                        dve.wait_ge(out_mm, 2 * n + 2)
                        nc.vector.tensor_tensor(
                            heads[:, bass.ds((n % BATCH) * 2, 2), bass.ds((n // BATCH) * 2 * HD, 2 * HD)]
                            .rearrange("p s (h d) -> p h s d", h=2),
                            ps_out[:, i, 0:4 * HD].rearrange("p (h s d) -> p h s d", h=2, s=2),
                            inv[:].unsqueeze(3).broadcast_to([P, 2, 2, HD]), ALU.mult).then_inc(done, 1)

                    def body(m, j):
                        q, r, a, o = m, m - 1, m - 2, m - 3
                        lq, lr, la, lo = (live(x, TURNS) for x in (q, r, a, o))
                        if la:
                            maximum(a, 0, 0)
                        if lo:
                            weigh(o, 1)
                        if lq:
                            components(q, j, 0)
                        if la:
                            maximum(a, 0, 1)
                        if lo:
                            collect(o, 1)
                        if lq:
                            components(q, j, 1)
                        if lr:
                            inverses(r, 1 - j, 0)
                        if la:
                            maximum(a, 1, 0)
                            weigh(a, 0)
                        if lr:
                            units(r, 1 - j, 0)
                        if lq:
                            clamp(q, j)
                        if la:
                            maximum(a, 1, 1)
                        if lr:
                            inverses(r, 1 - j, 1)
                        if la:
                            collect(a, 0)
                        if lr:
                            units(r, 1 - j, 1)
                    skewed(dve, TURNS, 3, body)

        token_projection(nc, sh, "lo", heads, woT, bob)


def token_projection(nc, sh, name, src, w, bias):
    CH = TOK // 512
    with Phase(nc, name) as ps:
        bank, ps_y = ps.bank("bank", (P, 2, 512)), ps.bank("ps_y", (P, 2, 512))
        srcT = ps.sb("srcT", [P, 2, 512])
        turned, kept, y_mm, biased, added = (ps.sem(x) for x in ("turned", "kept", "y_mm", "biased", "added"))
        with nc.Block() as block:
            @block.tensor
            def _(pe):
                for c in range(CH):
                    reached(pe, kept, c - 1)
                    for i in range(4):
                        ins = nc.tensor.transpose(bank[:, c % 2, i * P:(i + 1) * P], src[:, 4 * c + i, :], sh.ident[:])
                    ins.then_inc(turned, 1)
                    pe.wait_ge(kept, c + 1)
                    reached(pe, added, c - 1)
                    for i in range(4):
                        ins = nc.tensor.matmul(ps_y[:, c % 2, i * P:(i + 1) * P], srcT[:, c % 2, i * P:(i + 1) * P], w[:],
                                               start=True, stop=True)
                    ins.then_inc(y_mm, 1)

            @block.scalar
            def _(act):
                for c in range(CH):
                    act.wait_ge(turned, c + 1)
                    reached(act, y_mm, c - 1)
                    nc.scalar.activation(srcT[:, c % 2, :], bank[:, c % 2, :], ACT.Copy).then_inc(kept, 1)

            @block.gpsimd
            def _(pool):
                for c in range(CH):
                    x = sh.X[:, 4 * c:4 * c + 4, :]
                    nc.gpsimd.tensor_tensor(x, x, bias[:].unsqueeze(1).broadcast_to([P, 4, P]), ALU.add).then_inc(biased, 1)

            @block.vector
            def _(dve):
                for c in range(CH):
                    dve.wait_ge(y_mm, c + 1)
                    dve.wait_ge(biased, c + 1)
                    x = sh.X[:, 4 * c:4 * c + 4, :]
                    nc.vector.tensor_tensor(x, x, ps_y[:, c % 2, :].rearrange("p (t c) -> p t c", t=4),
                                            ALU.add).then_inc(added, 1)


def delta_attention(nc, sh, Wv, Wo, Wg, Wb):
    HD = P // HEADS
    SLOT = 32
    HALF = BATCH // 2
    SLOTS = SEQ // SLOT
    CH = TOK // 512
    with Phase(nc, "da") as ph:
        vT, betaT, gateT = (ph.sb(x, [P, TOK]) for x in ("vT", "betaT", "gateT"))
        out = ph.sb("out", [P, BATCH, SEQ + 1])
        rT = ph.sb("rT", [P, TOK])
        woT = ph.sb("woT", [P, P])
        spread = ph.sb("spread", [P, HD, P])

        with Phase(nc, "ds") as ps:
            raw = ps.sb("raw", [P, 2, P])
            small = ps.sb("small", [P, 2, HEADS])
            wT = ps.sb("wT", [P, 3, P])
            n2 = ps.sb("n2", [P, TILES, HEADS])
            norm, inv = ps.sb("norm", [P, TILES, HEADS]), ps.sb("inv", [P, TILES, HEADS])
            th = ps.sb("th", [P, 2, 512])
            bank = ps.bank("bank", (P, 2, 512))
            (loaded, turned, kept, chain, sqrt_in, sqrt_ok, unit_ok, zeroed, spread_ok, p_mm, p_ok, th_ok, half_ok, r_mm,
             r_ok) = (ps.sem(x) for x in (
                 "loaded", "turned", "kept", "chain", "sqrt_in", "sqrt_ok", "unit_ok", "zeroed", "spread_ok", "p_mm",
                 "p_ok", "th_ok", "half_ok", "r_mm", "r_ok"))
            sq = rT[:].rearrange("p (t c) -> p t c", t=TILES)
            with nc.Block() as block:
                @block.sync
                def _(sp):
                    for i, m in enumerate((Wv, Wo)):
                        sp.dma_start(raw[:, i, :], m).then_inc(loaded, 16)
                    with nc.allow_non_contiguous_dma("two gates of two thousand weights"):
                        for i, m in enumerate((Wb, Wg)):
                            sp.dma_start(small[:, i, :], m.rearrange("h c -> c h")).then_inc(loaded, 16)

                @block.gpsimd
                def _(pool):
                    nc.gpsimd.memset(spread[:], 0.0).then_inc(zeroed, 1)
                    pool.wait_ge(zeroed, 1)
                    for k in range(HD):
                        nc.gpsimd.tensor_copy(
                            spread[:, k, :].rearrange("p (h d) -> p h d", d=HD),
                            sh.ident[:].rearrange("p (h d) -> p h d", d=HD)[:, :, k:k + 1].broadcast_to([P, HEADS, HD])
                        ).then_inc(spread_ok, 1)

                @block.tensor
                def _(pe):
                    pe.wait_ge(loaded, 64)
                    for i in range(2):
                        ins = nc.tensor.transpose(bank[:, 0, i * P:(i + 1) * P], raw[:, i, :], sh.ident[:])
                    ins.then_inc(turned, 1)
                    pe.wait_ge(kept, 4)
                    for n in range(3 * CH):
                        if 2 <= n <= CH + 1:
                            pe.wait_ge(p_ok, n - 1)
                        elif n > CH + 1:
                            pe.wait_ge(th_ok, n - 1 - CH)
                            pe.wait_ge(p_ok, CH)
                        nc.tensor.matmul(bank[:, n % 2, :], wT[:, n // CH, :], sh.XNT[:, (n % CH) * 512:(n % CH + 1) * 512],
                                         start=True, stop=True).then_inc(p_mm, 1)
                    pe.wait_ge(th_ok, 2 * CH)
                    pe.wait_ge(unit_ok, 1)
                    for c in range(CH):
                        reached(pe, r_ok, c - 1)
                        for i in range(4):
                            ins = nc.tensor.transpose(bank[:, c % 2, i * P:(i + 1) * P], sh.XN[:, 4 * c + i, :], sh.ident[:])
                        ins.then_inc(r_mm, 1)

                @block.scalar
                def _(act):
                    act.wait_ge(turned, 1)
                    nc.scalar.activation(wT[:, 0, :], bank[:, 0, 0:P], ACT.Copy).then_inc(kept, 1)
                    nc.scalar.activation(woT[:], bank[:, 0, P:2 * P], ACT.Copy).then_inc(kept, 1)
                    act.wait_ge(loaded, 64)
                    for i in range(2):
                        nc.scalar.activation(wT[:, 1 + i, :].rearrange("p (h d) -> p h d", d=HD),
                                             small[:, i, :].unsqueeze(2).broadcast_to([P, HEADS, HD]),
                                             ACT.Copy).then_inc(kept, 1)
                    for n in range(3 * CH):
                        act.wait_ge(p_mm, n + 1)
                        at = slice((n % CH) * 512, (n % CH + 1) * 512)
                        if n < CH:
                            nc.scalar.activation(vT[:, at], bank[:, n % 2, :], ACT.Copy).then_inc(p_ok, 1)
                        else:
                            reached(act, half_ok, n - CH - 1)
                            nc.scalar.activation(th[:, n % 2, :], bank[:, n % 2, :], ACT.Tanh, scale=0.5).then_inc(th_ok, 1)
                    act.wait_ge(sqrt_in, 1)
                    nc.scalar.activation(norm[:].rearrange("p t h -> p (t h)"), n2[:].rearrange("p t h -> p (t h)"),
                                         ACT.Sqrt).then_inc(sqrt_ok, 1)
                    for c in range(CH):
                        act.wait_ge(r_mm, c + 1)
                        nc.scalar.activation(rT[:, c * 512:(c + 1) * 512], bank[:, c % 2, :], ACT.Copy).then_inc(r_ok, 1)

                @block.vector
                def _(dve):
                    wide = [P, TILES, HEADS, HD]
                    heads = sh.XN[:].rearrange("p t (h d) -> p t h d", d=HD)
                    nc.vector.tensor_tensor(sq, sh.XN[:], sh.XN[:], ALU.mult).then_inc(chain, 1)
                    dve.wait_ge(chain, 1)
                    nc.vector.tensor_reduce(n2[:], sq.rearrange("p t (h d) -> p t h d", d=HD), AX.X,
                                            ALU.add).then_inc(chain, 1)
                    dve.wait_ge(chain, 2)
                    nc.vector.tensor_scalar(n2[:], n2[:], 1e-24, None, ALU.max).then_inc(sqrt_in, 1)
                    for n in range(2 * CH):
                        dve.wait_ge(th_ok, n + 1)
                        dst = (betaT, gateT)[n // CH]
                        nc.vector.tensor_scalar(dst[:, (n % CH) * 512:(n % CH + 1) * 512], th[:, n % 2, :], 0.5, 0.5,
                                                ALU.mult, ALU.add).then_inc(half_ok, 1)
                    dve.wait_ge(sqrt_ok, 1)
                    nc.vector.reciprocal(inv[:], norm[:]).then_inc(chain, 1)
                    dve.wait_ge(chain, 3)
                    nc.vector.tensor_tensor(heads, heads, inv[:].unsqueeze(3).broadcast_to(wide), ALU.mult).then_inc(unit_ok, 1)
                    dve.wait_ge(p_ok, CH)
                    dve.wait_ge(half_ok, CH)
                    nc.vector.tensor_tensor(vT[:], vT[:], betaT[:], ALU.mult).then_inc(chain, 1)

        with Phase(nc, "dr") as ps:
            R = ps.sb("R", [P, 2, HD, BATCH, SLOT])
            S = ps.sb("S", [P, HD, BATCH])
            step, prod = ps.sb("step", [P, HD, BATCH]), ps.sb("prod", [P, HD, BATCH])
            want, err = ps.sb("want", [P, BATCH]), ps.sb("err", [P, BATCH])
            bank = ps.bank("bank", (P, 2, 512))
            r_mm, r_ok, want_ok, err_ok, step_ok, s_ok, prod_ok, o_ok = (ps.sem(x) for x in (
                "r_mm", "r_ok", "want_ok", "err_ok", "step_ok", "s_ok", "prod_ok", "o_ok"))
            r, beta, v = (t[:].rearrange("p (b t) -> p b t", b=BATCH) for t in (rT, betaT, vT))

            with nc.Block() as block:
                @block.tensor
                def _(pe):
                    for c in turns(pe, SLOTS):
                        for k in range(HD):
                            reached(pe, r_ok, HD * c + max(k - 1, 0))
                            nc.tensor.matmul(bank[:, k % 2, :], spread[:, k, :], r[:, :, bass.ds(c * SLOT, SLOT)],
                                             start=True, stop=True).then_inc(r_mm, 1)

                @block.scalar
                def _(act):
                    def slot(c, half):
                        reached(act, step_ok, 2 * (SLOT * (c - 1) + 1))
                        for k in range(HD):
                            act.wait_ge(r_mm, HD * c + k + 1)
                            nc.scalar.activation(R[:, half, k, :, :].rearrange("p b t -> p (b t)"), bank[:, k % 2, :],
                                                 ACT.Copy).then_inc(r_ok, 1)
                    slot(0, 0)
                    slot(1, 1)
                    with act.Fori(1, SLOTS // 2) as m:
                        slot(2 * m, 0)
                        slot(2 * m + 1, 1)

                @block.vector
                def _(dve):
                    def at(a, i):
                        return a[:, :, bass.ds(i, 1)].rearrange("p b t -> p (b t)")

                    def key(half, j):
                        return R[:, half, :, :, bass.ds(j, 1)].rearrange("p k b t -> p k (b t)")

                    def steps(first, j, w, r_):
                        t = first + j
                        for stage in range(6):
                            for i, part in enumerate((slice(0, HALF), slice(HALF, BATCH))):
                                wide = [P, HD, HALF]
                                b, v_, o, o1 = (at(x, y)[:, part] for x, y in ((beta, t), (v, t), (out, t), (out, t + 1)))
                                wait, err_, step_, s_, prod_ = (x[:, part] if len(x.shape) == 2 else x[:, :, part]
                                                                for x in (want, err, step, S, prod))
                                count = 2 * t + i + 1
                                if stage == 0:
                                    dve.wait_ge(o_ok, count)
                                    nc.vector.tensor_tensor(wait, b, o, ALU.mult).then_inc(want_ok, 1)
                                elif stage == 1:
                                    dve.wait_ge(want_ok, count)
                                    nc.vector.tensor_tensor(err_, v_, wait, ALU.subtract).then_inc(err_ok, 1)
                                elif stage == 2:
                                    dve.wait_ge(err_ok, count)
                                    nc.vector.tensor_tensor(step_, w[:, :, part], err_.unsqueeze(1).broadcast_to(wide),
                                                            ALU.mult).then_inc(step_ok, 1)
                                elif stage == 3:
                                    dve.wait_ge(step_ok, count)
                                    nc.vector.tensor_tensor(s_, s_, step_, ALU.add).then_inc(s_ok, 1)
                                elif stage == 4:
                                    dve.wait_ge(s_ok, count + 2)
                                    nc.vector.tensor_tensor(prod_, r_[:, :, part], s_, ALU.mult).then_inc(prod_ok, 1)
                                else:
                                    dve.wait_ge(prod_ok, count)
                                    nc.vector.tensor_reduce(o1, prod_.rearrange("p k b -> p b k"), AX.X,
                                                            ALU.add).then_inc(o_ok, 1)

                    nc.vector.memset(S[:], 0.0).then_inc(s_ok, 1)
                    nc.vector.memset(R[:, 1, :, :, SLOT - 1:SLOT], 0.0).then_inc(s_ok, 1)
                    nc.vector.memset(out[:, 0:HALF, 0:1], 0.0).then_inc(o_ok, 1)
                    nc.vector.memset(out[:, HALF:BATCH, 0:1], 0.0).then_inc(o_ok, 1)
                    dve.wait_ge(s_ok, 2)
                    with dve.Fori(0, SLOTS // 2) as m:
                        for half in range(2):
                            c = 2 * m + half
                            dve.wait_ge(r_ok, HD * (c + 1))
                            for j in range(SLOT):
                                steps(c * SLOT, j, key(half, j - 1) if j else key(1 - half, SLOT - 1), key(half, j))

        with Phase(nc, "do") as ps:
            bank = ps.bank("bank", (P, 2, 512))
            gated, y_mm, added = ps.sem("gated"), ps.sem("y_mm"), ps.sem("added")
            with nc.Block() as block:
                @block.gpsimd
                def _(pool):
                    g = gateT[:].rearrange("p (b t) -> p b t", b=BATCH)
                    for c in range(CH):
                        o = out[:, 2 * c:2 * c + 2, 1:SEQ + 1]
                        nc.gpsimd.tensor_tensor(g[:, 2 * c:2 * c + 2, :], g[:, 2 * c:2 * c + 2, :], o,
                                                ALU.mult).then_inc(gated, 1)

                @block.tensor
                def _(pe):
                    for c in range(CH):
                        pe.wait_ge(gated, c + 1)
                        reached(pe, added, c - 1)
                        for i in range(4):
                            t = 4 * c + i
                            ins = nc.tensor.matmul(bank[:, c % 2, i * P:(i + 1) * P], gateT[:, t * P:(t + 1) * P], woT[:],
                                                   start=True, stop=True)
                        ins.then_inc(y_mm, 1)

                @block.vector
                def _(dve):
                    for c in range(CH):
                        dve.wait_ge(y_mm, c + 1)
                        x = sh.X[:, 4 * c:4 * c + 4, :]
                        nc.vector.tensor_tensor(x, x, bank[:, c % 2, :].rearrange("p (t c) -> p t c", t=4),
                                                ALU.add).then_inc(added, 1)


def store(nc, sh, out):
    with Phase(nc, "st") as ph:
        stored = ph.sem("stored")
        with nc.Block() as block:
            @block.sync
            def _(sp):
                sp.dma_start(out.rearrange("b (h p) c -> p (b h) c", p=P), sh.X[:]).then_inc(stored, 16)
                sp.wait_ge(stored, 16)


def hybrid_kernel(nc, a, out):
    def args(prefix, names):
        return [a[f"{prefix}_{n}"] for n in names.split()]

    with ExitStack() as ctx:
        sh = Shared(nc, ctx)
        load_and_constants(nc, sh, a["L0_attn_a_x"])
        layernorm(nc, sh, "n1")
        lookahead_attention(nc, sh, *args("L0_attn_a", "W_qkv W_out"))
        layernorm(nc, sh, "n2", sh.XN)
        top2_mixture(nc, sh, "fa", *args("L0_ffn", "Wg bg W1 b1 W2 b2 gamma beta"))
        layernorm(nc, sh, "n3")
        latent_attention(nc, sh, *args("L0_attn_b", "w_kv_down w_kv_up w_q w_out"))
        layernorm(nc, sh, "n4", sh.XN)
        top2_mixture(nc, sh, "fb", *args("L0_ffn", "Wg bg W1 b1 W2 b2 gamma beta"))
        layernorm(nc, sh, "n5")
        helical_attention(nc, sh, *args("L1_attn_a", "Wq bq Wk bk Wv bv Wo bo Whel bhel"))
        with ExitStack() as experts:
            ew = ExpertWeights(nc, experts)
            load_experts(nc, sh, ew, *args("L1_ffn", "shared_gate shared_up shared_down r_gate r_up r_down"))
            layernorm(nc, sh, "n6", sh.XN)
            routed_mixture(nc, sh, ew, "fc", a["L1_ffn_gate_w"])
            layernorm(nc, sh, "n7", sh.XN)
            delta_attention(nc, sh, *args("L1_attn_b", "Wv Wo Wg Wb"))
            layernorm(nc, sh, "n8", sh.XN)
            routed_mixture(nc, sh, ew, "fd", a["L1_ffn_gate_w"])
        store(nc, sh, out)


def kernel(**inputs):
    import numpy as _np
    import concourse.bacc as _bacc
    from concourse import mybir as _mybir
    from concourse.bass_utils import run_bass_kernel_spmd as _run

    nc = _bacc.Bacc("TRN2", target_bir_lowering=False, num_devices=1)
    arrays, args = {}, {}
    for name, value in inputs.items():
        array = _np.ascontiguousarray(value)
        arrays[f"in_{name}"] = array
        args[name] = nc.dram_tensor(f"in_{name}", array.shape, _mybir.dt.from_np(array.dtype), kind="ExternalInput").ap()
    out = nc.dram_tensor("out", (BATCH, SEQ, P), F32, kind="ExternalOutput").ap()
    hybrid_kernel(nc, args, out)
    return _run(nc, [arrays], core_ids=[0]).results[0]["out"]
```

```python
from contextlib import ExitStack

import concourse.bass as bass
from concourse import mybir

F32 = mybir.dt.float32
BF16 = mybir.dt.bfloat16
I32 = mybir.dt.int32
ACT = mybir.ActivationFunctionType
ALU = mybir.AluOpType
AX = mybir.AxisListType

P = 128
BATCH = 16
SEQ = 256
TOK = BATCH * SEQ
TILES = TOK // P
HEADS = 16
PAIRS = HEADS // 2
STEPS = PAIRS * BATCH
TRI = 3 * P
NEG = -3.0e38


def reached(eng, sem, count):
    if not isinstance(count, int) or count > 0:
        eng.wait_ge(sem, count)


def skewed(eng, steps, lag, body, unroll=2):
    head = -(-lag // unroll) * unroll
    for n in range(head):
        body(n, n % unroll)
    with eng.Fori(head // unroll, steps // unroll) as m:
        for k in range(unroll):
            body(unroll * m + k, k)
    for n in range(steps, steps + lag):
        body(n, n % unroll)


def live(n, steps):
    return not isinstance(n, int) or 0 <= n < steps


def turns(eng, count):
    yield 0
    with eng.Fori(1, count) as i:
        yield i


class Phase:

    def __init__(self, nc, name):
        self.nc, self.name, self.ctx, self.sems = nc, name, ExitStack(), []

    def sb(self, name, shape, dt=F32):
        return self.ctx.enter_context(self.nc.sbuf_tensor(f"{self.name}_{name}", shape, dt))

    def bank(self, name, shape=(P, 512), dt=F32):
        return self.ctx.enter_context(self.nc.psum_tensor(f"{self.name}_{name}", list(shape), dt))

    def sem(self, name):
        s = self.nc.alloc_semaphore(f"{self.name}_{name}")
        self.sems.append(s)
        return s

    def __enter__(self):
        return self

    def __exit__(self, *error):
        if error[0] is None:
            self.nc.clear_and_free_semaphores(self.sems)
            self.nc.all_engine_barrier()
        self.ctx.close()


class Shared:

    def __init__(self, nc, ctx):
        def sb(name, shape, dt=F32):
            return ctx.enter_context(nc.sbuf_tensor(name, shape, dt))

        self.X = sb("X", [P, TILES, P])
        self.XN = sb("XN", [P, TILES, P])
        self.XNT = sb("XNT", [P, TOK])
        self.ident = sb("ident", [P, P])
        self.ident16 = sb("ident16", [P, P], BF16)
        self.future16 = sb("future16", [P, P], BF16)


def load_and_constants(nc, sh, x):
    with Phase(nc, "ld") as ph:
        loaded, zeroed, made = ph.sem("loaded"), ph.sem("zeroed"), ph.sem("made")
        with nc.Block() as block:
            @block.sync
            def _(sp):
                sp.dma_start(sh.X[:], x.rearrange("b (h p) c -> p (b h) c", p=P)).then_inc(loaded, 16)
                sp.wait_ge(loaded, 16)

            @block.gpsimd
            def _(pool):
                nc.gpsimd.memset(sh.ident[:], 0.0).then_inc(zeroed, 1)
                nc.gpsimd.memset(sh.ident16[:], 0.0).then_inc(zeroed, 1)
                nc.gpsimd.memset(sh.future16[:], 0.0).then_inc(zeroed, 1)
                pool.wait_ge(zeroed, 3)
                for t in (sh.ident, sh.ident16):
                    nc.gpsimd.affine_select(out=t[:], in_=t[:], compare_op=ALU.not_equal, fill=1.0, base=0,
                                            pattern=[[-1, P]], channel_multiplier=1).then_inc(made, 1)
                nc.gpsimd.affine_select(out=sh.future16[:], in_=sh.future16[:], compare_op=ALU.is_ge, fill=NEG,
                                        base=0, pattern=[[-1, P]], channel_multiplier=1).then_inc(made, 1)
                pool.wait_ge(made, 3)


def row_statistics(nc, dve, st, mean, rstd, work, chain, sqrt_in, sqrt_done):
    even, odd = (st[:, :, 1], st[:, :, 2]), (st[:, :, 4], st[:, :, 5])
    a, b, c = work[:, 0, :], work[:, 1, :], work[:, 2, :]
    nc.vector.tensor_tensor(a, even[0], odd[0], ALU.add).then_inc(chain, 1)
    nc.vector.tensor_tensor(b, even[0], odd[0], ALU.subtract).then_inc(chain, 1)
    nc.vector.tensor_tensor(c, even[1], odd[1], ALU.add).then_inc(chain, 1)
    dve.wait_ge(chain, 3)
    nc.vector.tensor_scalar(mean[:], a, 0.5, None, ALU.mult).then_inc(chain, 1)
    nc.vector.scalar_tensor_tensor(out=work[:, 3, :], in0=b, scalar=0.25, in1=b, op0=ALU.mult,
                                   op1=ALU.mult).then_inc(chain, 1)
    dve.wait_ge(chain, 5)
    nc.vector.scalar_tensor_tensor(out=work[:, 4, :], in0=c, scalar=1.0 / P, in1=work[:, 3, :], op0=ALU.mult,
                                   op1=ALU.add).then_inc(chain, 1)
    dve.wait_ge(chain, 6)
    nc.vector.tensor_scalar(work[:, 5, :], work[:, 4, :], 1e-5, None, ALU.add).then_inc(sqrt_in, 1)
    dve.wait_ge(sqrt_done, 1)
    nc.vector.reciprocal(rstd[:], work[:, 6, :]).then_inc(chain, 1)
    dve.wait_ge(chain, 7)


def tile_statistics(nc, dve, st, src, stats):
    with dve.Fori(0, TILES // 8) as m:
        for i in range(8):
            t = 8 * m + i
            nc.vector.bn_stats(st[:, bass.ds(t, 1), :].rearrange("p a s -> p (a s)"),
                               src[:, bass.ds(t, 1), :].rearrange("p a c -> p (a c)")).then_inc(stats, 1)
    dve.wait_ge(stats, TILES)


def layernorm(nc, sh, name):
    G = TILES // 4
    with Phase(nc, name) as ph:
        st, mean, rstd, work = ph.sb("st", [P, TILES, 6]), ph.sb("mean", [P, TILES]), ph.sb("rstd", [P, TILES]), \
            ph.sb("work", [P, 7, TILES])
        turned = ph.bank("turned", (P, 4, 512))
        stats, chain, sqrt_in, sqrt_done = ph.sem("stats"), ph.sem("chain"), ph.sem("sqrt_in"), ph.sem("sqrt_done")
        normed, turn, evac = ph.sem("normed"), ph.sem("turn"), ph.sem("evac")
        with nc.Block() as block:
            @block.vector
            def _(dve):
                tile_statistics(nc, dve, st, sh.X, stats)
                row_statistics(nc, dve, st, mean, rstd, work, chain, sqrt_in, sqrt_done)
                for g in range(G):
                    for t in range(4 * g, 4 * g + 4):
                        ins = nc.vector.tensor_scalar(sh.XN[:, t, :], sh.X[:, t, :], mean[:, t:t + 1], rstd[:, t:t + 1],
                                                      ALU.subtract, ALU.mult)
                    ins.then_inc(normed, 1)

            @block.scalar
            def _(act):
                act.wait_ge(sqrt_in, 1)
                nc.scalar.activation(work[:, 6, :], work[:, 5, :], ACT.Sqrt).then_inc(sqrt_done, 1)
                for g in range(G):
                    act.wait_ge(turn, g + 1)
                    nc.scalar.activation(sh.XNT[:, g * 512:(g + 1) * 512], turned[:, g % 4, :], ACT.Copy).then_inc(evac, 1)

            @block.tensor
            def _(pe):
                for g in range(G):
                    pe.wait_ge(normed, g + 1)
                    reached(pe, evac, g - 3)
                    for i in range(4):
                        ins = nc.tensor.transpose(turned[:, g % 4, i * P:(i + 1) * P], sh.XN[:, 4 * g + i, :], sh.ident[:])
                    ins.then_inc(turn, 1)


def lookahead_attention(nc, sh, W_qkv, W_out):
    D = 64
    SCALE = D ** -0.5
    with Phase(nc, "aa") as ph:
        w = ph.sb("w", [P, 6, P])
        wo = ph.sb("wo", [P, P])
        xs = ph.sb("xs", [P, 2, SEQ])
        qkv = ph.sb("qkv", [P, 2, 3, 2, SEQ])
        causal = ph.sb("causal", [P, TRI])
        ahead = ph.sb("ahead", [P, TRI])
        th_look, th_su = ph.sb("th_look", [P, 2, TRI]), ph.sb("th_su", [P, 2, TRI])
        look, term = ph.sb("look", [P, 2, TRI]), ph.sb("term", [P, 2, TRI])
        gated, minus = ph.sb("gated", [P, 2, TRI]), ph.sb("minus", [P, 2, TRI])
        prob, probT = ph.sb("prob", [P, 2, TRI]), ph.sb("probT", [P, 2, TRI])
        low, total, inv = ph.sb("low", [P, 2, 2]), ph.sb("total", [P, 2, 2]), ph.sb("inv", [P, 2, 2])
        headsT = ph.sb("headsT", [P, SEQ])
        carrier = ph.sb("carrier", [P, 1])
        proj = ph.bank("proj", (P, 2, 512))
        ps_look, ps_term, ps_score, ps_su, ps_turn, ps_out = (
            ph.bank(x) for x in ("ps_look", "ps_term", "ps_score", "ps_su", "ps_turn", "ps_out"))
        w_in, wo_in, masks0, masks, staged = (ph.sem(x) for x in ("w_in", "wo_in", "masks0", "masks", "staged"))
        projected, kept = ph.sem("projected"), ph.sem("kept")
        look_mm, term_mm, score_mm, su_mm, turned, out_mm, y_mm = (
            ph.sem(x) for x in ("look_mm", "term_mm", "score_mm", "su_mm", "turned", "out_mm", "y_mm"))
        th_look_ok, th_su_ok, exp_ok, heads_ok = (ph.sem(x) for x in ("th_look_ok", "th_su_ok", "exp_ok", "heads_ok"))
        look_ok, term_ok, gated_ok, minus_ok, inv_ok, prob_ok, probT_ok, added = (
            ph.sem(x) for x in ("look_ok", "term_ok", "gated_ok", "minus_ok", "inv_ok", "prob_ok", "probT_ok", "added"))
        w_dram = W_qkv.rearrange("c (j q) -> c j q", j=6)
        QU, KU, VU, QC, KC, VC = range(6)

        with nc.Block() as block:
            @block.sync
            def _(sp):
                for p in turns(sp, PAIRS):
                    reached(sp, projected, 3 * BATCH * p)
                    sp.dma_start(w[:], w_dram[:, :, bass.ds(p * P, P)]).then_inc(w_in, 16)
                    reached(sp, y_mm, BATCH * p)
                    sp.dma_start(wo[:], W_out[bass.ds(p * P, P), :]).then_inc(wo_in, 16)

            @block.gpsimd
            def _(pool):
                nc.gpsimd.memset(causal[:], 1.0).then_inc(masks0, 1)
                nc.gpsimd.memset(ahead[:], -0.25).then_inc(masks0, 1)
                pool.wait_ge(masks0, 2)
                for at in (0, 2 * P):
                    nc.gpsimd.affine_select(out=causal[:, at:at + P], in_=causal[:, at:at + P], compare_op=ALU.is_ge,
                                            fill=0.0, base=0, pattern=[[1, P]], channel_multiplier=-1).then_inc(masks, 1)
                    nc.gpsimd.affine_select(out=ahead[:, at:at + P], in_=ahead[:, at:at + P], compare_op=ALU.is_gt,
                                            fill=0.0, base=0, pattern=[[-1, P]], channel_multiplier=1).then_inc(masks, 1)

                def stage(n, k):
                    reached(pool, projected, 3 * (n - 1))
                    nc.gpsimd.tensor_copy(xs[:, k, :], sh.XNT[:, bass.ds((n % BATCH) * SEQ, SEQ)]).then_inc(staged, 1)
                skewed(pool, STEPS, 2, lambda n, k: stage(n, k) if live(n, STEPS) else None)

            @block.tensor
            def _(pe):
                def project(n, k, j):
                    if j == 0:
                        pe.wait_ge(staged, n + 1)
                        pe.wait_ge(w_in, 16 * (n // BATCH + 1))
                    reached(pe, kept, 3 * n + j - 1)
                    bank = proj[:, (k + j) % 2, :]
                    pair = ((QU, QC), (KU, KC), (VU,))[j]
                    for i, m in enumerate(pair):
                        ins = nc.tensor.matmul(bank[:, i * SEQ:(i + 1) * SEQ], w[:, m, :], xs[:, k, :],
                                               start=True, stop=True)
                    if j == 2:
                        for t in range(2):
                            ins = nc.tensor.matmul(bank[:, SEQ + t * P:SEQ + (t + 1) * P], xs[:, k, t * P:(t + 1) * P],
                                                   w[:, VC, :], start=True, stop=True)
                    ins.then_inc(projected, 1)

                def rows(k, h, part, side):
                    return qkv[64 * h:64 * h + 64, k, part, side, :]

                def look_and_term(n, k, h):
                    q, kk, vu, qc = rows(k, h, 0, 0), rows(k, h, 1, 0), rows(k, h, 2, 0), rows(k, h, 0, 1)
                    pe.wait_ge(kept, 3 * n + 2)
                    reached(pe, th_look_ok, 2 * n + h)
                    nc.tensor.matmul(ps_look[:, 0:P], kk[:, 0:P], q[:, 0:P], start=True, stop=True)
                    nc.tensor.matmul(ps_look[:, P:TRI], kk[:, P:SEQ], q, start=True, stop=True).then_inc(look_mm, 1)
                    pe.wait_ge(kept, 3 * n + 3)
                    reached(pe, term_ok, 2 * n + h)
                    nc.tensor.matmul(ps_term[:, 0:SEQ], vu[:, 0:P], qc, start=True, stop=True)
                    nc.tensor.matmul(ps_term[:, SEQ:TRI], vu[:, P:SEQ], qc[:, P:SEQ], start=True,
                                     stop=True).then_inc(term_mm, 1)

                def score(n, k, h):
                    qc, kc = rows(k, h, 0, 1), rows(k, h, 1, 1)
                    reached(pe, minus_ok, 2 * n + h)
                    nc.tensor.matmul(ps_score[:, 0:P], qc[:, 0:P], kc[:, 0:P], start=True, stop=False)
                    nc.tensor.matmul(ps_score[:, 0:P], sh.ident16[:], sh.future16[:], start=False, stop=True)
                    nc.tensor.matmul(ps_score[:, P:TRI], qc[:, P:SEQ], kc, start=True, stop=False)
                    nc.tensor.matmul(ps_score[:, SEQ:TRI], sh.ident16[:], sh.future16[:], start=False,
                                     stop=True).then_inc(score_mm, 1)

                def lookup_sum(n, h):
                    pe.wait_ge(look_ok, 2 * n + h + 1)
                    pe.wait_ge(term_ok, 2 * n + h + 1)
                    reached(pe, gated_ok, 2 * n + h)
                    T, L = term[:, h, :], look[:, h, :]
                    nc.tensor.matmul(ps_su[:, P:TRI], T[:, SEQ:TRI], L[:, P:TRI], start=True, stop=False)
                    nc.tensor.matmul(ps_su[:, P:SEQ], T[:, P:SEQ], L[:, 0:P], start=False, stop=True)
                    nc.tensor.matmul(ps_su[:, 0:P], T[:, 0:P], L[:, 0:P], start=True, stop=True).then_inc(su_mm, 1)

                def turn(n, h):
                    pe.wait_ge(prob_ok, 2 * n + h + 1)
                    reached(pe, probT_ok, 2 * n + h)
                    for b in range(3):
                        ins = nc.tensor.transpose(ps_turn[:, b * P:(b + 1) * P], prob[:, h, b * P:(b + 1) * P],
                                                  sh.ident[:])
                    ins.then_inc(turned, 1)

                def attend(n, k):
                    pe.wait_ge(probT_ok, 2 * n + 2)
                    reached(pe, added, n)
                    v = qkv[:, k, 2, 1, :]
                    for h in range(2):
                        nc.tensor.matmul(ps_out[64 * h:64 * h + 64, 0:SEQ], v[:, 64 * h:64 * h + 64],
                                         probT[:, h, 0:SEQ], start=True, stop=False)
                    for h in range(2):
                        ins = nc.tensor.matmul(ps_out[64 * h:64 * h + 64, P:SEQ], v[:, P + 64 * h:P + 64 * h + 64],
                                               probT[:, h, SEQ:TRI], start=False, stop=True)
                    ins.then_inc(out_mm, 1)

                def output(n):
                    pe.wait_ge(heads_ok, n + 1)
                    pe.wait_ge(wo_in, 16 * (n // BATCH + 1))
                    for t in range(2):
                        ins = nc.tensor.matmul(ps_out[:, SEQ + t * P:SEQ + (t + 1) * P], headsT[:, t * P:(t + 1) * P],
                                               wo[:], start=True, stop=True)
                    ins.then_inc(y_mm, 1)

                def body(n, k):
                    q, a, o, y = (live(n - lag, STEPS) for lag in range(4))
                    ka = 1 - k
                    if a:
                        look_and_term(n - 1, ka, 0)
                    if q:
                        project(n, k, 0)
                    if y:
                        output(n - 3)
                    if a:
                        lookup_sum(n - 1, 0)
                        score(n - 1, ka, 0)
                    if o:
                        turn(n - 2, 1)
                    if a:
                        look_and_term(n - 1, ka, 1)
                    if q:
                        project(n, k, 1)
                    if o:
                        attend(n - 2, k)
                    if a:
                        lookup_sum(n - 1, 1)
                        score(n - 1, ka, 1)
                    if q:
                        project(n, k, 2)
                    if a:
                        turn(n - 1, 0)
                pe.wait_ge(masks, 4)
                skewed(pe, STEPS, 3, body)

            @block.scalar
            def _(act):
                def keep(n, k, j):
                    act.wait_ge(projected, 3 * n + j + 1)
                    reached(act, score_mm, 2 * n - 2)
                    if j == 2:
                        reached(act, out_mm, n - 1)
                    nc.scalar.activation(qkv[:, k, j, :, :].rearrange("p a b -> p (a b)"), proj[:, (k + j) % 2, :], ACT.Copy,
                                         scale=SCALE if j == 0 else 1.0).then_inc(kept, 1)

                def tanh_look(n, h):
                    act.wait_ge(look_mm, 2 * n + h + 1)
                    reached(act, look_ok, 2 * n + h - 1)
                    nc.scalar.activation(th_look[:, h, :], ps_look[:, 0:TRI], ACT.Tanh, scale=0.5).then_inc(th_look_ok, 1)

                def tanh_su(n, h):
                    act.wait_ge(su_mm, 2 * n + h + 1)
                    reached(act, gated_ok, 2 * n + h - 1)
                    nc.scalar.activation(th_su[:, h, :], ps_su[:, 0:TRI], ACT.Tanh, scale=-1.0).then_inc(th_su_ok, 1)

                def exps(n, h):
                    act.wait_ge(minus_ok, 2 * n + h + 1)
                    reached(act, turned, 2 * n + h - 1)
                    for t, (a, b) in enumerate(((0, P), (P, TRI))):
                        nc.scalar.activation(prob[:, h, a:b], minus[:, h, a:b], ACT.Exp, bias=low[:, h, t:t + 1],
                                             scale=-1.0, accum_out=total[:, h, t:t + 1]).then_inc(exp_ok, 1)

                def heads(n):
                    act.wait_ge(out_mm, n + 1)
                    reached(act, y_mm, n)
                    nc.scalar.activation(headsT[:], ps_out[:, 0:SEQ], ACT.Copy).then_inc(heads_ok, 1)

                def body(n, k):
                    q, a, o = live(n, STEPS), live(n - 1, STEPS), live(n - 2, STEPS)
                    if a:
                        tanh_look(n - 1, 0)
                    if o:
                        exps(n - 2, 1)
                    if q:
                        keep(n, k, 0)
                    if a:
                        tanh_su(n - 1, 0)
                        tanh_look(n - 1, 1)
                        exps(n - 1, 0)
                    if q:
                        keep(n, k, 1)
                    if o:
                        heads(n - 2)
                    if a:
                        tanh_su(n - 1, 1)
                    if q:
                        keep(n, k, 2)
                skewed(act, STEPS, 2, body)

            @block.vector
            def _(dve):
                def mask_term(n, h):
                    dve.wait_ge(term_mm, 2 * n + h + 1)
                    reached(dve, su_mm, 2 * n + h - 1)
                    nc.vector.tensor_tensor(term[:, h, :], ps_term[:, 0:TRI], causal[:], ALU.mult).then_inc(term_ok, 1)

                def mask_look(n, h):
                    dve.wait_ge(th_look_ok, 2 * n + h + 1)
                    reached(dve, su_mm, 2 * n + h - 1)
                    nc.vector.scalar_tensor_tensor(out=look[:, h, :], in0=th_look[:, h, :], scalar=1.0, in1=ahead[:],
                                                   op0=ALU.add, op1=ALU.mult).then_inc(look_ok, 1)

                def gate(n, h):
                    dve.wait_ge(th_su_ok, 2 * n + h + 1)
                    reached(dve, minus_ok, 2 * n + h - 1)
                    nc.vector.scalar_tensor_tensor(out=gated[:, h, :], in0=th_su[:, h, :], scalar=1.0,
                                                   in1=ps_su[:, 0:TRI], op0=ALU.add, op1=ALU.mult).then_inc(gated_ok, 1)

                def may_lower(n, h):
                    dve.wait_ge(gated_ok, 2 * n + h + 1)
                    dve.wait_ge(score_mm, 2 * n + h + 1)
                    reached(dve, exp_ok, 2 * (2 * n + h - 1))

                def lowest(n, h):
                    for t, (a, b) in enumerate(((0, P), (P, TRI))):
                        ins = nc.vector.tensor_tensor_reduce(
                            out=minus[:, h, a:b], in0=gated[:, h, a:b], in1=ps_score[:, a:b], scale=-1.0, scalar=3.0e38,
                            op0=ALU.add, op1=ALU.min, accum_out=low[:, h, t:t + 1])
                    ins.then_inc(minus_ok, 1)

                def normalise(n, h):
                    dve.wait_ge(exp_ok, 2 * (2 * n + h) + 2)
                    nc.vector.reciprocal(inv[:, h, :], total[:, h, :]).then_inc(inv_ok, 1)
                    dve.wait_ge(inv_ok, 2 * n + h + 1)
                    for t, (a, b) in enumerate(((0, P), (P, TRI))):
                        ins = nc.vector.tensor_scalar(prob[:, h, a:b], prob[:, h, a:b], inv[:, h, t:t + 1], None, ALU.mult)
                    ins.then_inc(prob_ok, 1)

                def keep_turned(n, h):
                    dve.wait_ge(turned, 2 * n + h + 1)
                    reached(dve, out_mm, n)
                    nc.vector.tensor_copy(probT[:, h, :], ps_turn[:, 0:TRI]).then_inc(probT_ok, 1)

                def add(n):
                    dve.wait_ge(y_mm, n + 1)
                    x = sh.X[:, bass.ds((n % BATCH) * 2, 2), :]
                    nc.vector.tensor_tensor(x, x, ps_out[:, SEQ:512].rearrange("p (t c) -> p t c", t=2),
                                            ALU.add).then_inc(added, 1)

                def body(n, k):
                    a, o, y = live(n - 1, STEPS), live(n - 2, STEPS), live(n - 3, STEPS)
                    if a:
                        mask_look(n - 1, 0)
                        mask_term(n - 1, 0)
                    if o:
                        normalise(n - 2, 1)
                    if y:
                        add(n - 3)
                    if a:
                        gate(n - 1, 0)
                        may_lower(n - 1, 0)
                    if o:
                        keep_turned(n - 2, 1)
                    if a:
                        lowest(n - 1, 0)
                        mask_term(n - 1, 1)
                        mask_look(n - 1, 1)
                        normalise(n - 1, 0)
                        gate(n - 1, 1)
                        may_lower(n - 1, 1)
                        nc.vector.memset(carrier[:], 0.0)
                        lowest(n - 1, 1)
                        keep_turned(n - 1, 0)
                dve.wait_ge(masks, 4)
                skewed(dve, STEPS, 3, body)


def latent_attention(nc, sh, w_down, w_up, w_q, w_out):
    SCALE = 64 ** -0.5
    HD = HEADS * 64
    CHUNKS = TOK // 512
    with Phase(nc, "ab") as ph:
        wd = ph.sb("wd", [P, P])
        latT = ph.sb("latT", [P, TOK])
        w = ph.sb("w", [P, 3, P])
        wo = ph.sb("wo", [P, P])
        xs = ph.sb("xs", [P, 2, SEQ])
        qkv = ph.sb("qkv", [P, 2, 3, SEQ])
        prob, probT = ph.sb("prob", [P, 2, TRI]), ph.sb("probT", [P, 2, TRI])
        low, total, inv = (ph.sb(x, [P, 2, 2]) for x in ("low", "total", "inv"))
        headsT = ph.sb("headsT", [P, SEQ])
        proj, ps_score, ps_turn = (ph.bank(x, (P, 2, 512)) for x in ("proj", "ps_score", "ps_turn"))
        ps_out = ph.bank("ps_out", (P, 2, 512))
        (wd_in, lat_mm, lat_ok, w_in, wo_in, staged, projected, kept, score_mm, turned, out_mm, y_mm, exp_ok, heads_ok,
         low_ok, inv_ok, prob_ok, probT_ok, added) = (ph.sem(x) for x in (
             "wd_in", "lat_mm", "lat_ok", "w_in", "wo_in", "staged", "projected", "kept", "score_mm", "turned",
             "out_mm", "y_mm", "exp_ok", "heads_ok", "low_ok", "inv_ok", "prob_ok", "probT_ok", "added"))

        with nc.Block() as block:
            @block.sync
            def _(sp):
                sp.dma_start(wd[:], w_down).then_inc(wd_in, 16)
                for p in turns(sp, PAIRS):
                    reached(sp, projected, 2 * BATCH * p)
                    sp.dma_start(w[:, 0, :], w_q[:, bass.ds(p * P, P)]).then_inc(w_in, 16)
                    sp.dma_start(w[:, 1:3, :], w_up.rearrange("c (j q) -> c j q", j=2)[:, :, bass.ds(p * P, P)]
                                 ).then_inc(w_in, 16)
                    reached(sp, y_mm, BATCH * p)
                    sp.dma_start(wo[:], w_out[bass.ds(p * P, P), :]).then_inc(wo_in, 16)

            @block.gpsimd
            def _(pool):
                def stage(n, k):
                    reached(pool, projected, 2 * (n - 1))
                    nc.gpsimd.tensor_copy(xs[:, k, :], latT[:, bass.ds((n % BATCH) * SEQ, SEQ)]).then_inc(staged, 1)
                pool.wait_ge(lat_ok, CHUNKS)
                skewed(pool, STEPS, 2, lambda n, k: stage(n, k) if live(n, STEPS) else None)

            @block.tensor
            def _(pe):
                def project(n, k, j):
                    reached(pe, kept, 2 * n + j - 1)
                    if j == 0:
                        pe.wait_ge(staged, n + 1)
                        pe.wait_ge(w_in, 32 * (n // BATCH + 1))
                        nc.tensor.matmul(proj[:, 0, 0:SEQ], w[:, 0, :], sh.XNT[:, bass.ds((n % BATCH) * SEQ, SEQ)],
                                         start=True, stop=True)
                        nc.tensor.matmul(proj[:, 0, SEQ:512], w[:, 1, :], xs[:, k, :], start=True,
                                         stop=True).then_inc(projected, 1)
                    else:
                        for t in range(2):
                            ins = nc.tensor.matmul(proj[:, 1, t * P:(t + 1) * P], xs[:, k, t * P:(t + 1) * P], w[:, 2, :],
                                                   start=True, stop=True)
                        ins.then_inc(projected, 1)

                def score(n, k, h):
                    q, kk = (qkv[64 * h:64 * h + 64, k, i, :] for i in range(2))
                    bank = ps_score[:, h, :]
                    pe.wait_ge(kept, 2 * n + 1)
                    reached(pe, exp_ok, 2 * (2 * n + h - 1))
                    nc.tensor.matmul(bank[:, 0:P], q[:, 0:P], kk[:, 0:P], start=True, stop=False)
                    nc.tensor.matmul(bank[:, 0:P], sh.ident16[:], sh.future16[:], start=False, stop=True)
                    nc.tensor.matmul(bank[:, P:TRI], q[:, P:SEQ], kk, start=True, stop=False)
                    nc.tensor.matmul(bank[:, SEQ:TRI], sh.ident16[:], sh.future16[:], start=False,
                                     stop=True).then_inc(score_mm, 1)

                def turn(n, h):
                    pe.wait_ge(prob_ok, 2 * n + h + 1)
                    reached(pe, probT_ok, 2 * n + h - 1)
                    for b in range(3):
                        ins = nc.tensor.transpose(ps_turn[:, h, b * P:(b + 1) * P], prob[:, h, b * P:(b + 1) * P],
                                                  sh.ident[:])
                    ins.then_inc(turned, 1)

                def attend(n, k):
                    pe.wait_ge(kept, 2 * n + 2)
                    pe.wait_ge(probT_ok, 2 * n + 2)
                    reached(pe, heads_ok, n)
                    v = qkv[:, k, 2, :]
                    for h in range(2):
                        nc.tensor.matmul(ps_out[64 * h:64 * h + 64, 0, 0:SEQ], v[:, 64 * h:64 * h + 64],
                                         probT[:, h, 0:SEQ], start=True, stop=False)
                    for h in range(2):
                        ins = nc.tensor.matmul(ps_out[64 * h:64 * h + 64, 0, P:SEQ], v[:, P + 64 * h:P + 64 * h + 64],
                                               probT[:, h, SEQ:TRI], start=False, stop=True)
                    ins.then_inc(out_mm, 1)

                def output(n):
                    pe.wait_ge(heads_ok, n + 1)
                    pe.wait_ge(wo_in, 16 * (n // BATCH + 1))
                    reached(pe, added, n)
                    for t in range(2):
                        ins = nc.tensor.matmul(ps_out[:, 1, t * P:(t + 1) * P], headsT[:, t * P:(t + 1) * P], wo[:],
                                               start=True, stop=True)
                    ins.then_inc(y_mm, 1)

                def body(n, k):
                    q, a, o, y = (live(n - lag, STEPS) for lag in range(4))
                    if a:
                        score(n - 1, 1 - k, 0)
                    if o:
                        turn(n - 2, 1)
                    if a:
                        score(n - 1, 1 - k, 1)
                    if y:
                        output(n - 3)
                    if q:
                        project(n, k, 0)
                    if o:
                        attend(n - 2, k)
                    if q:
                        project(n, k, 1)
                    if a:
                        turn(n - 1, 0)

                pe.wait_ge(wd_in, 16)
                for c in range(CHUNKS):
                    reached(pe, lat_ok, c - 1)
                    nc.tensor.matmul(proj[:, c % 2, :], wd[:], sh.XNT[:, c * 512:(c + 1) * 512], start=True,
                                     stop=True).then_inc(lat_mm, 1)
                pe.wait_ge(lat_ok, CHUNKS)
                skewed(pe, STEPS, 3, body)

            @block.scalar
            def _(act):
                def keep(n, k, j):
                    act.wait_ge(projected, 2 * n + j + 1)
                    if j == 0:
                        reached(act, score_mm, 2 * n - 2)
                        nc.scalar.activation(qkv[:, k, 0, :], proj[:, 0, 0:SEQ], ACT.Copy, scale=SCALE)
                        nc.scalar.activation(qkv[:, k, 1, :], proj[:, 0, SEQ:512], ACT.Copy).then_inc(kept, 1)
                    else:
                        reached(act, out_mm, n - 1)
                        nc.scalar.activation(qkv[:, k, 2, :], proj[:, 1, 0:SEQ], ACT.Copy).then_inc(kept, 1)

                def exps(n, h):
                    act.wait_ge(low_ok, 2 * n + h + 1)
                    reached(act, turned, 2 * n + h - 1)
                    for t, (a, b) in enumerate(((0, P), (P, TRI))):
                        nc.scalar.activation(prob[:, h, a:b], ps_score[:, h, a:b], ACT.Exp, bias=low[:, h, t:t + 1],
                                             accum_out=total[:, h, t:t + 1]).then_inc(exp_ok, 1)

                def heads(n):
                    act.wait_ge(out_mm, n + 1)
                    reached(act, y_mm, n)
                    nc.scalar.activation(headsT[:], ps_out[:, 0, 0:SEQ], ACT.Copy).then_inc(heads_ok, 1)

                def body(n, k):
                    q, a, o = live(n, STEPS), live(n - 1, STEPS), live(n - 2, STEPS)
                    if a:
                        exps(n - 1, 0)
                    if q:
                        keep(n, k, 0)
                    if a:
                        exps(n - 1, 1)
                    if o:
                        heads(n - 2)
                    if q:
                        keep(n, k, 1)

                for c in range(CHUNKS):
                    act.wait_ge(lat_mm, c + 1)
                    nc.scalar.activation(latT[:, c * 512:(c + 1) * 512], proj[:, c % 2, :], ACT.Copy).then_inc(lat_ok, 1)
                skewed(act, STEPS, 2, body)

            @block.vector
            def _(dve):
                def maximum(n, h):
                    dve.wait_ge(score_mm, 2 * n + h + 1)
                    reached(dve, exp_ok, 2 * (2 * n + h - 1))
                    for t, (a, b) in enumerate(((0, P), (P, TRI))):
                        ins = nc.vector.tensor_reduce(low[:, h, t:t + 1], ps_score[:, h, a:b], AX.X, ALU.max, negate=True)
                    ins.then_inc(low_ok, 1)

                def normalise(n, h):
                    dve.wait_ge(exp_ok, 2 * (2 * n + h) + 2)
                    nc.vector.reciprocal(inv[:, h, :], total[:, h, :]).then_inc(inv_ok, 1)
                    dve.wait_ge(inv_ok, 2 * n + h + 1)
                    for t, (a, b) in enumerate(((0, P), (P, TRI))):
                        ins = nc.vector.tensor_scalar(prob[:, h, a:b], prob[:, h, a:b], inv[:, h, t:t + 1], None, ALU.mult)
                    ins.then_inc(prob_ok, 1)

                def keep_turned(n, h):
                    dve.wait_ge(turned, 2 * n + h + 1)
                    reached(dve, out_mm, n)
                    nc.vector.tensor_copy(probT[:, h, :], ps_turn[:, h, 0:TRI]).then_inc(probT_ok, 1)

                def add(n):
                    dve.wait_ge(y_mm, n + 1)
                    x = sh.X[:, bass.ds((n % BATCH) * 2, 2), :]
                    nc.vector.tensor_tensor(x, x, ps_out[:, 1, 0:SEQ].rearrange("p (t c) -> p t c", t=2),
                                            ALU.add).then_inc(added, 1)

                def body(n, k):
                    a, o, y = (live(n - lag, STEPS) for lag in (1, 2, 3))
                    if o:
                        keep_turned(n - 2, 1)
                    if a:
                        maximum(n - 1, 0)
                        maximum(n - 1, 1)
                        normalise(n - 1, 0)
                    if y:
                        add(n - 3)
                    if a:
                        normalise(n - 1, 1)
                        keep_turned(n - 1, 0)
                skewed(dve, STEPS, 3, body)


def top2_mixture(nc, sh, name, Wg, bg, W1, b1, W2, b2, gamma, beta):
    E, F = 8, 256
    CHUNKS = TOK // 512
    N = E * CHUNKS
    with Phase(nc, name) as ph:
        wg = ph.sb("wg", [P, E])
        bgb = ph.sb("bgb", [P, E])
        w1, b1s = ph.sb("w1", [P, E, F]), ph.sb("b1s", [P, E, 2])
        w2, b2s = ph.sb("w2", [P, E, 2, P]), ph.sb("b2s", [E, P])
        gam, bet = ph.sb("gam", [P, P]), ph.sb("bet", [P, P])
        prefer = ph.sb("prefer", [P, E])
        logit, hit, first, second, gate = (ph.sb(x, [P, TILES, E]) for x in ("logit", "hit", "first", "second", "gate"))
        m1, m2, best, e, weight1, weight2 = (ph.sb(x, [P, TILES]) for x in ("m1", "m2", "best", "e", "weight1", "weight2"))
        gateT = ph.sb("gateT", [E, TOK])
        hid = ph.sb("hid", [P, 2, 2, 512])
        acc = sh.XN
        ps_gate, ps_b2 = ph.bank("ps_gate"), ph.bank("ps_b2")
        ps_hid = ph.bank("ps_hid", (P, 4, 512))
        ps_y = ph.bank("ps_y", (P, 2, 512))
        (loaded, wl, preferred, logit_mm, chain, exp_in, exp_ok, gate_ok, gateT_mm, gateT_ok, b2_mm, b2_ok, up_mm, hid_ok,
         down_mm, acc_ok) = (ph.sem(x) for x in (
             "loaded", "wl", "preferred", "logit_mm", "chain", "exp_in", "exp_ok", "gate_ok", "gateT_mm", "gateT_ok",
             "b2_mm", "b2_ok", "up_mm", "hid_ok", "down_mm", "acc_ok"))
        st, mean, rstd, work = ph.sb("st", [P, TILES, 6]), ph.sb("mean", [P, TILES]), ph.sb("rstd", [P, TILES]), \
            ph.sb("work", [P, 7, TILES])
        stats, chain2, sqrt_in, sqrt_done, centred, shifted, summed = (ph.sem(x) for x in (
            "stats", "chain2", "sqrt_in", "sqrt_done", "centred", "shifted", "summed"))

        def two_chunks(n, first):
            return range(2 * (n - first), 2 * (n - first) + 2) if isinstance(n, int) and first <= n < first + 4 else ()

        with nc.Block() as block:
            @block.sync
            def _(sp):
                sp.dma_start(wg[:], Wg).then_inc(wl, 16)
                sp.dma_start(bgb[:], bg.partition_broadcast(P)).then_inc(wl, 16)
                sp.dma_start(b2s[:], b2).then_inc(wl, 16)
                sp.dma_start(w1[:], W1.rearrange("e d f -> d e f")).then_inc(loaded, 16)
                sp.dma_start(w2[:], W2.rearrange("e (j f) d -> f e j d", j=2)).then_inc(loaded, 16)
                with nc.allow_non_contiguous_dma("the biases are a few thousand values"):
                    sp.dma_start(b1s[:], b1.rearrange("e (j f) -> f e j", j=2)).then_inc(loaded, 16)
                sp.dma_start(gam[:], gamma.partition_broadcast(P)).then_inc(loaded, 16)
                sp.dma_start(bet[:], beta.partition_broadcast(P)).then_inc(loaded, 16)

            @block.gpsimd
            def _(pool):
                for i in range(E):
                    ins = nc.gpsimd.memset(prefer[:, i:i + 1], float(E - i))
                ins.then_inc(preferred, 1)
                pool.wait_ge(loaded, 80)
                with pool.Fori(0, CHUNKS) as c:
                    x = sh.X[:, bass.ds(4 * c, 4), :]
                    nc.gpsimd.tensor_tensor(x, x, bet[:].unsqueeze(1).broadcast_to([P, 4, P]), ALU.add).then_inc(shifted, 1)
                pool.wait_ge(shifted, CHUNKS)

            @block.tensor
            def _(pe):
                pe.wait_ge(wl, 48)
                for t in range(TILES):
                    ins = nc.tensor.matmul(ps_gate[:, t * E:(t + 1) * E], sh.XNT[:, t * P:(t + 1) * P], wg[:],
                                           start=True, stop=True)
                ins.then_inc(logit_mm, 1)

                def turn_gate(c):
                    pe.wait_ge(gate_ok, 1)
                    reached(pe, gateT_ok, c)
                    for i in range(4):
                        ins = nc.tensor.transpose(ps_gate[0:E, i * P:(i + 1) * P], gate[:, 4 * c + i, :], sh.ident[:])
                    ins.then_inc(gateT_mm, 1)

                def bias2(c):
                    pe.wait_ge(gateT_ok, c + 1)
                    reached(pe, b2_ok, c)
                    for i in range(4):
                        t = 4 * c + i
                        ins = nc.tensor.matmul(ps_b2[:, i * P:(i + 1) * P], gateT[:, t * P:(t + 1) * P], b2s[:],
                                               start=True, stop=True)
                    ins.then_inc(b2_mm, 1)

                def up(n, e_):
                    bank = 2 * (e_ % 2)
                    reached(pe, hid_ok, 2 * (n - 1))
                    for j in range(2):
                        nc.tensor.matmul(ps_hid[:, bank + j, :], w1[:, e_, j * P:(j + 1) * P],
                                         sh.XNT[:, bass.ds((n // E) * 512, 512)], start=True,
                                         stop=True).then_inc(up_mm, 1)

                def down(n, e_):
                    pe.wait_ge(hid_ok, 2 * (n + 1))
                    reached(pe, acc_ok, n - 1)
                    for i in range(4):
                        for j in range(2):
                            ins = nc.tensor.matmul(ps_y[:, e_ % 2, i * P:(i + 1) * P], hid[:, e_ % 2, j, i * P:(i + 1) * P],
                                                   w2[:, e_, j, :], start=j == 0, stop=j == 1)
                    ins.then_inc(down_mm, 1)

                def body(n, e_):
                    if live(n, N):
                        up(n, e_)
                    if live(n - 1, N):
                        down(n - 1, (e_ - 1) % E)
                    for c in two_chunks(n, 1):
                        turn_gate(c)
                    for c in two_chunks(n, 4):
                        bias2(c)
                pe.wait_ge(loaded, 80)
                skewed(pe, N, 1, body, E)

            @block.scalar
            def _(act):
                act.wait_ge(exp_in, 1)
                nc.scalar.activation(e[:], m2[:], ACT.Exp).then_inc(exp_ok, 1)

                def relu(n, e_):
                    reached(act, down_mm, n - 1)
                    for j in range(2):
                        act.wait_ge(up_mm, 2 * n + j + 1)
                        nc.scalar.activation(hid[:, e_ % 2, j, :], ps_hid[:, 2 * (e_ % 2) + j, :], ACT.Relu,
                                             bias=b1s[:, e_, j:j + 1]).then_inc(hid_ok, 1)

                def body(n, e_):
                    if live(n, N):
                        relu(n, e_)
                    for c in two_chunks(n, 1):
                        act.wait_ge(gateT_mm, c + 1)
                        nc.scalar.activation(gateT[:, c * 512:(c + 1) * 512], ps_gate[0:E, :], ACT.Copy).then_inc(gateT_ok, 1)
                act.wait_ge(loaded, 80)
                skewed(act, N, 1, body, E)

            @block.vector
            def _(dve):
                wide = [P, TILES, E]
                count = [0]

                def then(ins):
                    count[0] += 1
                    ins.then_inc(chain, 1)
                    dve.wait_ge(chain, count[0])

                def choose(onehot, top):
                    then(nc.vector.tensor_reduce(top[:], logit[:], AX.X, ALU.max))
                    then(nc.vector.tensor_tensor(hit[:], logit[:], top[:].unsqueeze(2).broadcast_to(wide), ALU.is_equal))
                    then(nc.vector.tensor_tensor(hit[:], hit[:], prefer[:].unsqueeze(1).broadcast_to(wide), ALU.mult))
                    then(nc.vector.tensor_reduce(best[:], hit[:], AX.X, ALU.max))
                    then(nc.vector.tensor_tensor(onehot[:], hit[:], best[:].unsqueeze(2).broadcast_to(wide), ALU.is_equal))

                dve.wait_ge(wl, 48)
                dve.wait_ge(preferred, 1)
                dve.wait_ge(logit_mm, 1)
                then(nc.vector.tensor_tensor(logit[:], ps_gate[:, 0:TILES * E].rearrange("p (t e) -> p t e", e=E),
                                             bgb[:].unsqueeze(1).broadcast_to(wide), ALU.add))
                choose(first, m1)
                then(nc.vector.scalar_tensor_tensor(out=logit[:], in0=first[:], scalar=NEG, in1=logit[:], op0=ALU.mult,
                                                    op1=ALU.add))
                choose(second, m2)
                nc.vector.tensor_tensor(m2[:], m2[:], m1[:], ALU.subtract).then_inc(exp_in, 1)
                dve.wait_ge(exp_ok, 1)
                then(nc.vector.tensor_scalar(m1[:], e[:], 1.0, None, ALU.add))
                then(nc.vector.reciprocal(weight1[:], m1[:]))
                then(nc.vector.tensor_tensor(weight2[:], e[:], weight1[:], ALU.mult))
                then(nc.vector.tensor_tensor(first[:], first[:], weight1[:].unsqueeze(2).broadcast_to(wide), ALU.mult))
                then(nc.vector.tensor_tensor(second[:], second[:], weight2[:].unsqueeze(2).broadcast_to(wide), ALU.mult))
                nc.vector.tensor_tensor(gate[:], first[:], second[:], ALU.add).then_inc(gate_ok, 1)
                dve.wait_ge(gate_ok, 1)

                def weigh(n, e_):
                    dve.wait_ge(down_mm, n + 1)
                    reached(dve, acc_ok, n)
                    for i in range(4):
                        a = acc[:, bass.ds((n // E) * 4 + i, 1), :].rearrange("p a c -> p (a c)")
                        ins = nc.vector.scalar_tensor_tensor(
                            out=a, in0=ps_y[:, e_ % 2, i * P:(i + 1) * P],
                            scalar=gate[:, bass.ds((n // E) * 4 + i, 1), e_:e_ + 1].rearrange("p a c -> p (a c)"), in1=a,
                            op0=ALU.mult, op1=ALU.add)
                    ins.then_inc(acc_ok, 1)

                def add_bias2(n, c):
                    dve.wait_ge(b2_mm, c + 1)
                    dve.wait_ge(acc_ok, n + 1)
                    nc.vector.tensor_tensor(acc[:, 4 * c:4 * c + 4, :], acc[:, 4 * c:4 * c + 4, :],
                                            ps_b2[:].rearrange("p (t c) -> p t c", t=4), ALU.add).then_inc(b2_ok, 1)
                    dve.wait_ge(b2_ok, c + 1)

                def chunk_statistics(n):
                    dve.wait_ge(acc_ok, n)
                    for i in range(4):
                        t = (n // E) * 4 - 4 + i
                        nc.vector.bn_stats(st[:, bass.ds(t, 1), :].rearrange("p a s -> p (a s)"),
                                           acc[:, bass.ds(t, 1), :].rearrange("p a c -> p (a c)")).then_inc(stats, 1)

                def body(n, e_):
                    if live(n, N):
                        weigh(n, e_)
                    for c in two_chunks(n, 3):
                        add_bias2(n, c)
                    if e_ == 0 and not (isinstance(n, int) and n == 0):
                        chunk_statistics(n)
                skewed(dve, N, 1, body, E)

        with nc.Block() as block:
            @block.vector
            def _(dve):
                dve.wait_ge(stats, TILES)
                row_statistics(nc, dve, st, mean, rstd, work, chain2, sqrt_in, sqrt_done)
                with dve.Fori(0, TILES // 8) as m:
                    for i in range(8):
                        t = 8 * m + i
                        a, x = (buf[:, bass.ds(t, 1), :].rearrange("p a c -> p (a c)") for buf in (acc, sh.X))
                        nc.vector.scalar_tensor_tensor(out=a, in0=a, scalar=mean[:, bass.ds(t, 1)], in1=gam[:],
                                                       op0=ALU.subtract, op1=ALU.mult).then_inc(centred, 1)
                    for i in range(8):
                        t = 8 * m + i
                        a, x = (buf[:, bass.ds(t, 1), :].rearrange("p a c -> p (a c)") for buf in (acc, sh.X))
                        dve.wait_ge(centred, t + 1)
                        nc.vector.scalar_tensor_tensor(out=x, in0=a, scalar=rstd[:, bass.ds(t, 1)], in1=x,
                                                       op0=ALU.mult, op1=ALU.add).then_inc(summed, 1)

            @block.scalar
            def _(act):
                act.wait_ge(sqrt_in, 1)
                nc.scalar.activation(work[:, 6, :], work[:, 5, :], ACT.Sqrt).then_inc(sqrt_done, 1)


def routed_mixture(nc, sh, ew, name, gate_w):
    E, F = 8, 256
    CHUNKS = TOK // 512
    N = E * CHUNKS
    with Phase(nc, name) as ph:
        wg = ph.sb("wg", [P, E])
        prefer = ph.sb("prefer", [P, E])
        logit, hit, chosen = (ph.sb(x, [P, TILES, E]) for x in ("logit", "hit", "chosen"))
        top, best, score, e = (ph.sb(x, [P, TILES]) for x in ("top", "best", "score", "e"))
        xr = ph.sb("xr", [P, 2, 4, P])
        xsT = ph.sb("xsT", [P, TOK])
        th, gu, hid = ph.sb("th", [P, 2, 512]), ph.sb("gu", [P, 2, 512]), ph.sb("hid", [P, 2, 2, 512])
        ps_g, ps_u, ps_y, ps_t = (ph.bank(x, (P, 2, 512)) for x in ("ps_g", "ps_u", "ps_y", "ps_t"))
        (wl, preferred, logit_mm, chain, exp_in, exp_ok, scaled, turned, xs_ok, up_mm, th_ok, gu_ok, hid_ok, down_mm,
         acc_ok) = (ph.sem(x) for x in (
             "wl", "preferred", "logit_mm", "chain", "exp_in", "exp_ok", "scaled", "turned", "xs_ok", "up_mm", "th_ok",
             "gu_ok", "hid_ok", "down_mm", "acc_ok"))

        def each_step(early, late, aside, eng):
            def run(f, n, k):
                if f is None or (isinstance(n, int) and not -CHUNKS <= n < N):
                    return
                if isinstance(n, int) and n < 0:
                    f(n + CHUNKS, n % 2, E, n + CHUNKS)
                else:
                    f(n + CHUNKS, k % 2, k % E, n // E)

            for n in range(-CHUNKS, E):
                run(early, n, n)
                run(late, n - 1, n - 1)
                aside(n + CHUNKS)
            with eng.Fori(1, N // E) as c:
                for k in range(E):
                    run(early, c * E + k, k)
                    run(late, c * E + k - 1, (k - 1) % E)
            run(late, N - 1, E - 1)

        with nc.Block() as block:
            @block.sync
            def _(sp):
                with nc.allow_non_contiguous_dma("the router has a thousand weights"):
                    sp.dma_start(wg[:], gate_w.rearrange("e h -> h e")).then_inc(wl, 16)

            @block.gpsimd
            def _(pool):
                for i in range(E):
                    ins = nc.gpsimd.memset(prefer[:, i:i + 1], float(E - i))
                ins.then_inc(preferred, 1)

            @block.tensor
            def _(pe):
                pe.wait_ge(wl, 16)
                for t in range(TILES):
                    ins = nc.tensor.matmul(ps_t[:, 0, t * E:(t + 1) * E], sh.XNT[:, t * P:(t + 1) * P], wg[:],
                                           start=True, stop=True)
                ins.then_inc(logit_mm, 1)

                def turn(s):
                    g = s - 1
                    if 0 <= g < CHUNKS:
                        pe.wait_ge(scaled, g + 1)
                        reached(pe, xs_ok, g - 1)
                        for i in range(4):
                            ins = nc.tensor.transpose(ps_t[:, g % 2, i * P:(i + 1) * P], xr[:, g % 2, i, :], sh.ident[:])
                        ins.then_inc(turned, 1)

                def up(s, k, e_, c):
                    x = sh.XNT if e_ == E else xsT
                    if e_ != E:
                        pe.wait_ge(xs_ok, c + 1)
                    for j in range(2):
                        reached(pe, hid_ok, 2 * (s - 1) + j + 1)
                        for ps, w in ((ps_g, ew.gate), (ps_u, ew.up)):
                            ins = nc.tensor.matmul(ps[:, j, :], w[:, 2 * e_ + j, :], x[:, bass.ds(c * 512, 512)],
                                                   start=True, stop=True)
                        ins.then_inc(up_mm, 1)

                def down(s, k, e_, c):
                    pe.wait_ge(hid_ok, 2 * (s + 1))
                    reached(pe, acc_ok, s - 1)
                    for i in range(4):
                        for j in range(2):
                            ins = nc.tensor.matmul(ps_y[:, k, i * P:(i + 1) * P], hid[:, k, j, i * P:(i + 1) * P],
                                                   ew.down[:, 2 * e_ + j, :], start=j == 0, stop=j == 1)
                    ins.then_inc(down_mm, 1)
                each_step(up, down, turn, pe)

            @block.scalar
            def _(act):
                act.wait_ge(exp_in, 1)
                nc.scalar.activation(e[:], top[:], ACT.Exp, scale=-1.0).then_inc(exp_ok, 1)

                def keep_turned(s):
                    g = s - 1
                    if 0 <= g < CHUNKS:
                        act.wait_ge(turned, g + 1)
                        nc.scalar.activation(xsT[:, g * 512:(g + 1) * 512], ps_t[:, g % 2, :], ACT.Copy).then_inc(xs_ok, 1)

                def tanh(s, k, e_, c):
                    for j in range(2):
                        act.wait_ge(up_mm, 2 * s + j + 1)
                        reached(act, gu_ok, 2 * (s - 1) + j + 1)
                        nc.scalar.activation(th[:, j, :], ps_g[:, j, :], ACT.Tanh, scale=0.5).then_inc(th_ok, 1)
                each_step(tanh, None, keep_turned, act)

            @block.vector
            def _(dve):
                wide = [P, TILES, E]
                count = [0]

                def then(ins):
                    count[0] += 1
                    ins.then_inc(chain, 1)
                    dve.wait_ge(chain, count[0])

                dve.wait_ge(wl, 16)
                dve.wait_ge(preferred, 1)
                dve.wait_ge(logit_mm, 1)
                then(nc.vector.tensor_copy(logit[:], ps_t[:, 0, 0:TILES * E].rearrange("p (t e) -> p t e", e=E)))
                then(nc.vector.tensor_reduce(top[:], logit[:], AX.X, ALU.max))
                then(nc.vector.tensor_tensor(hit[:], logit[:], top[:].unsqueeze(2).broadcast_to(wide), ALU.is_equal))
                then(nc.vector.tensor_tensor(hit[:], hit[:], prefer[:].unsqueeze(1).broadcast_to(wide), ALU.mult))
                then(nc.vector.tensor_reduce(best[:], hit[:], AX.X, ALU.max))
                nc.vector.tensor_tensor(chosen[:], hit[:], best[:].unsqueeze(2).broadcast_to(wide),
                                        ALU.is_equal).then_inc(exp_in, 1)
                dve.wait_ge(exp_ok, 1)
                then(nc.vector.tensor_scalar(best[:], e[:], 1.0, None, ALU.add))
                then(nc.vector.reciprocal(score[:], best[:]))

                def scale(g):
                    if g < CHUNKS:
                        reached(dve, turned, g - 1)
                        for i in range(4):
                            t = 4 * g + i
                            ins = nc.vector.tensor_scalar(xr[:, g % 2, i, :], sh.XN[:, t, :], score[:, t:t + 1], None,
                                                          ALU.mult)
                        ins.then_inc(scaled, 1)
                dve.wait_ge(exp_in, 1)

                def hidden(s, k, e_, c):
                    for j in range(2):
                        dve.wait_ge(th_ok, 2 * s + j + 1)
                        reached(dve, hid_ok, 2 * (s - 1) + j + 1)
                        nc.vector.scalar_tensor_tensor(out=gu[:, j, :], in0=th[:, j, :], scalar=1.0, in1=ps_g[:, j, :],
                                                       op0=ALU.add, op1=ALU.mult).then_inc(gu_ok, 1)
                        dve.wait_ge(gu_ok, 2 * s + j + 1)
                        reached(dve, down_mm, s - 1)
                        nc.vector.scalar_tensor_tensor(out=hid[:, k, j, :], in0=gu[:, j, :], scalar=0.5,
                                                       in1=ps_u[:, j, :], op0=ALU.mult, op1=ALU.mult).then_inc(hid_ok, 1)

                def collect(s, k, e_, c):
                    dve.wait_ge(down_mm, s + 1)
                    reached(dve, acc_ok, s)
                    if e_ == E:
                        x = sh.X[:, bass.ds(4 * c, 4), :]
                        nc.vector.tensor_tensor(x, x, ps_y[:, k, :].rearrange("p (t c) -> p t c", t=4),
                                                ALU.add).then_inc(acc_ok, 1)
                        return
                    for i in range(4):
                        x = sh.X[:, bass.ds(4 * c + i, 1), :].rearrange("p a c -> p (a c)")
                        ins = nc.vector.scalar_tensor_tensor(
                            out=x, in0=ps_y[:, k, i * P:(i + 1) * P],
                            scalar=chosen[:, bass.ds(4 * c + i, 1), e_:e_ + 1].rearrange("p a c -> p (a c)"), in1=x,
                            op0=ALU.mult, op1=ALU.add)
                    ins.then_inc(acc_ok, 1)
                each_step(hidden, collect, scale, dve)


class ExpertWeights:

    def __init__(self, nc, ctx):
        def sb(name):
            return ctx.enter_context(nc.sbuf_tensor(name, [P, 18, P], F32))
        self.gate, self.up, self.down = sb("gateT"), sb("upT"), sb("downT")


def load_experts(nc, sh, ew, shared_gate, shared_up, shared_down, r_gate, r_up, r_down):
    with Phase(nc, "ew") as ph:
        raw = ph.sb("raw", [P, 3, 18, P])
        bank = ph.bank("bank", (P, 2, 512))
        turned, kept = ph.sem("turned"), ph.sem("kept")
        loaded = [ph.sem(f"loaded{m}") for m in range(3)]
        groups = [(t, m, i) for t, m in ((ew.gate, 0), (ew.up, 1), (ew.down, 2)) for i in range(0, 18, 3)]
        with nc.Block() as block:
            @block.sync
            def _(sp):
                for m, (r, s) in enumerate(((r_gate, shared_gate), (r_up, shared_up))):
                    sp.dma_start(raw[:, m, 0:16, :], r.rearrange("e (j f) h -> f (e j) h", j=2)
                                 ).then_inc(loaded[m], 16)
                    sp.dma_start(raw[:, m, 16:18, :], s.rearrange("(j f) h -> f j h", j=2)).then_inc(loaded[m], 16)
                sp.dma_start(raw[:, 2, 0:16, :].rearrange("p (e j) f -> p e (j f)", j=2),
                             r_down.rearrange("e h f -> h e f")).then_inc(loaded[2], 16)
                sp.dma_start(raw[:, 2, 16:18, :].rearrange("p j f -> p (j f)"), shared_down).then_inc(loaded[2], 16)

            @block.tensor
            def _(pe):
                for n, (_, m, i) in enumerate(groups):
                    pe.wait_ge(loaded[m], 32)
                    reached(pe, kept, n - 1)
                    for b in range(3):
                        ins = nc.tensor.transpose(bank[:, n % 2, b * P:(b + 1) * P], raw[:, m, i + b, :], sh.ident[:])
                    ins.then_inc(turned, 1)

            @block.scalar
            def _(act):
                for n, (dst, m, i) in enumerate(groups):
                    act.wait_ge(turned, n + 1)
                    nc.scalar.activation(dst[:, i:i + 3, :].rearrange("p b c -> p (b c)"), bank[:, n % 2, 0:3 * P],
                                         ACT.Copy).then_inc(kept, 1)
                act.wait_ge(kept, len(groups))


def helical_attention(nc, sh, Wq, bq, Wk, bk, Wv, bv, Wo, bo, Whel, bhel):
    HD, HX = 8, 64
    TURNS = STEPS // 2
    HALF = SEQ // 2
    DOT = (HX // 2) / HD ** 0.5
    SCALE = 0.5 / (HX // 2)
    with Phase(nc, "la") as ph:
        woT = ph.sb("woT", [P, P])
        bob, bvb = ph.sb("bob", [P, P]), ph.sb("bvb", [P, P])
        qk = ph.sb("qk", [P, 2, TOK])
        v = ph.sb("v", [P, TILES, P])
        stack = ph.sb("stack", [P, 2, 2 * BATCH, HALF])
        helT = ph.sb("helT", [P, PAIRS, 2, P])
        bias = ph.sb("bias", [P, PAIRS, 2])
        heads = sh.XN

        with Phase(nc, "ls") as ps:
            raw = ps.sb("raw", [P, 4, P])
            wT = ps.sb("wT", [P, 4, P])
            hel = ps.sb("hel", [P, PAIRS, 2, P])
            pick = ps.sb("pick", [P, 2, 2, P])
            bqs, bks = ps.sb("bqs", [P, 1]), ps.sb("bks", [P, 1])
            bank = ps.bank("bank", (P, 2, 512))
            (loaded, zeroed, picked, hloaded, turned, kept, q_mm, q_ok, s_mm, s_ok, v_mm, v_ok) = (
                ps.sem(x) for x in ("loaded", "zeroed", "picked", "hloaded", "turned", "kept", "q_mm", "q_ok",
                                    "s_mm", "s_ok", "v_mm", "v_ok"))
            CH = TOK // 512
            with nc.Block() as block:
                @block.sync
                def _(sp):
                    for i, m in enumerate((Wq, Wk, Wv, Wo)):
                        sp.dma_start(raw[:, i, :], m).then_inc(loaded, 16)
                    sp.dma_start(bqs[:], bq.rearrange("(p a) -> p a", a=1)).then_inc(loaded, 16)
                    sp.dma_start(bks[:], bk.rearrange("(p a) -> p a", a=1)).then_inc(loaded, 16)
                    sp.dma_start(bvb[:], bv.partition_broadcast(P)).then_inc(loaded, 16)
                    sp.dma_start(bob[:], bo.partition_broadcast(P)).then_inc(loaded, 16)
                    sp.wait_ge(zeroed, 1)
                    for head in range(HEADS):
                        for c1 in range(2):
                            row, col = 64 * (head % 2) + 32 * c1, 16 * (head % 8) + 8 * c1
                            sp.dma_start(hel[row:row + 32, head // 2, :, col:col + HD],
                                         Whel[head].rearrange("(p c) d -> p c d", c=2)).then_inc(hloaded, 16)
                            sp.dma_start(bias[row:row + 32, head // 2, :],
                                         bhel[head].rearrange("(p c) -> p c", c=2)).then_inc(hloaded, 16)

                @block.gpsimd
                def _(pool):
                    nc.gpsimd.memset(hel[:], 0.0).then_inc(zeroed, 1)
                    nc.gpsimd.memset(pick[:], 0.0).then_inc(zeroed, 1)
                    pool.wait_ge(zeroed, 2)
                    for half in range(2):
                        for c1 in range(2):
                            view = pick[:, half, c1, :].rearrange("p (h c d) -> p h c d", c=2, d=HD)[:, :, c1, :]
                            nc.gpsimd.affine_select(out=view, in_=view, compare_op=ALU.not_equal, fill=1.0,
                                                    base=-64 * half, pattern=[[-HD, 8], [-1, HD]],
                                                    channel_multiplier=1).then_inc(picked, 1)

                blocks = [raw[:, i, :] for i in range(4)] + [hel[:, p, c, :] for p in range(PAIRS) for c in range(2)]

                @block.tensor
                def _(pe):
                    pe.wait_ge(loaded, 128)
                    def turn(g):
                        reached(pe, kept, g - 1)
                        for i in range(4):
                            ins = nc.tensor.transpose(bank[:, g % 2, i * P:(i + 1) * P], blocks[4 * g + i], sh.ident[:])
                        ins.then_inc(turned, 1)
                    turn(0)
                    pe.wait_ge(kept, 1)
                    for n in range(2 * CH):
                        reached(pe, q_ok, n - 1)
                        nc.tensor.matmul(bank[:, n % 2, :], wT[:, n // CH, :],
                                         sh.XNT[:, (n % CH) * 512:(n % CH + 1) * 512], start=True,
                                         stop=True).then_inc(q_mm, 1)
                    pe.wait_ge(q_ok, 2 * CH)
                    for c in range(CH):
                        reached(pe, v_ok, c - 1)
                        for i in range(4):
                            t = 4 * c + i
                            ins = nc.tensor.matmul(bank[:, c % 2, i * P:(i + 1) * P], sh.XNT[:, t * P:(t + 1) * P],
                                                   wT[:, 2, :], start=True, stop=True)
                        ins.then_inc(v_mm, 1)
                    pe.wait_ge(v_ok, CH)
                    pe.wait_ge(picked, 4)
                    n = 0
                    for side in range(2):
                        pairs = qk[:, side, :].rearrange("p (b s c) -> p b s c", b=BATCH, c=2)
                        for half in range(2):
                            for g in range(4):
                                reached(pe, s_ok, n - 1)
                                for c1 in range(2):
                                    ins = nc.tensor.matmul(bank[:, n % 2, :], pick[:, half, c1, :],
                                                           pairs[:, 4 * g:4 * g + 4, :, c1], start=c1 == 0, stop=c1 == 1)
                                ins.then_inc(s_mm, 1)
                                n += 1
                    pe.wait_ge(s_ok, n)
                    pe.wait_ge(hloaded, 16 * 4 * HEADS)
                    for g in range(1, 5):
                        turn(g)

                @block.scalar
                def _(act):
                    act.wait_ge(turned, 1)
                    nc.scalar.activation(wT[:].rearrange("p i c -> p (i c)"), bank[:, 0, :], ACT.Copy).then_inc(kept, 1)
                    act.wait_ge(kept, 1)
                    nc.scalar.activation(woT[:], wT[:, 3, :], ACT.Copy)
                    act.wait_ge(loaded, 128)
                    for n in range(2 * CH):
                        act.wait_ge(q_mm, n + 1)
                        nc.scalar.activation(qk[:, n // CH, (n % CH) * 512:(n % CH + 1) * 512], bank[:, n % 2, :],
                                             ACT.Identity, bias=(bqs, bks)[n // CH][:]).then_inc(q_ok, 1)
                    for n in range(16):
                        act.wait_ge(s_mm, n + 1)
                        side, half, g = n // 8, n // 4 % 2, n % 4
                        nc.scalar.activation(
                            stack[:, side, half * BATCH + 4 * g:half * BATCH + 4 * g + 4, :].rearrange("p b s -> p (b s)"),
                            bank[:, n % 2, :], ACT.Copy).then_inc(s_ok, 1)
                    for g in range(1, 5):
                        act.wait_ge(turned, g + 1)
                        nc.scalar.activation(helT[:, 2 * g - 2:2 * g, :, :].rearrange("p i c m -> p (i c m)"),
                                             bank[:, g % 2, :], ACT.Copy).then_inc(kept, 1)
                    nc.scalar.mul(qk[:, 0, :], qk[:, 0, :], DOT * SCALE)

                @block.vector
                def _(dve):
                    dve.wait_ge(loaded, 128)
                    for c in range(CH):
                        dve.wait_ge(v_mm, c + 1)
                        nc.vector.tensor_tensor(v[:, 4 * c:4 * c + 4, :],
                                                bank[:, c % 2, :].rearrange("p (t c) -> p t c", t=4),
                                                bvb[:].unsqueeze(1).broadcast_to([P, 4, P]), ALU.add).then_inc(v_ok, 1)

        with Phase(nc, "lm") as ps:
            wh = ps.sb("wh", [P, 2, P])
            comp = ps.sb("comp", [P, 2, 2, 2, 2, HALF])
            sq = ps.sb("sq", [P, 2, 2, 2, HALF])
            n2, norm, inv_n = (ps.sb(x, [P, 2, 2, 2, HALF]) for x in ("n2", "norm", "inv_n"))
            unit = ps.sb("unit", [P, 2, 2, 2, 2, 2, HALF])
            prob, probT = ps.sb("prob", [P, 2, 2, SEQ]), ps.sb("probT", [P, 2, 2, SEQ])
            low = ps.sb("low", [P, 2, 2])
            totals, inv = ps.sb("totals", [P, 2, 2, 2]), ps.sb("inv", [P, 2, 2])
            ps_hel, ps_score, ps_turn = (ps.bank(x, (P, 2, 512)) for x in ("ps_hel", "ps_score", "ps_turn"))
            ps_out = ps.bank("ps_out", (P, 2, 512))
            (wh_ok, hel_mm, comp_ok, sq_ok, n2_ok, cl_ok, norm_ok, inv_ok, unit_ok, bare, score_mm, low_ok,
             exp_ok, turned, probT_ok, out_mm, rec_ok, done) = (ps.sem(x) for x in (
                 "wh_ok", "hel_mm", "comp_ok", "sq_ok", "n2_ok", "cl_ok", "norm_ok", "inv_ok", "unit_ok", "bare",
                 "score_mm", "low_ok", "exp_ok", "turned", "probT_ok", "out_mm", "rec_ok", "done"))

            feat_ok = [[ps.sem(f"feat_ok{j}{i}") for i in range(2)] for j in range(2)]

            with nc.Block() as block:
                @block.sync
                def _(sp):
                    def features(p, m, j, i):
                        n = 2 * m + i
                        for h in range(2):
                            reached(sp, score_mm, 2 * n - 7 + h)
                            row = 64 * (1 - h)
                            sp.dma_start(unit[row:row + HD, j, i, h, :, :, :].rearrange("p a c s -> p a (c s)"),
                                         qk[(2 * p + h) * HD:(2 * p + h + 1) * HD, :, bass.ds((n % BATCH) * SEQ, SEQ)]
                                         ).then_inc(feat_ok[j][i], 16)

                    sp.wait_ge(bare, 2)
                    for p in range(PAIRS):
                        for b in turns(sp, BATCH // 4):
                            for j in range(2):
                                for i in range(2):
                                    features(p, p * (BATCH // 2) + 2 * b + j, j, i)

                @block.gpsimd
                def _(pool):
                    def squares(m, j, i):
                        n = 2 * m + i
                        pool.wait_ge(comp_ok, n + 1)
                        reached(pool, n2_ok, n - 1)
                        nc.gpsimd.tensor_tensor(sq[:, i], comp[:, j, i], comp[:, j, i], ALU.mult).then_inc(sq_ok, 1)
                        reached(pool, norm_ok, m - 1)
                        pool.wait_ge(sq_ok, n + 1)
                        nc.gpsimd.tensor_tensor(n2[:, j, i], sq[:, i, :, 0, :], sq[:, i, :, 1, :], ALU.add
                                                ).then_inc(n2_ok, 1)

                    for p in turns(pool, PAIRS):
                        reached(pool, hel_mm, BATCH * p)
                        nc.gpsimd.tensor_copy(wh[:], helT[:, bass.ds(p, 1), :, :].rearrange("p a c m -> p (a c) m")
                                              ).then_inc(wh_ok, 1)
                        for b in turns(pool, BATCH // 4):
                            for j in range(2):
                                for i in range(2):
                                    squares(p * (BATCH // 2) + 2 * b + j, j, i)

                @block.tensor
                def _(pe):
                    def helical(m, i):
                        n = 2 * m + i
                        pe.wait_ge(wh_ok, n // BATCH + 1)
                        reached(pe, comp_ok, n - 1)
                        at = (n // (4 * BATCH)) * BATCH + n % BATCH
                        for c in range(2):
                            for side in range(2):
                                col = (2 * side + c) * HALF
                                ins = nc.tensor.matmul(
                                    ps_hel[:, i, col:col + HALF], wh[:, c, :],
                                    stack[:, side, bass.ds(at, 1), :].rearrange("p a s -> p (a s)"), start=True, stop=True)
                        ins.then_inc(hel_mm, 1)

                    def score(m, j, i, h):
                        n = 2 * m + i
                        pe.wait_ge(unit_ok, n + 1)
                        pe.wait_ge(feat_ok[j][i], 32 * (m // 2 + 1))
                        reached(pe, exp_ok, 2 * (2 * n + h - 1))
                        for c in range(2):
                            ins = nc.tensor.matmul(ps_score[:, h, c * SEQ:(c + 1) * SEQ], unit[:, j, i, h, 0, c, :],
                                                   unit[:, j, i, h, 1, :, :], start=True, stop=True)
                        ins.then_inc(score_mm, 1)

                    def turn(m, i, h):
                        g = 2 * (2 * m + i) + h
                        pe.wait_ge(exp_ok, 2 * g + 2)
                        reached(pe, probT_ok, g - 1)
                        for t in range(2):
                            for s in range(2):
                                ins = nc.tensor.transpose(ps_turn[:, h, t * SEQ + s * P:t * SEQ + (s + 1) * P],
                                                          prob[:, h, s, t * P:(t + 1) * P], sh.ident[:])
                        ins.then_inc(turned, 1)

                    def attend(m, i, h):
                        n = 2 * m + i
                        g = 2 * n + h
                        pe.wait_ge(probT_ok, g + 1)
                        reached(pe, done, n - 1)
                        for s in range(2):
                            for t in range(2):
                                ins = nc.tensor.matmul(
                                    ps_out[:, i, (2 * h + s) * HD:(2 * h + s + 1) * HD],
                                    probT[:, h, t, s * P:(s + 1) * P],
                                    v[:, bass.ds((n % BATCH) * 2 + t, 1), bass.ds((n // BATCH) * 2 * HD + h * HD, HD)]
                                    .rearrange("p a d -> p (a d)"), start=t == 0, stop=t == 1)
                        ins.then_inc(out_mm, 1)

                    def body(m, j):
                        q, a, o = m, m - 2, m - 3
                        lq, la, lo = live(q, TURNS), live(a, TURNS), live(o, TURNS)
                        if la:
                            score(a, j, 0, 0)
                        if lo:
                            turn(o, 1, 1)
                        if lq:
                            helical(q, 0)
                        if lo:
                            attend(o, 1, 0)
                        if la:
                            score(a, j, 0, 1)
                        if lo:
                            attend(o, 1, 1)
                        if lq:
                            helical(q, 1)
                        if la:
                            turn(a, 0, 0)
                            score(a, j, 1, 0)
                            attend(a, 0, 0)
                            turn(a, 0, 1)
                            score(a, j, 1, 1)
                            attend(a, 0, 1)
                            turn(a, 1, 0)
                    skewed(pe, TURNS, 3, body)

                @block.scalar
                def _(act):
                    def root(m, j):
                        act.wait_ge(cl_ok, m + 1)
                        reached(act, inv_ok, 2 * m - 2)
                        nc.scalar.activation(norm[:, j].rearrange("p i a s -> p (i a s)"),
                                             n2[:, j].rearrange("p i a s -> p (i a s)"), ACT.Sqrt, scale=1 / SCALE
                                             ).then_inc(norm_ok, 1)

                    def exps(m, i, h):
                        n = 2 * m + i
                        g = 2 * n + h
                        act.wait_ge(low_ok, g + 1)
                        reached(act, turned, g - 1)
                        reached(act, rec_ok, n - 1)
                        for s in range(2):
                            nc.scalar.activation(prob[:, h, s, :], ps_score[:, h, s * SEQ:(s + 1) * SEQ], ACT.Exp,
                                                 bias=low[:, h, s:s + 1],
                                                 accum_out=totals[:, i, h, s:s + 1]).then_inc(exp_ok, 1)

                    def keep_turned(m, i, h):
                        g = 2 * (2 * m + i) + h
                        act.wait_ge(turned, g + 1)
                        reached(act, out_mm, g - 1)
                        nc.scalar.activation(probT[:, h].rearrange("p t s -> p (t s)"), ps_turn[:, h, :],
                                             ACT.Copy).then_inc(probT_ok, 1)

                    def body(m, j):
                        r, a, o = m - 1, m - 2, m - 3
                        lr, la, lo = live(r, TURNS), live(a, TURNS), live(o, TURNS)
                        if lr:
                            root(r, 1 - j)
                        if lo:
                            keep_turned(o, 1, 1)
                        if la:
                            exps(a, 0, 0)
                            exps(a, 0, 1)
                            keep_turned(a, 0, 0)
                            exps(a, 1, 0)
                            keep_turned(a, 0, 1)
                            exps(a, 1, 1)
                            keep_turned(a, 1, 0)
                    skewed(act, TURNS, 3, body)

                @block.vector
                def _(dve):
                    wide = [P, 2, 2, HALF]
                    for h in range(2):
                        row = 64 * (1 - h)
                        nc.vector.memset(unit[row:row + 64, :, :, h], 0.0).then_inc(bare, 1)

                    def components(m, j, i):
                        n = 2 * m + i
                        dve.wait_ge(hel_mm, n + 1)
                        reached(dve, unit_ok, n - 3)
                        nc.vector.tensor_tensor(
                            comp[:, j, i], ps_hel[:, i, :].rearrange("p (a c s) -> p a c s", a=2, c=2),
                            bias[:, bass.ds(n // BATCH, 1), :].unsqueeze(3).broadcast_to([P, 1, 2, HALF])
                            .broadcast_to(wide), ALU.add).then_inc(comp_ok, 1)

                    def clamp(m, j):
                        dve.wait_ge(n2_ok, 2 * m + 2)
                        f = n2[:, j].rearrange("p i a s -> p (i a s)")
                        nc.vector.tensor_scalar(f, f, 1e-24, None, ALU.max).then_inc(cl_ok, 1)

                    def inverses(m, j, i):
                        n = 2 * m + i
                        dve.wait_ge(norm_ok, m + 1)
                        reached(dve, unit_ok, n - 3)
                        nc.vector.reciprocal(inv_n[:, j, i], norm[:, j, i]).then_inc(inv_ok, 1)

                    def units(m, j, i):
                        n = 2 * m + i
                        dve.wait_ge(inv_ok, n + 1)
                        reached(dve, score_mm, 2 * n - 6)
                        for h in range(2):
                            rows = slice(64 * h, 64 * h + 64)
                            ins = nc.vector.tensor_tensor(unit[rows, j, i, h], comp[rows, j, i],
                                                          inv_n[rows, j, i].unsqueeze(2).broadcast_to([64, 2, 2, HALF]),
                                                          ALU.mult)
                        ins.then_inc(unit_ok, 1)

                    def maximum(m, i, h):
                        g = 2 * (2 * m + i) + h
                        dve.wait_ge(score_mm, g + 1)
                        reached(dve, exp_ok, 2 * (g - 1))
                        nc.vector.tensor_reduce(low[:, h, :], ps_score[:, h, :].rearrange("p (s t) -> p s t", s=2), AX.X,
                                                ALU.max, negate=True).then_inc(low_ok, 1)

                    def weigh(m, i):
                        n = 2 * m + i
                        dve.wait_ge(exp_ok, 4 * n + 4)
                        reached(dve, done, n)
                        nc.vector.reciprocal(inv[:], totals[:, i]).then_inc(rec_ok, 1)

                    def collect(m, i):
                        n = 2 * m + i
                        dve.wait_ge(rec_ok, n + 1)
                        dve.wait_ge(out_mm, 2 * n + 2)
                        nc.vector.tensor_tensor(
                            heads[:, bass.ds((n % BATCH) * 2, 2), bass.ds((n // BATCH) * 2 * HD, 2 * HD)]
                            .rearrange("p s (h d) -> p h s d", h=2),
                            ps_out[:, i, 0:4 * HD].rearrange("p (h s d) -> p h s d", h=2, s=2),
                            inv[:].unsqueeze(3).broadcast_to([P, 2, 2, HD]), ALU.mult).then_inc(done, 1)

                    def body(m, j):
                        q, r, a, o = m, m - 1, m - 2, m - 3
                        lq, lr, la, lo = (live(x, TURNS) for x in (q, r, a, o))
                        if la:
                            maximum(a, 0, 0)
                        if lo:
                            weigh(o, 1)
                        if lq:
                            components(q, j, 0)
                        if la:
                            maximum(a, 0, 1)
                        if lr:
                            inverses(r, 1 - j, 0)
                        if lo:
                            collect(o, 1)
                        if lq:
                            components(q, j, 1)
                        if la:
                            maximum(a, 1, 0)
                            weigh(a, 0)
                        if lr:
                            units(r, 1 - j, 0)
                        if lq:
                            clamp(q, j)
                        if la:
                            maximum(a, 1, 1)
                        if lr:
                            inverses(r, 1 - j, 1)
                        if la:
                            collect(a, 0)
                        if lr:
                            units(r, 1 - j, 1)
                    skewed(dve, TURNS, 3, body)

        token_projection(nc, sh, "lo", heads, woT, bob)


def token_projection(nc, sh, name, src, w, bias):
    CH = TOK // 512
    with Phase(nc, name) as ps:
        bank, ps_y = ps.bank("bank", (P, 2, 512)), ps.bank("ps_y", (P, 2, 512))
        srcT = ps.sb("srcT", [P, 2, 512])
        turned, kept, y_mm, biased, added = (ps.sem(x) for x in ("turned", "kept", "y_mm", "biased", "added"))
        with nc.Block() as block:
            @block.tensor
            def _(pe):
                for c in range(CH):
                    reached(pe, kept, c - 1)
                    for i in range(4):
                        ins = nc.tensor.transpose(bank[:, c % 2, i * P:(i + 1) * P], src[:, 4 * c + i, :], sh.ident[:])
                    ins.then_inc(turned, 1)
                    pe.wait_ge(kept, c + 1)
                    reached(pe, added, c - 1)
                    for i in range(4):
                        ins = nc.tensor.matmul(ps_y[:, c % 2, i * P:(i + 1) * P], srcT[:, c % 2, i * P:(i + 1) * P], w[:],
                                               start=True, stop=True)
                    ins.then_inc(y_mm, 1)

            @block.scalar
            def _(act):
                for c in range(CH):
                    act.wait_ge(turned, c + 1)
                    reached(act, y_mm, c - 1)
                    nc.scalar.activation(srcT[:, c % 2, :], bank[:, c % 2, :], ACT.Copy).then_inc(kept, 1)

            @block.gpsimd
            def _(pool):
                for c in range(CH):
                    x = sh.X[:, 4 * c:4 * c + 4, :]
                    nc.gpsimd.tensor_tensor(x, x, bias[:].unsqueeze(1).broadcast_to([P, 4, P]), ALU.add).then_inc(biased, 1)

            @block.vector
            def _(dve):
                for c in range(CH):
                    dve.wait_ge(y_mm, c + 1)
                    dve.wait_ge(biased, c + 1)
                    x = sh.X[:, 4 * c:4 * c + 4, :]
                    nc.vector.tensor_tensor(x, x, ps_y[:, c % 2, :].rearrange("p (t c) -> p t c", t=4),
                                            ALU.add).then_inc(added, 1)


def delta_attention(nc, sh, Wv, Wo, Wg, Wb):
    HD = P // HEADS
    SLOT = 16
    HALF = BATCH // 2
    SLOTS = SEQ // SLOT
    CH = TOK // 512
    with Phase(nc, "da") as ph:
        vT, betaT, gateT = (ph.sb(x, [P, TOK]) for x in ("vT", "betaT", "gateT"))
        out = sh.XNT[:].rearrange("p (b t) -> p b t", b=BATCH)
        rT = ph.sb("rT", [P, TOK])
        woT = ph.sb("woT", [P, P])
        spread = ph.sb("spread", [P, HD, P])

        with Phase(nc, "ds") as ps:
            raw = ps.sb("raw", [P, 2, P])
            small = ps.sb("small", [P, 2, HEADS])
            wT = ps.sb("wT", [P, 3, P])
            n2 = ps.sb("n2", [P, TILES, HEADS])
            norm, inv = ps.sb("norm", [P, TILES, HEADS]), ps.sb("inv", [P, TILES, HEADS])
            th = ps.sb("th", [P, 2, 512])
            bank = ps.bank("bank", (P, 2, 512))
            (loaded, turned, kept, chain, sq_ok, sqrt_in, sqrt_ok, unit_ok, zeroed, spread_ok, p_mm, p_ok, th_ok, half_ok, r_mm,
             r_ok) = (ps.sem(x) for x in (
                 "loaded", "turned", "kept", "chain", "sq_ok", "sqrt_in", "sqrt_ok", "unit_ok", "zeroed", "spread_ok", "p_mm",
                 "p_ok", "th_ok", "half_ok", "r_mm", "r_ok"))
            sq = rT[:].rearrange("p (t c) -> p t c", t=TILES)
            with nc.Block() as block:
                @block.sync
                def _(sp):
                    for i, m in enumerate((Wv, Wo)):
                        sp.dma_start(raw[:, i, :], m).then_inc(loaded, 16)
                    with nc.allow_non_contiguous_dma("two gates of two thousand weights"):
                        for i, m in enumerate((Wb, Wg)):
                            sp.dma_start(small[:, i, :], m.rearrange("h c -> c h")).then_inc(loaded, 16)

                @block.gpsimd
                def _(pool):
                    nc.gpsimd.memset(spread[:], 0.0).then_inc(zeroed, 1)
                    pool.wait_ge(zeroed, 1)
                    for k in range(HD):
                        nc.gpsimd.tensor_copy(
                            spread[:, k, :].rearrange("p (h d) -> p h d", d=HD),
                            sh.ident[:].rearrange("p (h d) -> p h d", d=HD)[:, :, k:k + 1].broadcast_to([P, HEADS, HD])
                        ).then_inc(spread_ok, 1)

                @block.tensor
                def _(pe):
                    pe.wait_ge(loaded, 64)
                    for i in range(2):
                        ins = nc.tensor.transpose(bank[:, 0, i * P:(i + 1) * P], raw[:, i, :], sh.ident[:])
                    ins.then_inc(turned, 1)
                    pe.wait_ge(kept, 4)
                    for n in range(3 * CH):
                        if 2 <= n <= CH + 1:
                            pe.wait_ge(p_ok, n - 1)
                        elif n > CH + 1:
                            pe.wait_ge(th_ok, n - 1 - CH)
                            pe.wait_ge(p_ok, CH)
                        nc.tensor.matmul(bank[:, n % 2, :], wT[:, n // CH, :], sh.XNT[:, (n % CH) * 512:(n % CH + 1) * 512],
                                         start=True, stop=True).then_inc(p_mm, 1)
                    pe.wait_ge(th_ok, 2 * CH)
                    for c in range(CH):
                        pe.wait_ge(unit_ok, c + 1)
                        reached(pe, r_ok, c - 1)
                        for i in range(4):
                            ins = nc.tensor.transpose(bank[:, c % 2, i * P:(i + 1) * P], sh.XN[:, 4 * c + i, :], sh.ident[:])
                        ins.then_inc(r_mm, 1)

                @block.scalar
                def _(act):
                    nc.scalar.activation(sq, sh.XN[:], ACT.Square).then_inc(sq_ok, 1)
                    act.wait_ge(turned, 1)
                    nc.scalar.activation(wT[:, 0, :], bank[:, 0, 0:P], ACT.Copy).then_inc(kept, 1)
                    nc.scalar.activation(woT[:], bank[:, 0, P:2 * P], ACT.Copy).then_inc(kept, 1)
                    act.wait_ge(loaded, 64)
                    for i in range(2):
                        nc.scalar.activation(wT[:, 1 + i, :].rearrange("p (h d) -> p h d", d=HD),
                                             small[:, i, :].unsqueeze(2).broadcast_to([P, HEADS, HD]),
                                             ACT.Copy).then_inc(kept, 1)
                    for n in range(3 * CH):
                        act.wait_ge(p_mm, n + 1)
                        at = slice((n % CH) * 512, (n % CH + 1) * 512)
                        if n < CH:
                            nc.scalar.activation(vT[:, at], bank[:, n % 2, :], ACT.Copy).then_inc(p_ok, 1)
                        else:
                            reached(act, half_ok, n - CH - 1)
                            nc.scalar.activation(th[:, n % 2, :], bank[:, n % 2, :], ACT.Tanh, scale=0.5).then_inc(th_ok, 1)
                    act.wait_ge(sqrt_in, 1)
                    nc.scalar.activation(norm[:].rearrange("p t h -> p (t h)"), n2[:].rearrange("p t h -> p (t h)"),
                                         ACT.Sqrt).then_inc(sqrt_ok, 1)
                    for c in range(CH):
                        act.wait_ge(r_mm, c + 1)
                        nc.scalar.activation(rT[:, c * 512:(c + 1) * 512], bank[:, c % 2, :], ACT.Copy).then_inc(r_ok, 1)

                @block.vector
                def _(dve):
                    heads = sh.XN[:].rearrange("p t (h d) -> p t h d", d=HD)
                    dve.wait_ge(sq_ok, 1)
                    nc.vector.tensor_reduce(n2[:], sq.rearrange("p t (h d) -> p t h d", d=HD), AX.X,
                                            ALU.add).then_inc(chain, 1)
                    dve.wait_ge(chain, 1)
                    nc.vector.tensor_scalar(n2[:], n2[:], 1e-24, None, ALU.max).then_inc(sqrt_in, 1)
                    for n in range(2 * CH):
                        dve.wait_ge(th_ok, n + 1)
                        dst = (betaT, gateT)[n // CH]
                        nc.vector.tensor_scalar(dst[:, (n % CH) * 512:(n % CH + 1) * 512], th[:, n % 2, :], 0.5, 0.5,
                                                ALU.mult, ALU.add).then_inc(half_ok, 1)
                    dve.wait_ge(sqrt_ok, 1)
                    nc.vector.reciprocal(inv[:], norm[:]).then_inc(chain, 1)
                    dve.wait_ge(chain, 2)
                    for c in range(CH):
                        t = slice(4 * c, 4 * c + 4)
                        nc.vector.tensor_tensor(heads[:, t], heads[:, t], inv[:, t, :].unsqueeze(3)
                                                .broadcast_to([P, 4, HEADS, HD]), ALU.mult).then_inc(unit_ok, 1)
                    dve.wait_ge(p_ok, CH)
                    dve.wait_ge(half_ok, CH)
                    nc.vector.tensor_tensor(vT[:], vT[:], betaT[:], ALU.mult).then_inc(chain, 1)
                    dve.wait_ge(chain, 3)
                    b, r = (x[:].rearrange("p (b t) -> p b t", b=BATCH) for x in (betaT, rT))
                    nc.vector.memset(b[:, :, 0:1], 0.0)
                    for c in range(CH):
                        dve.wait_ge(r_ok, c + 1)
                        two = slice(2 * c, 2 * c + 2)
                        nc.vector.tensor_tensor(b[:, two, 1:SEQ], b[:, two, 1:SEQ], r[:, two, 0:SEQ - 1], ALU.mult)

        with Phase(nc, "dr") as ps:
            RW = ps.sb("RW", [P, 2, HD, 2, BATCH, SLOT])
            WV = sh.XN[:].rearrange("p t c -> p (t c)").rearrange("p (i k b t) -> p i k b t", i=2, k=HD, b=BATCH)
            O = ps.sb("O", [P, 2, BATCH, SLOT])
            S, toward = ps.sb("S", [P, HD, BATCH]), ps.sb("toward", [P, HD, BATCH])
            away, prod = ps.sb("away", [P, HD, BATCH]), ps.sb("prod", [P, HD, BATCH])
            bank = ps.bank("bank", (P, HD, 512))
            r_mm, r_ok, wv_ok, toward_ok, away_ok, s_ok, prod_ok, o_ok, out_ok = (ps.sem(x) for x in (
                "r_mm", "r_ok", "wv_ok", "toward_ok", "away_ok", "s_ok", "prod_ok", "o_ok", "out_ok"))
            r, wb, v = (t[:].rearrange("p (b t) -> p b t", b=BATCH) for t in (rT, betaT, vT))
            PARTS = (slice(0, HALF), slice(HALF, BATCH))
            PIECES = 2 * HD + 1
            START = 5
            wide = [P, HD, HALF]

            with nc.Block() as block:
                @block.tensor
                def _(pe):
                    for c in turns(pe, SLOTS):
                        for k in range(HD):
                            reached(pe, r_ok, HD * (c - 1) + k + 1)
                            for i, src in enumerate((r, wb)):
                                ins = nc.tensor.matmul(bank[:, k, i * BATCH * SLOT:(i + 1) * BATCH * SLOT], spread[:, k, :],
                                                       src[:, :, bass.ds(c * SLOT, SLOT)], start=True, stop=True)
                            ins.then_inc(r_mm, 1)

                @block.scalar
                def _(act):
                    def keep_outputs(c, half):
                        act.wait_ge(o_ok, 2 + 2 * SLOT * (c + 1))
                        nc.scalar.activation(out[:, :, bass.ds(c * SLOT, SLOT)], O[:, half], ACT.Copy).then_inc(out_ok, 1)

                    def slot(c, half):
                        if live(c - 2, SLOTS):
                            keep_outputs(c - 2, half)
                            act.wait_ge(wv_ok, PIECES * c)
                        for k in range(HD):
                            act.wait_ge(r_mm, HD * c + k + 1)
                            nc.scalar.activation(RW[:, half, k].rearrange("p i b t -> p (i b t)"), bank[:, k, :],
                                                 ACT.Copy).then_inc(r_ok, 1)
                    slot(0, 0)
                    slot(1, 1)
                    with act.Fori(1, SLOTS // 2) as m:
                        slot(2 * m, 0)
                        slot(2 * m + 1, 1)
                    keep_outputs(SLOTS - 2, 0)
                    keep_outputs(SLOTS - 1, 1)

                @block.gpsimd
                def _(pool):
                    def piece(c, half, q):
                        if q == PIECES - 1:
                            nc.gpsimd.tensor_tensor(
                                WV[:, half, :, :, 0], RW[:, 1 - half, :, 0, :, SLOT - 1],
                                v[:, :, bass.ds(c * SLOT, 1)].rearrange("p b t -> p (b t)").unsqueeze(1)
                                .broadcast_to([P, HD, BATCH]), ALU.mult).then_inc(wv_ok, 1)
                            return
                        k, part = q // 2, PARTS[q % 2]
                        nc.gpsimd.tensor_tensor(WV[:, half, k, part, 1:SLOT], RW[:, half, k, 0, part, 0:SLOT - 1],
                                                v[:, part, bass.ds(c * SLOT + 1, SLOT - 1)], ALU.mult).then_inc(wv_ok, 1)

                    def steps(c, half, last):
                        pool.wait_ge(wv_ok, PIECES * (c + 1))
                        for j in range(SLOT):
                            t = c * SLOT + j
                            if j == START and not last:
                                pool.wait_ge(r_ok, HD * (c + 2))
                            for i, part in enumerate(PARTS):
                                pool.wait_ge(s_ok, 2 * t + i + 1)
                                nc.gpsimd.tensor_tensor(toward[:, :, part], S[:, :, part], WV[:, half, :, part, j],
                                                        ALU.add).then_inc(toward_ok, 1)
                            if j >= START and not last:
                                for q in range(PIECES * (j - START) // (SLOT - START),
                                               PIECES * (j + 1 - START) // (SLOT - START)):
                                    piece(c + 1, 1 - half, q)

                    with pool.Fori(0, SLOTS // 2 - 1) as m:
                        steps(2 * m, 0, False)
                        steps(2 * m + 1, 1, False)
                    steps(SLOTS - 2, 0, False)
                    steps(SLOTS - 1, 1, True)

                @block.vector
                def _(dve):
                    def step(c, half, j):
                        t = c * SLOT + j
                        before = O[:, half, :, j - 1] if j else O[:, 1 - half, :, SLOT - 1]
                        for stage in range(4):
                            for i, part in enumerate(PARTS):
                                count = 2 * t + i + 1
                                if stage == 0:
                                    dve.wait_ge(o_ok, count)
                                    nc.vector.tensor_tensor(away[:, :, part], RW[:, half, :, 1, part, j],
                                                            before[:, part].unsqueeze(1).broadcast_to(wide),
                                                            ALU.mult).then_inc(away_ok, 1)
                                elif stage == 1:
                                    dve.wait_ge(away_ok, count)
                                    dve.wait_ge(toward_ok, count)
                                    nc.vector.tensor_tensor(S[:, :, part], toward[:, :, part], away[:, :, part],
                                                            ALU.subtract).then_inc(s_ok, 1)
                                elif stage == 2:
                                    dve.wait_ge(s_ok, count + 2)
                                    nc.vector.tensor_tensor(prod[:, :, part], RW[:, half, :, 0, part, j], S[:, :, part],
                                                            ALU.mult).then_inc(prod_ok, 1)
                                else:
                                    dve.wait_ge(prod_ok, count)
                                    nc.vector.tensor_reduce(O[:, half, part, j], prod[:, :, part].rearrange("p k b -> p b k"),
                                                            AX.X, ALU.add).then_inc(o_ok, 1)

                    for part in PARTS:
                        nc.vector.memset(S[:, :, part], 0.0).then_inc(s_ok, 1)
                        nc.vector.memset(O[:, 1, part, SLOT - 1:SLOT], 0.0).then_inc(o_ok, 1)
                    nc.vector.memset(WV[:, 0, :, :, 0], 0.0).then_inc(wv_ok, 1)
                    dve.wait_ge(r_ok, HD)
                    for k in range(HD):
                        ins = nc.vector.tensor_tensor(WV[:, 0, k, :, 1:SLOT], RW[:, 0, k, 0, :, 0:SLOT - 1], v[:, :, 1:SLOT],
                                                      ALU.mult)
                    ins.then_inc(wv_ok, PIECES - 1)
                    for m in turns(dve, SLOTS // 2):
                        for half in range(2):
                            c = 2 * m + half
                            dve.wait_ge(r_ok, HD * (c + 1))
                            reached(dve, out_ok, c - 1)
                            for j in range(SLOT):
                                step(c, half, j)

        with Phase(nc, "do") as ps:
            bank = ps.bank("bank", (P, 2, 512))
            gated, y_mm, added = ps.sem("gated"), ps.sem("y_mm"), ps.sem("added")
            with nc.Block() as block:
                @block.gpsimd
                def _(pool):
                    g = gateT[:].rearrange("p (b t) -> p b t", b=BATCH)
                    for c in range(CH):
                        o = out[:, 2 * c:2 * c + 2, :]
                        nc.gpsimd.tensor_tensor(g[:, 2 * c:2 * c + 2, :], g[:, 2 * c:2 * c + 2, :], o,
                                                ALU.mult).then_inc(gated, 1)

                @block.tensor
                def _(pe):
                    for c in range(CH):
                        pe.wait_ge(gated, c + 1)
                        reached(pe, added, c - 1)
                        for i in range(4):
                            t = 4 * c + i
                            ins = nc.tensor.matmul(bank[:, c % 2, i * P:(i + 1) * P], gateT[:, t * P:(t + 1) * P], woT[:],
                                                   start=True, stop=True)
                        ins.then_inc(y_mm, 1)

                @block.vector
                def _(dve):
                    for c in range(CH):
                        dve.wait_ge(y_mm, c + 1)
                        x = sh.X[:, 4 * c:4 * c + 4, :]
                        nc.vector.tensor_tensor(x, x, bank[:, c % 2, :].rearrange("p (t c) -> p t c", t=4),
                                                ALU.add).then_inc(added, 1)


def store(nc, sh, out):
    with Phase(nc, "st") as ph:
        stored = ph.sem("stored")
        with nc.Block() as block:
            @block.sync
            def _(sp):
                sp.dma_start(out.rearrange("b (h p) c -> p (b h) c", p=P), sh.X[:]).then_inc(stored, 16)
                sp.wait_ge(stored, 16)


def hybrid_kernel(nc, a, out):
    def args(prefix, names):
        return [a[f"{prefix}_{n}"] for n in names.split()]

    with ExitStack() as ctx:
        sh = Shared(nc, ctx)
        load_and_constants(nc, sh, a["L0_attn_a_x"])
        layernorm(nc, sh, "n1")
        lookahead_attention(nc, sh, *args("L0_attn_a", "W_qkv W_out"))
        layernorm(nc, sh, "n2")
        top2_mixture(nc, sh, "fa", *args("L0_ffn", "Wg bg W1 b1 W2 b2 gamma beta"))
        layernorm(nc, sh, "n3")
        latent_attention(nc, sh, *args("L0_attn_b", "w_kv_down w_kv_up w_q w_out"))
        layernorm(nc, sh, "n4")
        top2_mixture(nc, sh, "fb", *args("L0_ffn", "Wg bg W1 b1 W2 b2 gamma beta"))
        layernorm(nc, sh, "n5")
        helical_attention(nc, sh, *args("L1_attn_a", "Wq bq Wk bk Wv bv Wo bo Whel bhel"))
        with ExitStack() as experts:
            ew = ExpertWeights(nc, experts)
            load_experts(nc, sh, ew, *args("L1_ffn", "shared_gate shared_up shared_down r_gate r_up r_down"))
            layernorm(nc, sh, "n6")
            routed_mixture(nc, sh, ew, "fc", a["L1_ffn_gate_w"])
            layernorm(nc, sh, "n7")
            delta_attention(nc, sh, *args("L1_attn_b", "Wv Wo Wg Wb"))
            layernorm(nc, sh, "n8")
            routed_mixture(nc, sh, ew, "fd", a["L1_ffn_gate_w"])
        store(nc, sh, out)


def kernel(**inputs):
    import numpy as _np
    import concourse.bacc as _bacc
    from concourse import mybir as _mybir
    from concourse.bass_utils import run_bass_kernel_spmd as _run

    nc = _bacc.Bacc("TRN2", target_bir_lowering=False, num_devices=1)
    arrays, args = {}, {}
    for name, value in inputs.items():
        array = _np.ascontiguousarray(value)
        arrays[f"in_{name}"] = array
        args[name] = nc.dram_tensor(f"in_{name}", array.shape, _mybir.dt.from_np(array.dtype), kind="ExternalInput").ap()
    out = nc.dram_tensor("out", (BATCH, SEQ, P), F32, kind="ExternalOutput").ap()
    hybrid_kernel(nc, args, out)
    return _run(nc, [arrays], core_ids=[0]).results[0]["out"]
```
